# Optimizing a Trainium2 kernel written in Bass

```python
import numpy as np
import jax
import jax.numpy as jnp

def _softmax(x, axis=-1):
    return jax.nn.softmax(x, axis=axis)

def _gelu(x):
    return jax.nn.gelu(x, approximate=True)

def _silu(x):
    return jax.nn.silu(x)

def _sigmoid(x):
    return jax.nn.sigmoid(x)

def _layernorm(x, axis=-1, eps=1e-05):
    m = jnp.mean(x, axis=axis, keepdims=True)
    v = jnp.var(x, axis=axis, keepdims=True)
    return (x - m) / jnp.sqrt(v + eps)

def _scatter_add(tgt, idx, src, axis=0):
    return tgt.at[idx].add(src)

def _segment_sum(src, seg, n):
    return jax.ops.segment_sum(src, seg, n)
kernel_name = 'mk_decoder_postln_d1_seqx_r2_4d4750'

def setup_inputs(seed: int=0):
    np.random.seed(seed)
    _w = jnp.asarray

    def _rec_inputs():
        import jax
        import jax.numpy as jnp
        _rk = jax.random.key(seed)
        x = 0.000341 + 1 * jax.random.normal(jax.random.fold_in(_rk, 1), (16, 256, 512), jnp.float32)
        _lenS = 256 - jax.random.randint(jax.random.fold_in(_rk, 7), (16,), 0, max(1, 256 // 4) + 1, jnp.int32)
        _lenS2 = 256 - jax.random.randint(jax.random.fold_in(_rk, 8), (16,), 0, max(1, 256 // 4) + 1, jnp.int32)
        _ctx_1024P = jax.random.normal(jax.random.fold_in(_rk, 11), (16, 16, 512), jnp.float32)
        _ctx_1024c = jax.random.dirichlet(jax.random.fold_in(_rk, 511), 0.3 * jnp.ones((16,), jnp.float32), (16, 256))
        _ctx_1024t = jnp.einsum('bsk,bkd->bsd', _ctx_1024c, _ctx_1024P)
        _ctx_1024t = _ctx_1024t * jax.lax.rsqrt(jnp.mean(jnp.square(_ctx_1024t)) + 1e-12) * 0.953939
        ctx_1024 = -0.000392918 + 0.999932 * (_ctx_1024t + 0.3 * jax.random.normal(jax.random.fold_in(_rk, 611), (16, 256, 512), jnp.float32))
        _validS = jnp.arange(256)[None, :] < _lenS[:, None]
        _validS2 = jnp.arange(256)[None, :] < _lenS2[:, None]
        _causal = jnp.tril(jnp.ones((256, 256), dtype=bool))
        mask_BxSxS2_ik1 = jnp.where(jnp.broadcast_to(_validS2[:, None, :], (16, 256, 256)), 1, 0).astype(jnp.int32)
        return (x, ctx_1024, mask_BxSxS2_ik1)
    x, ctx_1024, mask_BxSxS2_ik1 = _rec_inputs()

    def _L0_attn_setup():
        import jax, jax.numpy as jnp
        import numpy as np
        D_MODEL, D_K, D_V, H = (512, 64, 64, 16)
        B, N = (2, 1024)
        key = jax.random.key(seed)
        ks = jax.random.split(key, 5)
        y = jax.random.normal(ks[0], (B, N, D_MODEL), dtype=jnp.float32)
        Wq = 0.001 * jax.random.normal(ks[1], (H * D_K, D_MODEL), dtype=jnp.float32)
        Wk = 0.001 * jax.random.normal(ks[2], (H * D_K, D_MODEL), dtype=jnp.float32)
        Wv = 0.001 * jax.random.normal(ks[3], (H * D_V, D_MODEL), dtype=jnp.float32)
        Wo = 0.001 * jax.random.normal(ks[4], (D_MODEL, H * D_V), dtype=jnp.float32)
        bq = jnp.zeros((H * D_K,), jnp.float32)
        bk = jnp.zeros((H * D_K,), jnp.float32)
        bv = jnp.zeros((H * D_V,), jnp.float32)
        bo = jnp.zeros((D_MODEL,), jnp.float32)
        return {'y': y, 'Wq': Wq, 'bq': bq, 'Wk': Wk, 'bk': bk, 'Wv': Wv, 'bv': bv, 'Wo': Wo, 'bo': bo}
    _L0_attn_all = _L0_attn_setup()
    _L0_attn_in = {k: v for k, v in _L0_attn_all.items() if k in ('Wq', 'bq', 'Wk', 'bk', 'Wv', 'bv', 'Wo', 'bo')}
    del _L0_attn_all

    def _L0_xattn_setup():
        import jax, jax.numpy as jnp
        import numpy as np
        EMBED = 512
        HEAD_DIM = 64
        key = jax.random.key(seed)
        ks = jax.random.split(key, 9)
        B, L = (4, 2048)
        values = jax.random.normal(ks[0], (B, L, EMBED), dtype=jnp.float32)
        keys_ = jax.random.normal(ks[1], (B, L, EMBED), dtype=jnp.float32)
        queries = jax.random.normal(ks[2], (B, L, EMBED), dtype=jnp.float32)
        mask = jax.random.randint(ks[3], (B, L, L), 0, 2, dtype=jnp.int32)
        s = 1.0 / np.sqrt(EMBED)
        Wv = jax.random.normal(ks[4], (EMBED, HEAD_DIM), dtype=jnp.float32) * s
        Wk = jax.random.normal(ks[5], (EMBED, HEAD_DIM), dtype=jnp.float32) * s
        Wq = jax.random.normal(ks[6], (EMBED, HEAD_DIM), dtype=jnp.float32) * s
        Wo = jax.random.normal(ks[7], (HEAD_DIM, EMBED), dtype=jnp.float32) * (1.0 / np.sqrt(HEAD_DIM))
        bo = jnp.zeros((EMBED,), dtype=jnp.float32)
        return {'values': values, 'keys': keys_, 'queries': queries, 'mask': mask, 'Wv': Wv, 'Wk': Wk, 'Wq': Wq, 'Wo': Wo, 'bo': bo}
    _L0_xattn_all = _L0_xattn_setup()
    _L0_xattn_in = {k: v for k, v in _L0_xattn_all.items() if k in ('Wv', 'Wk', 'Wq', 'Wo', 'bo')}
    del _L0_xattn_all

    def _L0_ffn_setup():
        import jax, jax.numpy as jnp
        import numpy as np
        TOP_K = 8
        NUM_EXPERTS = 32
        CAPACITY = 512
        key = jax.random.key(seed)
        k1, k2, k3, k4 = jax.random.split(key, 4)
        B, S, H, E, F = (2, 512, 512, NUM_EXPERTS, 384)
        return {'hidden_states': jax.random.normal(k1, (B, S, H), dtype=jnp.float32), 'gate_weight': jax.random.normal(k2, (E, H), dtype=jnp.float32) * 0.02, 'gate_up_proj': jax.random.normal(k3, (E, 2 * F, H), dtype=jnp.float32) * 0.02, 'down_proj': jax.random.normal(k4, (E, H, F), dtype=jnp.float32) * 0.02}
    _L0_ffn_all = _L0_ffn_setup()
    _L0_ffn_in = {k: v for k, v in _L0_ffn_all.items() if k in ('gate_weight', 'gate_up_proj', 'down_proj')}
    del _L0_ffn_all
    return {'x': x, 'ctx_1024': ctx_1024, 'mask_BxSxS2_ik1': mask_BxSxS2_ik1, 'L0_attn_Wq': _L0_attn_in['Wq'], 'L0_attn_bq': _L0_attn_in['bq'], 'L0_attn_Wk': _L0_attn_in['Wk'], 'L0_attn_bk': _L0_attn_in['bk'], 'L0_attn_Wv': _L0_attn_in['Wv'], 'L0_attn_bv': _L0_attn_in['bv'], 'L0_attn_Wo': _L0_attn_in['Wo'], 'L0_attn_bo': _L0_attn_in['bo'], 'L0_xattn_Wv': _L0_xattn_in['Wv'], 'L0_xattn_Wk': _L0_xattn_in['Wk'], 'L0_xattn_Wq': _L0_xattn_in['Wq'], 'L0_xattn_Wo': _L0_xattn_in['Wo'], 'L0_xattn_bo': _L0_xattn_in['bo'], 'L0_ffn_gate_weight': _L0_ffn_in['gate_weight'], 'L0_ffn_gate_up_proj': _L0_ffn_in['gate_up_proj'], 'L0_ffn_down_proj': _L0_ffn_in['down_proj']}

def reference(x, ctx_1024, mask_BxSxS2_ik1, L0_attn_Wq, L0_attn_bq, L0_attn_Wk, L0_attn_bk, L0_attn_Wv, L0_attn_bv, L0_attn_Wo, L0_attn_bo, L0_xattn_Wv, L0_xattn_Wk, L0_xattn_Wq, L0_xattn_Wo, L0_xattn_bo, L0_ffn_gate_weight, L0_ffn_gate_up_proj, L0_ffn_down_proj):
    import jax
    import jax.numpy as jnp

    def _L0_attn_ref(y, Wq, bq, Wk, bk, Wv, bv, Wo, bo):
        import jax, jax.numpy as jnp
        import numpy as np
        D_MODEL, D_K, D_V, H = (512, 64, 64, 16)
        B, N = (2, 1024)
        b_s, n, _ = y.shape
        scale = 1.0 / np.sqrt(D_K).astype(np.float32)
        q = (jnp.einsum('bnd,ed->bne', y, Wq) + bq).reshape(b_s, n, H, D_K).transpose(0, 2, 1, 3)
        k = (jnp.einsum('bnd,ed->bne', y, Wk) + bk).reshape(b_s, n, H, D_K).transpose(0, 2, 1, 3)
        v = (jnp.einsum('bnd,ed->bne', y, Wv) + bv).reshape(b_s, n, H, D_V).transpose(0, 2, 1, 3)
        att = jnp.einsum('bhqd,bhkd->bhqk', q, k) * scale
        att = jax.nn.softmax(att, axis=-1)
        out = jnp.einsum('bhqk,bhkd->bhqd', att, v)
        out = out.transpose(0, 2, 1, 3).reshape(b_s, n, H * D_V)
        out = jnp.einsum('bne,de->bnd', out, Wo) + bo
        return out

    def _L0_xattn_ref(values, keys, queries, mask, Wv, Wk, Wq, Wo, bo):
        import jax, jax.numpy as jnp
        import numpy as np
        EMBED = 512
        HEAD_DIM = 64
        v = jnp.einsum('ble,ed->bld', values, Wv)
        k = jnp.einsum('ble,ed->bld', keys, Wk)
        q = jnp.einsum('ble,ed->bld', queries, Wq)
        scale = 1.0 / jnp.sqrt(jnp.asarray(HEAD_DIM, dtype=q.dtype))
        scores = jnp.einsum('bqd,bkd->bqk', q, k) * scale
        scores = scores + mask.astype(scores.dtype) * -1000000000.0
        attn = jax.nn.softmax(scores, axis=-1)
        out = jnp.einsum('bqk,bkd->bqd', attn, v)
        return jnp.einsum('bqd,de->bqe', out, Wo) + bo

    def _L0_ffn_ref(hidden_states, gate_weight, gate_up_proj, down_proj):
        import jax, jax.numpy as jnp
        import numpy as np
        TOP_K = 8
        NUM_EXPERTS = 32
        CAPACITY = 512
        B, S, H = hidden_states.shape
        E = gate_weight.shape[0]
        N = B * S
        x = hidden_states.reshape(N, H)
        logits = x @ gate_weight.T
        probs = jax.nn.softmax(logits.astype(jnp.float32), axis=-1)
        topw, topi = jax.lax.top_k(probs, TOP_K)
        topw = topw / topw.sum(-1, keepdims=True)
        topw = topw.astype(x.dtype)
        flat_e = topi.reshape(-1)
        flat_w = topw.reshape(-1)
        flat_x = jnp.repeat(x, TOP_K, axis=0)
        oh = jax.nn.one_hot(flat_e, E, dtype=jnp.int32)
        pos = (jnp.cumsum(oh, axis=0) * oh).sum(-1) - 1
        buf = jnp.zeros((E, CAPACITY, H), x.dtype).at[flat_e, pos].set(flat_x, mode='drop')
        gu = jnp.einsum('ech,efh->ecf', buf, gate_up_proj)
        gate, up = jnp.split(gu, 2, axis=-1)
        h = jax.nn.silu(gate) * up
        eo = jnp.einsum('ecf,ehf->ech', h, down_proj)
        tok_out = eo.at[flat_e, pos].get(mode='fill', fill_value=0)
        out = (tok_out * flat_w[:, None]).reshape(N, TOP_K, H).sum(1)
        return out.reshape(B, S, H)
    x = _layernorm(x + _L0_attn_ref(x, L0_attn_Wq, L0_attn_bq, L0_attn_Wk, L0_attn_bk, L0_attn_Wv, L0_attn_bv, L0_attn_Wo, L0_attn_bo), axis=-1)
    x = _layernorm(x + _L0_xattn_ref(ctx_1024, ctx_1024, x, mask_BxSxS2_ik1, L0_xattn_Wv, L0_xattn_Wk, L0_xattn_Wq, L0_xattn_Wo, L0_xattn_bo), axis=-1)
    x = _layernorm(x + _L0_ffn_ref(x, L0_ffn_gate_weight, L0_ffn_gate_up_proj, L0_ffn_down_proj), axis=-1)
    return x

_drawn_inputs = setup_inputs


def setup_inputs(seed=0):
    import zlib

    import numpy as np

    out = dict(_drawn_inputs(seed))
    spreads = {'L0_attn_bq': (0.0, 2.0),
     'L0_attn_bk': (0.0, 2.0),
     'L0_attn_bv': (0.0, 0.8),
     'L0_attn_bo': (0.0, 0.1),
     'L0_xattn_bo': (0.0, 0.1)}
    factors = {'L0_attn_Wq': 64.0,
     'L0_attn_Wk': 25.547,
     'L0_attn_Wv': 8.0,
     'L0_attn_Wo': 8.0,
     'L0_ffn_gate_weight': 5.67,
     'L0_ffn_gate_up_proj': 4.939,
     'L0_ffn_down_proj': 4.943}
    for name, (base, spread) in spreads.items():
        noise = np.random.default_rng([zlib.crc32(name.encode()), seed]).standard_normal(out[name].shape)
        drawn = base * np.exp(spread * noise) if base else spread * noise
        out[name] = jnp.asarray(drawn.astype(out[name].dtype))
    for name, factor in factors.items():
        out[name] = (out[name] * factor).astype(out[name].dtype)
    return out
```

```python
import concourse.bass as bass
from concourse import mybir
from contextlib import ExitStack


F32 = mybir.dt.float32
F16 = mybir.dt.float16
I32 = mybir.dt.int32
ALU = mybir.AluOpType
ACT = mybir.ActivationFunctionType
AX = mybir.AxisListType

P = 128
B, S, D = 16, 256, 512
N = B * S
H, DK = 16, 64
E = H * DK
DC = D // P
EC = E // P
TT = S // P
NX, TOP, CAP, F = 32, 8, 512, 384
FC = F // P
CC = CAP // P
XD = 64
WGU = DC * 2 * F
WDN = FC * D
EPS = 1e-5
SCORE = 1.0 / 8.0
W_SCALE = 256.0
P_SCALE = 4096.0
G_SCALE = 256.0
PARTS = ((0, 0), (0, 1), (1, 0))


def count(b, per, c=0):
    return b * per + c


def past(eng, sem, value):
    if isinstance(value, int) and value <= 0:
        return
    eng.wait_ge(sem, value)


def wait_apart(eng, sem, value, held, times):
    if not isinstance(value, int):
        value = eng.snap(eng.to_reg(value))
    eng.wait_ge(held, times)
    past(eng, sem, value)


def build(nc, xT, x_rows, ctxT, mask, wqT, wkT, wvT, woT, bq, bk, bv, bo,
          x_wv, x_wk, x_wq, x_wo, x_bo, gateT, wguT, wdnT, out):
    ctx = ExitStack()
    with ctx:
        def sb(name, shape, dt=F32):
            return ctx.enter_context(nc.sbuf_tensor(name, shape, dt))

        def sem(name):
            return ctx.enter_context(nc.semaphore(name))

        x2_rows = nc.dram_tensor("x2_rows", [N, D], F32, kind="Internal").ap()
        acc_rows = nc.dram_tensor("acc_rows", [N + CAP, D], F32, kind="Internal").ap()

        arena_w = sb("arena_w", [P, 3 * 2 * DC * E], F16)
        wqkv = arena_w[:, :].rearrange("p (w s c n) -> p w s c n", w=3, s=2, c=DC)
        arena_o = sb("arena_o", [P, 2 * EC * D], F16)
        wo = arena_o[:, :].rearrange("p (s c n) -> p s c n", s=2, c=EC)
        wx = sb("wx", [P, 2, 3, DC, XD], F16)
        wxo = sb("wxo", [XD, 2, D], F16)
        gate_w = sb("gate_w", [P, DC, NX])
        stage = sb("stage", [P, 2, WGU + WDN])
        bqkv = sb("bqkv", [P, 3, EC])
        bo_row = sb("bo_row", [P, D])
        xbo_row = sb("xbo_row", [P, D])

        ident = sb("ident", [P, P])
        before = sb("before", [P, P], F16)
        ones = sb("ones", [P, P], F16)
        iota = sb("iota", [P, P])
        row_i = sb("row_i", [P, 1], I32)
        row1 = sb("row1", [P, 1])
        thr_i = sb("thr_i", [P, CC], I32)
        thr = sb("thr", [P, CC])
        spare_i = sb("spare_i", [P, CC], I32)
        spare = sb("spare", [P, CC])
        neg_half = sb("neg_half", [P, 4])

        xt32 = sb("xt32", [P, DC, S])
        xt = sb("xt", [P, 2, DC, S], F16)
        qk32 = sb("qk32", [P, 2, 2 * S])
        qk = sb("qk", [P, 2, 2, 2 * S], F16)
        arena_v = sb("arena_v", [P, 2 * TT * E], F16)
        v = arena_v[:, :].rearrange("p (s t e) -> p s t e", s=2, t=TT)
        arena_p = sb("arena_p", [P, 4096])
        probs = arena_p[:, 0:2048].rearrange("p (b h q k) -> p b h q k", b=2, h=2, q=TT)
        pT = arena_p[:, 2048:4096].bitcast(F16).rearrange("p (b s h n) -> p b s h n", b=2, s=2, h=2)
        s_max = sb("s_max", [P, 2, 4])
        s_neg = sb("s_neg", [P, 2, 4])
        s_den = sb("s_den", [P, 2, 4])
        s_rden = sb("s_rden", [P, 2, 4])
        o32 = sb("o32", [P, 2, S])
        arena_a = sb("arena_a", [P, 2 * EC * S], F16)
        o = arena_a[:, :].rearrange("p (s j n) -> p s j n", s=2, j=EC)

        xr = sb("xr", [P, TT, D])
        z = sb("z", [P, TT, D])
        before_f32 = z[:, 0, 0:P]
        iota_i = z[:, 0, P:2 * P].bitcast(I32)
        x1 = sb("x1", [P, TT, D])
        x2 = sb("x2", [P, TT, D])
        stats1 = sb("stats1", [P, TT, 6])
        mv1 = sb("mv1", [P, TT, 2])
        ve1 = sb("ve1", [P, TT])
        rstd1 = sb("rstd1", [P, TT])
        stats2 = sb("stats2", [P, TT, 6])
        mv2 = sb("mv2", [P, TT, 2])
        ve2 = sb("ve2", [P, TT])
        rstd2 = sb("rstd2", [P, TT])

        ct32 = stage[:, 1, 0:1024].rearrange("p (c n) -> p c n", c=DC)
        ct = sb("ct", [P, 2, DC, S], F16)
        mask_i = sb("mask_i", [P, TT, S], I32)
        mask_add = stage[:, 1, 4096:4608].rearrange("p (t n) -> p t n", t=TT)
        x1T = sb("x1T", [P, 2, DC, S], F16)
        q2 = sb("q2", [XD, 2, S], F16)
        k2 = sb("k2", [XD, 2, S], F16)
        v2 = sb("v2", [P, 2, TT, XD], F16)
        p2 = sb("p2", [P, TT, S])
        m2 = sb("m2", [P, TT])
        n2 = sb("n2", [P, TT])
        den2 = sb("den2", [P, TT])
        rden2 = sb("rden2", [P, TT])
        p2T = sb("p2T", [P, 2, 2, S], F16)
        o2 = sb("o2", [XD, 2, S], F16)

        x2T = stage[:, 1, 1024:2048].rearrange("p (c n) -> p c n", c=DC)
        top_l = sb("top_l", [P, TT, 8])
        neg_l = sb("neg_l", [P, TT])
        ex = sb("ex", [P, TT, NX])
        den_l = sb("den_l", [P, TT])
        rden_l = sb("rden_l", [P, TT])
        pr = sb("pr", [P, TT, NX])
        top_p = sb("top_p", [P, TT, 8])
        left = sb("left", [P, TT, NX])
        sel = sb("sel", [P, TT, NX], F16)
        sel_sum = sb("sel_sum", [P, 2, NX], F16)
        w_sum = sb("w_sum", [P, TT])
        w_rsum = sb("w_rsum", [P, TT])
        w32 = sb("w32", [P, TT, NX])
        w_hi = sb("w_hi", [P, TT, NX], F16)
        w_lo = sb("w_lo", [P, TT, NX], F16)
        ge = sb("ge", [P, TT * NX, CC + 1])
        n_ge = sb("n_ge", [P, TT * NX])
        pos_in = sb("pos_in", [P, TT * NX])
        in_chunk = sb("in_chunk", [P, TT * NX, CC])
        chosen = sb("chosen", [P, TT * NX, CC])
        tile_no = sb("tile_no", [P, TT])
        said = sb("said", [P, TT * NX, 4, CC], F16)
        onehot = stage[:, 1, 2048:4096].bitcast(F16).rearrange("p (t e n) -> p t e n", t=TT, e=NX // 2)
        slots = sb("slots", [P, NX, 4, CC])
        tok, tok0, empty = in_chunk[:, 0:NX, :], in_chunk[:, NX:2 * NX, :], chosen[:, 0:NX, :]
        idx_from = sb("idx_from", [P, NX, CC], I32)
        idx_to = sb("idx_to", [P, NX, CC], I32)
        w_slot = sb("w_slot", [P, NX, CC])
        cur_from = sb("cur_from", [P, 2, CC], I32)
        cur_to = sb("cur_to", [P, 2, CC], I32)
        cur_w = sb("cur_w", [P, 2, CC])
        stats3 = sb("stats3", [P, 2, 4, 6])
        mv3 = sb("mv3", [P, 2, 4, 2])
        ve3 = sb("ve3", [P, 2, 4])
        rstd3 = sb("rstd3", [P, 2, 4])

        NW = WGU + WDN
        ew = arena_w[:, 0:4 * NW].rearrange("p (b s n) -> p b s n", b=2, s=2)
        ew_gu = ew[:, :, :, 0:WGU].rearrange("p b s (c f) -> p b s c f", c=DC)
        ew_dn = ew[:, :, :, WGU:NW].rearrange("p b s (c n) -> p b s c n", c=FC)
        hT = arena_w[:, 4 * NW:4 * NW + 2 * FC * CAP].rearrange("p (s f n) -> p s f n", s=2, f=FC)
        y = arena_o[:, :].bitcast(F32).rearrange("p (b c n) -> p b c n", b=2, c=CC)
        xg = arena_p[:, :].rearrange("p (b c n) -> p b c n", b=2, c=CC)
        xgT = arena_v[:, :].rearrange("p (s c n) -> p s c n", s=2, c=DC)
        act32 = arena_a[:, :].bitcast(F32).rearrange("p (k b n) -> p k b n", k=2, b=2)
        silu, h32 = act32[:, 0], act32[:, 1]

        bank = [ctx.enter_context(nc.psum_tensor(f"bank{i}", [P, 512], F32)) for i in range(8)]
        ps_qk = bank[0]
        ps_v = bank[1]
        ps_s = bank[2:4]
        ps_t = bank[4:6]
        ps_o = bank[6]
        ps_x = bank[7]
        ps_gate = bank[7][:, 0:TT * NX].rearrange("p (t e) -> p t e", t=TT)
        ps_pos = bank[7][:, 0:TT * NX]
        ps_slot = bank[1][:, 0:256]
        ps_h = (bank[0:2], bank[2:4])
        ps_xg = bank[4:6]
        ps_y = bank[6:8]

        HX = NX // 2

        s_const = sem("s_const")
        s_constv = sem("s_constv")
        ld_w = [sem("ld_w0"), sem("ld_w1")]
        ld_small = sem("ld_small")
        w_split_hi = sem("w_split_hi")
        w_split_lo = sem("w_split_lo")
        ld_x, ld_row, ld_ctx, ld_mask = sem("ld_x"), sem("ld_row"), sem("ld_ctx"), sem("ld_mask")
        xt_hi, xt_lo = sem("xt_hi"), sem("xt_lo")
        qk_mm, qk_hi, qk_lo = sem("qk_mm"), sem("qk_hi"), sem("qk_lo")
        s_mm, s_maxd, s_negd = sem("s_mm"), sem("s_maxd"), sem("s_negd")
        e_done, r_done, p_done = sem("e_done"), sem("r_done"), sem("p_done")
        t_mm, pt_hi, pt_lo = sem("t_mm"), sem("pt_hi"), sem("pt_lo")
        v_mm, v_hi, v_lo = sem("v_mm"), sem("v_hi"), sem("v_lo")
        pv_mm, o_hi, o_lo = sem("pv_mm"), sem("o_hi"), sem("o_lo")
        wo_mm, xb_done = sem("wo_mm"), sem("xb_done")
        ln1, ln1_rstd, x1_done, x1b_done = sem("ln1"), sem("ln1_rstd"), sem("x1_done"), sem("x1b_done")
        x1t_mm, x1t_hi, x1t_lo = sem("x1t_mm"), sem("x1t_hi"), sem("x1t_lo")
        ct_hi, ct_lo = sem("ct_hi"), sem("ct_lo")
        kv_mm, kv_hi, kv_lo = sem("kv_mm"), sem("kv_hi"), sem("kv_lo")
        q2_mm, q2_hi, q2_lo = sem("q2_mm"), sem("q2_hi"), sem("q2_lo")
        s2_mm, mask_done, s2_dve = sem("s2_mm"), sem("mask_done"), sem("s2_dve")
        e2_done, r2_done, p2_done = sem("e2_done"), sem("r2_done"), sem("p2_done")
        t2_mm, t2_hi, t2_lo = sem("t2_mm"), sem("t2_hi"), sem("t2_lo")
        pv2_mm, o2_hi, o2_lo = sem("pv2_mm"), sem("o2_hi"), sem("o2_lo")
        out2_mm = sem("out2_mm")
        ln2, ln2_rstd, x2_done = sem("ln2"), sem("ln2_rstd"), sem("x2_done")
        st_x2 = sem("st_x2")
        x2t_mm, x2t_done = sem("x2t_mm"), sem("x2t_done")
        gate_mm, rt_exp, rt = sem("gate_mm"), sem("rt_exp"), sem("rt")
        pos_mm, oh_done, slot_mm, slot_done = sem("pos_mm"), sem("oh_done"), sem("slot_mm"), sem("slot_done")
        table = sem("table")
        cur_done = sem("cur_done")
        ld_xg = [sem("ld_xg0"), sem("ld_xg1")]
        xg_mm, xg_hi, xg_lo = sem("xg_mm"), sem("xg_hi"), sem("xg_lo")
        ew_hi, ew_lo_gu, ew_lo_dn = sem("ew_hi"), sem("ew_lo_gu"), sem("ew_lo_dn")
        g_mm, u_mm, silu_done = sem("g_mm"), sem("u_mm"), sem("silu_done")
        h_f32, h_hi, h_lo = sem("h_f32"), sem("h_hi"), sem("h_lo")
        y_mm, y_done = sem("y_mm"), sem("y_done")
        st_y = sem("st_y")
        st_zero = sem("st_zero")
        ld_acc = [sem("ld_acc0"), sem("ld_acc1")]
        ln3, ln3_rstd, out_done = sem("ln3"), sem("ln3_rstd"), sem("out_done")
        st_out = [sem("st_out0"), sem("st_out1")]

        RT = 27
        N_CONST, N_CONSTV = 12, 8
        SETUP = 6

        def rounds(eng, work):
            work(0, True, False, False, False)
            work(1, True, True, False, False)
            work(2, True, True, True, False)
            work(3, True, True, True, True)
            with eng.Fori(4, B) as r:
                work(r, True, True, True, True)
            work(B, False, True, True, True)
            work(B + 1, False, False, True, True)
            work(B + 2, False, False, False, True)

        def pairs(b, head, tail):
            def call(stage_of, j):
                if j >= 0 and head:
                    stage_of(b, j)
                elif j < 0 and tail:
                    stage_of(b - 1, j + EC)
            return call

        def cols(r):
            return bass.ds(r * S, S)

        def rows_of(ap, b):
            return ap[bass.ds(b * S, S), :].rearrange("(t p) n -> p t n", p=P)

        block = ctx.enter_context(nc.Block())

        @block.sync
        def _(sp):
            def weight(n, dst, src):
                if n >= 2:
                    sp.wait_ge(w_split_hi, n - 1)
                    sp.wait_ge(w_split_lo, n - 1)
                sp.dma_start(dst, src).then_inc(ld_w[n % 2], 16)

            def staged(n, c):
                return stage[:, n % 2, 0:4096].rearrange("p (c n) -> p c n", c=c)

            weight(0, staged(0, DC), wqT.rearrange("(c p) n -> p c n", p=P))
            sp.dma_start(xt32[:, :, :], xT[:, 0:S].rearrange("(c p) n -> p c n", p=P)).then_inc(ld_x, 16)
            weight(1, staged(1, DC), wkT.rearrange("(c p) n -> p c n", p=P))
            for k, src in enumerate((bq, bk, bv)):
                sp.dma_start(bqkv[:, k, :], src).then_inc(ld_small, 16)
            sp.dma_start(bo_row[:, :], bo.partition_broadcast(P)).then_inc(ld_small, 16)
            sp.dma_start(xbo_row[:, :], x_bo.partition_broadcast(P)).then_inc(ld_small, 16)
            sp.dma_start(gate_w[:, :, :], gateT.rearrange("(c p) n -> p c n", p=P)).then_inc(ld_small, 16)
            weight(2, staged(2, DC), wvT.rearrange("(c p) n -> p c n", p=P))
            weight(3, staged(3, EC), woT.rearrange("(c p) n -> p c n", p=P))
            sp.wait_ge(w_split_hi, 3)
            sp.wait_ge(w_split_lo, 3)
            for k, src in enumerate((x_wq, x_wk, x_wv)):
                sp.dma_start(stage[:, 0, k * DC * XD:(k + 1) * DC * XD].rearrange("p (c n) -> p c n", c=DC),
                             src.rearrange("(c p) n -> p c n", p=P)).then_inc(ld_w[0], 16)
            weight(5, stage[0:XD, 1, 0:D], x_wo)

            def load_expert(e, k):
                sp.dma_start(stage[:, k, 0:WGU].rearrange("p (c f) -> p c f", c=DC),
                             wguT[e].rearrange("(c p) f -> p c f", p=P)).then_inc(ld_w[k], 16)
                sp.dma_start(stage[:, k, WGU:NW].rearrange("p (c n) -> p c n", c=FC),
                             wdnT[e].rearrange("(c p) n -> p c n", p=P)).then_inc(ld_w[k], 16)

            def work(r, head, tail, route, fill):
                if head and not (isinstance(r, int) and r == 0):
                    sp.wait_ge(xt_hi, count(r, 1))
                    sp.wait_ge(xt_lo, count(r, 1))
                    sp.dma_start(xt32[:, :, :], xT[:, cols(r)].rearrange("(c p) n -> p c n", p=P)).then_inc(ld_x, 16)
                if tail:
                    t = r - 1
                    if isinstance(r, int) and r == 1:
                        sp.wait_ge(w_split_hi, SETUP)
                        sp.wait_ge(w_split_lo, SETUP)
                    past(sp, ct_hi, count(t, 1))
                    past(sp, ct_lo, count(t, 1))
                    sp.dma_start(ct32[:, :, :], ctxT[:, cols(t)].rearrange("(c p) n -> p c n", p=P)).then_inc(ld_ctx, 16)
                    past(sp, mask_done, count(t, 1))
                    sp.dma_start(mask_i[:, :, :], rows_of(mask, t)).then_inc(ld_mask, 16)
                    past(sp, ln1, count(t, 7))
                    sp.dma_start(xr[:, :, :], rows_of(x_rows, t)).then_inc(ld_row, 16)
                if route:
                    t = r - 2
                    sp.wait_ge(x2_done, count(t, TT, TT))
                    sp.dma_start(rows_of(x2_rows, t), x2[:, :, :]).then_inc(st_x2, 16)
                    sp.dma_start(rows_of(acc_rows, t), x2[:, :, :]).then_inc(st_x2, 16)
                if isinstance(r, int) and r == 1:
                    load_expert(0, 0)

            rounds(sp, work)
            sp.wait_ge(slot_mm, B * 2)
            load_expert(1, 1)

            def expert(e, k, ahead):
                if ahead:
                    sp.wait_ge(ew_hi, count(e, 1, 1))
                    sp.wait_ge(ew_lo_gu, count(e, 1, 1))
                    sp.wait_ge(ew_lo_dn, count(e, 1, 1))
                    load_expert(e + 2, k)

            with sp.Fori(0, NX - 3, 2) as e:
                expert(e, 0, True)
                expert(e + 1, 1, True)

            sp.wait_ge(st_y, NX * 64)
            sp.wait_ge(y_done, NX * CC)
            GR = 4 * P

            def take(g, k):
                past(sp, out_done, count(g, 4, -4))
                sp.dma_start(y[:, k], acc_rows[bass.ds(g * GR, GR), :].rearrange("(t p) n -> p t n", p=P))\
                  .then_inc(ld_acc[k], 16)

            def give(g, k):
                sp.wait_ge(out_done, count(g, 4, 4))
                sp.dma_start(out[bass.ds(g * GR, GR), :].rearrange("(t p) n -> p t n", p=P), xg[:, k])\
                  .then_inc(st_out[k], 16)

            take(0, 0)
            take(1, 1)
            with sp.Fori(0, N // GR - 3, 2) as g:
                give(g, 0)
                take(g + 2, 0)
                give(g + 1, 1)
                take(g + 3, 1)
            give(N // GR - 2, 0)
            give(N // GR - 1, 1)
            sp.wait_ge(st_out[0], N // GR // 2 * 16)
            sp.wait_ge(st_out[1], N // GR // 2 * 16)

        @block.tensor
        def _(pe):
            def split_mm(out_ap, lhs, rhs, chunks):
                for n, (a, c) in enumerate(PARTS):
                    for i in range(chunks):
                        mm = pe.matmul(out_ap, lhs(a, i), rhs(c, i),
                                       start=(n == 0 and i == 0), stop=(n == 2 and i == chunks - 1))
                return mm

            def qk_pair(b, j):
                if j == 0:
                    pe.wait_ge(xt_lo, count(b, 1, 1))
                if isinstance(b, int) and b == 0 and j == 0:
                    pe.wait_ge(w_split_lo, 2)
                past(pe, qk_hi, count(b, EC, j))
                for w in range(2):
                    mm = split_mm(ps_qk[:, w * S:(w + 1) * S],
                                  lambda a, i: wqkv[:, w, a, i, j * P:(j + 1) * P],
                                  lambda c, i: xt[:, c, i, :], DC)
                mm.then_inc(qk_mm, 1)

            def scores(b, j):
                past(pe, e_done, count(b, EC, j))
                pe.wait_ge(qk_lo, count(b, EC, j + 1))
                pe.wait_ge(s_const, N_CONST)
                for n, (a, c) in enumerate(PARTS):
                    for t in range(TT):
                        for h in range(2):
                            hp = slice(h * DK, (h + 1) * DK)
                            mm = pe.matmul(ps_s[h][:, t * S:(t + 1) * S],
                                           qk[hp, j % 2, a, t * P:(t + 1) * P], qk[hp, j % 2, c, S:2 * S],
                                           start=(n == 0 and t == 0), stop=(n == 2 and t == TT - 1),
                                           skip_group_check=True)
                mm.then_inc(s_mm, 1)

            def values(b, g, tail, fill):
                half, t = g // 2, g % 2
                if isinstance(b, int) and b == 0 and g == 0:
                    pe.wait_ge(w_split_lo, 3)
                if g == 0 and fill:
                    pe.wait_ge(slot_done, count(b - 3, 2, 1))
                elif g == 0 and tail:
                    past(pe, kv_lo, count(b - 1, 2))
                if g:
                    pe.wait_ge(v_lo, count(b, 4, g))
                if g == 2 and fill:
                    pe.wait_ge(slot_done, count(b - 3, 2, 2))
                split_mm(ps_v[:, :],
                         lambda a, i: xt[:, a, i, t * P:(t + 1) * P],
                         lambda c, i: wqkv[:, 2, c, i, half * 512:(half + 1) * 512], DC).then_inc(v_mm, 1)

            def turn(b, j):
                pe.wait_ge(p_done, count(b, EC, j + 1))
                past(pe, pt_lo, count(b, 2 * EC, 2 * j))
                for h in range(2):
                    for c in range(2):
                        for t in range(TT):
                            mm = pe.transpose(ps_t[h][:, c * S + t * P:c * S + (t + 1) * P],
                                              probs[:, j % 2, h, t, c * P:(c + 1) * P], ident[:, :])
                    mm.then_inc(t_mm, 1)

            def weigh(b, j):
                past(pe, o_hi, count(b, EC, j))
                if j in (0, EC // 2):
                    pe.wait_ge(v_lo, count(b, 4, 2 if j == 0 else 4))
                pe.wait_ge(pt_lo, count(b, 2 * EC, 2 * j + 2))
                for n, (a, c) in enumerate(PARTS):
                    for i in range(2):
                        for h in range(2):
                            mm = pe.matmul(ps_o[h * DK:(h + 1) * DK, 0:S],
                                           v[:, a, i, (2 * j + h) * DK:(2 * j + h + 1) * DK],
                                           pT[:, j % 2, c, h, i * S:(i + 1) * S],
                                           start=(n == 0 and i == 0), stop=(n == 2 and i == 1),
                                           skip_group_check=True)
                mm.then_inc(pv_mm, 1)

            def project(b, t, route):
                if t == 0:
                    if isinstance(b, int) and b == 0:
                        pe.wait_ge(w_split_lo, SETUP)
                    pe.wait_ge(o_lo, count(b, EC, EC))
                    if route:
                        pe.wait_ge(x2t_done, count(b - 1, TT, TT))
                else:
                    pe.wait_ge(ln1, count(b, 7, t))
                split_mm(ps_x[:, :], lambda a, i: o[:, a, i, t * P:(t + 1) * P],
                         lambda c, i: wo[:, c, i, :], EC).then_inc(wo_mm, 1)

            def turn_x1(b, t, head, route, fill):
                pe.wait_ge(x1_done, count(b, TT, t + 1))
                if t == 0 and head:
                    pe.wait_ge(v_lo, count(b + 1, 4, 4))
                elif t == 0 and fill:
                    pe.wait_ge(slot_done, count(b - 2, 2, 2))
                elif t and route:
                    pe.wait_ge(rt, count(b - 1, RT, 20))
                into = (ps_v, ps_x)[t]
                for c in range(DC):
                    mm = pe.transpose(into[:, c * P:(c + 1) * P], x1[:, t, c * P:(c + 1) * P], ident[:, :])
                mm.then_inc(x1t_mm, 1)

            def ctx_kv(b):
                pe.wait_ge(ct_lo, count(b, 1, 1))
                pe.wait_ge(x1t_lo, count(b, TT, 1))
                split_mm(ps_v[0:XD, 0:S], lambda a, i: wx[:, a, 1, i, :], lambda c, i: ct[:, c, i, :], DC)
                for t in range(TT):
                    mm = split_mm(ps_v[:, S + t * XD:S + (t + 1) * XD],
                                  lambda a, i: ct[:, a, i, t * P:(t + 1) * P], lambda c, i: wx[:, c, 2, i, :], DC)
                mm.then_inc(kv_mm, 1)

            def cross_q(b):
                pe.wait_ge(x1t_lo, count(b, TT, TT))
                split_mm(ps_x[0:XD, 0:S], lambda a, i: wx[:, a, 0, i, :], lambda c, i: x1T[:, c, i, :], DC)\
                    .then_inc(q2_mm, 1)

            def cross_scores(b):
                pe.wait_ge(q2_lo, count(b, 1, 1))
                pe.wait_ge(kv_lo, count(b, 2, 1))
                pe.wait_ge(s_const, N_CONST)
                for t in range(TT):
                    mm = split_mm(ps_x[:, t * S:(t + 1) * S], lambda a, i: q2[:, a, t * P:(t + 1) * P],
                                  lambda c, i: k2[:, c, :], 1)
                mm.then_inc(s2_mm, 1)

            def cross_turn(b):
                pe.wait_ge(p2_done, count(b, 1, 1))
                for c in range(2):
                    for t in range(TT):
                        mm = pe.transpose(ps_x[:, c * S + t * P:c * S + (t + 1) * P],
                                          p2[:, t, c * P:(c + 1) * P], ident[:, :])
                mm.then_inc(t2_mm, 1)

            def cross_weigh(b):
                pe.wait_ge(t2_lo, count(b, 1, 1))
                split_mm(ps_x[0:XD, 0:S], lambda a, i: v2[:, a, i, :], lambda c, i: p2T[:, c, i, :], 2)\
                    .then_inc(pv2_mm, 1)

            def cross_project(b, t):
                if t == 0:
                    pe.wait_ge(o2_lo, count(b, 1, 1))
                else:
                    pe.wait_ge(ln2, count(b, 7, t))
                pe.wait_ge(s_const, N_CONST)
                split_mm(ps_x[:, :], lambda a, i: o2[:, a, t * P:(t + 1) * P], lambda c, i: wxo[:, c, :], 1)\
                    .then_inc(out2_mm, 1)

            def turn_x2(b, t):
                pe.wait_ge(x2_done, count(b, TT, t + 1))
                if t:
                    pe.wait_ge(x2t_done, count(b, TT, t))
                for c in range(DC):
                    mm = pe.transpose(ps_x[:, c * P:(c + 1) * P], x2[:, t, c * P:(c + 1) * P], ident[:, :])
                mm.then_inc(x2t_mm, 1)

            def gate(b, tail):
                pe.wait_ge(x2t_done, count(b, TT, TT))
                if tail:
                    pe.wait_ge(ln1, count(b + 1, 7, TT))
                for t in range(TT):
                    for c in range(DC):
                        mm = pe.matmul(ps_gate[:, t, :], x2T[:, c, t * P:(t + 1) * P], gate_w[:, c, :],
                                       start=(c == 0), stop=(c == DC - 1))
                mm.then_inc(gate_mm, 1)

            def positions(b):
                pe.wait_ge(rt, count(b, RT, 11))
                for t in range(TT):
                    pe.matmul(ps_pos[:, t * NX:(t + 1) * NX], before[:, :], sel[:, t, :], start=True, stop=False)
                    mm = pe.matmul(ps_pos[:, t * NX:(t + 1) * NX], ones[:, :], sel_sum[:, t, :],
                                   start=False, stop=True)
                mm.then_inc(pos_mm, 1)

            def fill_slots(b, k, head):
                pe.wait_ge(oh_done, count(b, 2 * TT, TT * (k + 1)))
                past(pe, slot_done, count(b, 2, k))
                if k == 0:
                    pe.wait_ge(rt, count(b, RT, 26))
                    pe.wait_ge(kv_lo, count(min(b + 2, B) if isinstance(b, int) else b + 2, 2))
                elif head:
                    pe.wait_ge(v_lo, count(b + 3, 4, 2))
                for e in range(HX):
                    for t in range(TT):
                        mm = pe.matmul(ps_slot[:, e * 16:(e + 1) * 16], onehot[:, t, e, :],
                                       said[:, t * NX + k * HX + e, :, :].rearrange("p a c -> p (a c)"),
                                       start=(t == 0), stop=(t == TT - 1))
                mm.then_inc(slot_mm, 1)

            def work(r, head, tail, route, fill):
                b, t, u, f = r, r - 1, r - 2, r - 3
                pair = pairs(r, head, tail)

                def step(s, between=()):
                    pair(scores, s - 2)
                    pair(turn, s - 3)
                    for on, run in between:
                        if on:
                            run()
                    pair(weigh, s - 4)
                    if head:
                        qk_pair(b, s)

                step(0, [(fill, lambda: fill_slots(f, 0, head))])
                if head:
                    values(b, 0, tail, fill)
                step(1, [(route, lambda: cross_turn(u))])
                if route:
                    cross_weigh(u)
                if head:
                    values(b, 1, tail, fill)
                step(2, [(route, lambda: cross_project(u, 0)), (fill, lambda: fill_slots(f, 1, head))])
                if route:
                    cross_project(u, 1)
                step(3)
                if route:
                    turn_x2(u, 0)
                if head:
                    values(b, 2, tail, fill)
                if route:
                    turn_x2(u, 1)
                step(4, [(tail, lambda: project(t, 0, route))])
                if tail:
                    project(t, 1, route)
                step(5, [(route, lambda: gate(u, tail))])
                if head:
                    values(b, 3, tail, fill)
                step(6, [(tail, lambda: turn_x1(t, 0, head, route, fill)), (route, lambda: positions(u))])
                if tail:
                    turn_x1(t, 1, head, route, fill)
                step(7, [(tail, lambda: ctx_kv(t)), (tail, lambda: cross_q(t))])
                if tail:
                    cross_scores(t)

            rounds(pe, work)

            def up_gate(e, k):
                pe.wait_ge(xg_lo, count(e, CC, CC))
                pe.wait_ge(ew_lo_gu, count(e, 1, 1))
                for f in range(FC):
                    n = FC * k + f
                    past(pe, h_f32, count(e, FC, f - 1))
                    split_mm(ps_h[n % 2][0][:, :], lambda a, i: ew_gu[:, k, a, i, f * P:(f + 1) * P],
                             lambda c, i: xgT[:, c, i, :], DC).then_inc(g_mm, 1)
                    split_mm(ps_h[n % 2][1][:, :], lambda a, i: ew_gu[:, k, a, i, F + f * P:F + (f + 1) * P],
                             lambda c, i: xgT[:, c, i, :], DC).then_inc(u_mm, 1)

            def down(e, k):
                pe.wait_ge(ew_lo_dn, count(e, 1, 1))
                for c in range(CC):
                    past(pe, y_done, count(e, CC, c - 1))
                    for f in range(FC):
                        if c == 0:
                            pe.wait_ge(h_lo, count(e, FC, f + 1))
                        for n, (a, w) in enumerate(PARTS):
                            mm = pe.matmul(ps_y[c % 2][:, :], hT[:, a, f, c * P:(c + 1) * P], ew_dn[:, k, w, f, :],
                                           start=(f == 0 and n == 0), stop=(f == FC - 1 and n == 2))
                    mm.then_inc(y_mm, 1)

            def expert(e, k, ahead, landed):
                up_gate(e, k)
                if ahead:
                    pe.wait_ge(ld_xg[1 - k], landed)
                    turn_xg_chunks(e + 1, 1 - k)
                down(e, k)

            def turn_xg_chunks(e, k):
                for c in range(CC):
                    past(pe, xg_lo, count(e, CC, c - 1))
                    for d in range(DC):
                        mm = pe.transpose(ps_xg[c % 2][:, d * P:(d + 1) * P], xg[:, k, c, d * P:(d + 1) * P], ident[:, :])
                    mm.then_inc(xg_mm, 1)

            pe.wait_ge(ld_xg[0], 64)
            turn_xg_chunks(0, 0)
            expert(0, 0, True, 64)
            expert(1, 1, True, 128)
            with pe.Fori(1, NX // 2 - 1) as m:
                expert(m * 2, 0, True, count(m, 64, 64))
                expert(m * 2 + 1, 1, True, count(m, 64, 128))
            expert(NX - 2, 0, True, NX // 2 * 64)
            expert(NX - 1, 1, False, 0)

        @block.scalar
        def _(act):
            def high(n, dst, src, loads):
                act.wait_ge(ld_w[n % 2], loads)
                nc.scalar.activation(dst, src, ACT.Copy, scale=W_SCALE).then_inc(w_split_hi, 1)

            def split_x(b):
                act.wait_ge(ld_x, count(b, 16, 16))
                past(act, qk_mm, count(b, EC))
                past(act, v_mm, count(b, 4))
                nc.scalar.activation(xt[:, 0, :, :], xt32[:, :, :], ACT.Copy).then_inc(xt_hi, 1)

            flat = lambda ap: ap.rearrange("p c n -> p (c n)")
            for w in range(2):
                high(w, flat(wqkv[:, w, 0]), stage[:, w, 0:4096], 16)
            split_x(0)
            high(2, flat(wqkv[:, 2, 0]), stage[:, 0, 0:4096], 32)

            def qk_out(b, j):
                past(act, s_mm, count(b, EC, j - 1))
                act.wait_ge(qk_mm, count(b, EC, j + 1))
                for w in range(2):
                    at = slice(w * S, (w + 1) * S)
                    nc.scalar.activation(qk32[:, j % 2, at], ps_qk[:, at], ACT.Identity,
                                         bias=bqkv[:, w, j:j + 1], scale=1.0 / W_SCALE)
                    ins = nc.scalar.activation(qk[:, j % 2, 0, at], ps_qk[:, at], ACT.Identity,
                                               bias=bqkv[:, w, j:j + 1], scale=1.0 / W_SCALE)
                ins.then_inc(qk_hi, 1)

            def heads_out(b, j):
                past(act, o_lo, count(b, EC, j - 1))
                if j == 0:
                    past(act, wo_mm, count(b, TT))
                act.wait_ge(pv_mm, count(b, EC, j + 1))
                for dst in (o32[:, j % 2, :], o[:, 0, j, :]):
                    ins = nc.scalar.activation(dst, ps_o[:, 0:S], ACT.Identity, bias=bqkv[:, 2, j:j + 1],
                                               scale=1.0 / P_SCALE)
                ins.then_inc(o_hi, 1)

            def exps(b, j):
                past(act, t_mm, count(b, 2 * EC, 2 * j - 2))
                act.wait_ge(s_negd, count(b, EC, j + 1))
                for h in range(2):
                    for t in range(TT):
                        n = 2 * h + t
                        ins = nc.scalar.activation(probs[:, j % 2, h, t, :], ps_s[h][:, t * S:(t + 1) * S], ACT.Exp,
                                                   bias=s_neg[:, j % 2, n:n + 1], scale=SCORE,
                                                   accum_out=s_den[:, j % 2, n:n + 1])
                ins.then_inc(e_done, 1)

            def values_hi(b, g):
                half, t = g // 2, g % 2
                if t == 0:
                    past(act, pv_mm, count(b, EC, half * EC // 2 - EC // 2))
                act.wait_ge(v_mm, count(b, 4, g + 1))
                nc.scalar.activation(v[:, 0, t, half * 512:(half + 1) * 512], ps_v[:, :], ACT.Copy,
                                     scale=1.0 / W_SCALE).then_inc(v_hi, 1)

            def turned_hi(b, j):
                past(act, pv_mm, count(b, EC, j - 1))
                for h in range(2):
                    act.wait_ge(t_mm, count(b, 2 * EC, 2 * j + h + 1))
                    nc.scalar.activation(pT[:, j % 2, 0, h, :], ps_t[h][:, :], ACT.Copy,
                                         scale=P_SCALE).then_inc(pt_hi, 1)

            def x1_hi(b, t):
                act.wait_ge(x1t_mm, count(b, TT, t + 1))
                past(act, q2_mm, count(b, 1))
                nc.scalar.activation(x1T[:, 0, :, t * P:(t + 1) * P],
                                     (ps_v, ps_x)[t][:, :].rearrange("p (c n) -> p c n", c=DC), ACT.Copy).then_inc(x1t_hi, 1)

            def split_ctx(b):
                act.wait_ge(ld_ctx, count(b, 16, 16))
                past(act, kv_mm, count(b, 1))
                nc.scalar.activation(ct[:, 0, :, :], ct32[:, :, :], ACT.Copy).then_inc(ct_hi, 1)

            def kv2_hi(b):
                act.wait_ge(kv_mm, count(b, 1, 1))
                past(act, pv2_mm, count(b, 1))
                nc.scalar.activation(k2[:, 0, :], ps_v[0:XD, 0:S], ACT.Copy, scale=1.0 / W_SCALE).then_inc(kv_hi, 1)
                nc.scalar.activation(v2[:, 0].rearrange("p t n -> p (t n)"), ps_v[:, S:S + TT * XD], ACT.Copy,
                                     scale=1.0 / W_SCALE).then_inc(kv_hi, 1)

            def q2_high(b):
                act.wait_ge(q2_mm, count(b, 1, 1))
                past(act, s2_mm, count(b, 1))
                nc.scalar.activation(q2[:, 0, :], ps_x[0:XD, 0:S], ACT.Copy, scale=1.0 / W_SCALE).then_inc(q2_hi, 1)

            def exp2(b):
                act.wait_ge(s2_dve, count(b, 3, 3))
                for t in range(TT):
                    ins = nc.scalar.activation(p2[:, t, :], p2[:, t, :], ACT.Exp, bias=n2[:, t:t + 1],
                                               accum_out=den2[:, t:t + 1])
                ins.then_inc(e2_done, 1)

            def turned2_hi(b):
                act.wait_ge(t2_mm, count(b, 1, 1))
                past(act, pv2_mm, count(b, 1))
                nc.scalar.activation(p2T[:, 0].rearrange("p c n -> p (c n)"), ps_x[:, :], ACT.Copy,
                                     scale=P_SCALE).then_inc(t2_hi, 1)

            def o2_high(b):
                act.wait_ge(pv2_mm, count(b, 1, 1))
                past(act, out2_mm, count(b, TT))
                nc.scalar.activation(o2[:, 0, :], ps_x[0:XD, 0:S], ACT.Copy, scale=1.0 / P_SCALE).then_inc(o2_hi, 1)

            W0 = 32 + 48
            W1 = 48

            def weights_hi(e, k, loads):
                act.wait_ge(ld_w[k], loads)
                past(act, y_mm, count(e, CC, -CC))
                nc.scalar.activation(ew[:, k, 0, :], stage[:, k, :], ACT.Copy, scale=W_SCALE).then_inc(ew_hi, 1)

            def x2_turned(b, t):
                act.wait_ge(x2t_mm, count(b, TT, t + 1))
                past(act, gate_mm, count(b, 1))
                nc.scalar.activation(x2T[:, :, t * P:(t + 1) * P],
                                     ps_x[:, :].rearrange("p (c n) -> p c n", c=DC), ACT.Copy).then_inc(x2t_done, 1)

            def gate_exp(b):
                act.wait_ge(rt, count(b, RT, 3))
                for t in range(TT):
                    ins = nc.scalar.activation(ex[:, t, :], ps_gate[:, t, :], ACT.Exp, bias=neg_l[:, t:t + 1],
                                               accum_out=den_l[:, t:t + 1])
                ins.then_inc(rt_exp, 1)

            def work(r, head, tail, route, fill):
                b, t, u = r, r - 1, r - 2
                pair = pairs(r, head, tail)

                def step(s, between=(), first=()):
                    pair(turned_hi, s - 3)
                    for on, run in first:
                        if on:
                            run()
                    pair(exps, s - 2)
                    for on, run in between:
                        if on:
                            run()
                    if s != 4:
                        pair(heads_out, s - 4)
                    if head:
                        qk_out(b, s)

                if head and not (isinstance(r, int) and r == 0):
                    split_x(b)
                if isinstance(r, int) and r == 0:
                    act.wait_ge(ld_small, 96)
                step(0, first=[(route, lambda: exp2(u))])
                if head:
                    values_hi(b, 0)
                step(1, [(route, lambda: turned2_hi(u))])
                if route:
                    o2_high(u)
                if head:
                    values_hi(b, 1)
                step(2)
                step(3)
                if route:
                    x2_turned(u, 0)
                if head:
                    values_hi(b, 2)
                if isinstance(r, int) and r == 0:
                    high(3, flat(wo[:, 0]), stage[:, 1, 0:4096], 32)
                    high(4, wx[:, 0].rearrange("p k c n -> p (k c n)"), stage[:, 0, 0:3 * DC * XD], 32 + 48)
                    high(5, wxo[:, 0, :], stage[0:XD, 1, 0:D], 48)
                if route:
                    x2_turned(u, 1)
                step(4)
                if tail:
                    split_ctx(t)
                pair(heads_out, 0)
                step(5, [(route, lambda: gate_exp(u))])
                if head:
                    values_hi(b, 3)
                step(6, [(tail, lambda: x1_hi(t, 0))])
                if tail:
                    x1_hi(t, 1)
                step(7, [(tail, lambda: kv2_hi(t)), (tail, lambda: q2_high(t))])
                if isinstance(r, int) and r == B:
                    act.wait_ge(qk_mm, B * EC)
                    act.wait_ge(v_mm, B * 4)
                    weights_hi(0, 0, W0 + 32)

            rounds(act, work)

            def tokens_hi(e):
                past(act, u_mm, count(e, FC))
                for c in range(CC):
                    act.wait_ge(xg_mm, count(e, CC, c + 1))
                    nc.scalar.activation(xgT[:, 0, :, c * P:(c + 1) * P],
                                         ps_xg[c % 2][:, :].rearrange("p (d n) -> p d n", d=DC), ACT.Copy)\
                      .then_inc(xg_hi, 1)

            def expert(e, k, ahead, loads):
                for f in range(FC):
                    n = FC * k + f
                    act.wait_ge(g_mm, count(e, FC, f + 1))
                    past(act, h_f32, count(e, FC, f - 1))
                    nc.scalar.activation(silu[:, n % 2, :], ps_h[n % 2][0][:, :], ACT.Silu, scale=1.0 / W_SCALE)\
                      .then_inc(silu_done, 1)
                    if f == 0 and ahead:
                        weights_hi(e + 1, 1 - k, loads)
                if ahead:
                    tokens_hi(e + 1)
                for c in range(CC):
                    act.wait_ge(y_mm, count(e, CC, c + 1))
                    if c == 0:
                        act.wait_ge(cur_done, count(e, 3, 3))
                        past(act, st_y, count(e, 64, -64))
                    nc.scalar.activation(y[:, k, c, :], ps_y[c % 2][:, :], ACT.Copy,
                                         scale=cur_w[:, k, c:c + 1]).then_inc(y_done, 1)

            tokens_hi(0)
            expert(0, 0, True, W1 + 32)
            expert(1, 1, True, W0 + 64)
            with act.Fori(1, NX // 2 - 1) as m:
                expert(m * 2, 0, True, count(m, 32, W1 + 32))
                expert(m * 2 + 1, 1, True, count(m, 32, W0 + 64))
            expert(NX - 2, 0, True, W1 + NX // 2 * 32)
            expert(NX - 1, 1, False, 0)

        @block.vector
        def _(dve):
            vec = nc.vector

            def low(dst, src, hi, scale=1.0):
                return vec.scalar_tensor_tensor(out=dst, in0=src, scalar=scale, in1=hi, op0=ALU.mult, op1=ALU.subtract)

            dve.wait_ge(s_const, N_CONST)
            vec.tensor_copy(before[:, :], before_f32[:, :]).then_inc(s_constv, 1)
            vec.tensor_copy(iota[:, :], iota_i[:, :]).then_inc(s_constv, 1)
            vec.tensor_copy(row1[:, :], row_i[:, :]).then_inc(s_constv, 1)
            vec.tensor_copy(thr[:, :], thr_i[:, :]).then_inc(s_constv, 1)
            vec.tensor_copy(spare[:, :], spare_i[:, :]).then_inc(s_constv, 1)
            vec.memset(sel_sum[:, :, :], 0.0).then_inc(s_constv, 1)
            vec.memset(ge[:, :, 0:1], 1.0).then_inc(s_constv, 1)
            vec.memset(slots[:, :, :, :], 0.0).then_inc(s_constv, 1)

            def low_w(n, dst, src, hi):
                dve.wait_ge(w_split_hi, n + 1)
                low(dst, src, hi, W_SCALE).then_inc(w_split_lo, 1)

            def split_x(b):
                dve.wait_ge(xt_hi, count(b, 1, 1))
                low(xt[:, 1, :, :], xt32[:, :, :], xt[:, 0, :, :]).then_inc(xt_lo, 1)

            flat = lambda ap: ap.rearrange("p c n -> p (c n)")
            for w in range(2):
                low_w(w, flat(wqkv[:, w, 1]), stage[:, w, 0:4096], flat(wqkv[:, w, 0]))
            split_x(0)
            low_w(2, flat(wqkv[:, 2, 1]), stage[:, 0, 0:4096], flat(wqkv[:, 2, 0]))

            def maxima(b, j):
                dve.wait_ge(s_mm, count(b, EC, j + 1))
                past(dve, e_done, count(b, EC, j - 1))
                for h in range(2):
                    vec.tensor_reduce(s_max[:, j % 2, 2 * h:2 * h + 2], ps_s[h][:, :].rearrange("p (t k) -> p t k", t=TT),
                                      AX.X, ALU.max).then_inc(s_maxd, 1)
                dve.wait_ge(s_maxd, count(b, 2 * EC, 2 * j + 2))
                vec.tensor_scalar(s_neg[:, j % 2, :], s_max[:, j % 2, :], -SCORE, None, ALU.mult).then_inc(s_negd, 1)

            def row_scales(b, j):
                past(dve, p_done, count(b, EC, j - 1))
                dve.wait_ge(e_done, count(b, EC, j + 1))
                vec.reciprocal(s_rden[:, j % 2, :], s_den[:, j % 2, :]).then_inc(r_done, 1)

            def values_lo(b, g):
                half, t = g // 2, g % 2
                cs = slice(half * 512, (half + 1) * 512)
                dve.wait_ge(v_hi, count(b, 4, g + 1))
                low(v[:, 1, t, cs], ps_v[:, :], v[:, 0, t, cs], 1.0 / W_SCALE).then_inc(v_lo, 1)

            def turned_lo(b, j):
                for h in range(2):
                    dve.wait_ge(pt_hi, count(b, 2 * EC, 2 * j + h + 1))
                    low(pT[:, j % 2, 1, h, :], ps_t[h][:, :], pT[:, j % 2, 0, h, :], P_SCALE).then_inc(pt_lo, 1)

            def residual1(b, t):
                dve.wait_ge(wo_mm, count(b, TT, t + 1))
                if t == 0:
                    dve.wait_ge(xb_done, count(b, 1, 1))
                    past(dve, x1b_done, count(b, 1))
                    past(dve, ln2, count(b, 7))
                vec.scalar_tensor_tensor(out=z[:, t, :], in0=ps_x[:, :], scalar=1.0 / W_SCALE, in1=xr[:, t, :],
                                         op0=ALU.mult, op1=ALU.add).then_inc(ln1, 1)

            def moments(b, rows, stats, mv, ve, ln, before_it):
                for t in range(TT):
                    dve.wait_ge(ln, count(b, 7, t + 1))
                    vec.bn_stats(stats[:, t, :], rows[:, t, :]).then_inc(ln, 1)
                for t in range(TT):
                    wait_apart(dve, ln, count(b, 7, TT + t + 1), s_constv, N_CONSTV)
                    vec.bn_aggr(mv[:, t, :], stats[:, t, :]).then_inc(ln, 1)
                past(dve, before_it, count(b, 1))
                dve.wait_ge(ln, count(b, 7, 6))
                vec.tensor_scalar(ve[:, :], mv[:, :, 1], EPS, None, ALU.add).then_inc(ln, 1)

            def norm1(b):
                for t in range(TT):
                    if t == 0:
                        dve.wait_ge(ln1_rstd, count(b, 1, 1))
                        past(dve, x2_done, count(b, TT))
                    vec.tensor_scalar(x1[:, t, :], z[:, t, :], mv1[:, t, 0:1], rstd1[:, t:t + 1],
                                      ALU.subtract, ALU.mult).then_inc(x1_done, 1)

            def x1_lo(b, t):
                dve.wait_ge(x1t_hi, count(b, TT, t + 1))
                low(x1T[:, 1, :, t * P:(t + 1) * P], (ps_v, ps_x)[t][:, :].rearrange("p (c n) -> p c n", c=DC),
                    x1T[:, 0, :, t * P:(t + 1) * P]).then_inc(x1t_lo, 1)

            def split_ctx(b):
                dve.wait_ge(ct_hi, count(b, 1, 1))
                low(ct[:, 1, :, :], ct32[:, :, :], ct[:, 0, :, :]).then_inc(ct_lo, 1)

            def kv2_lo(b):
                dve.wait_ge(kv_hi, count(b, 2, 2))
                low(k2[:, 1, :], ps_v[0:XD, 0:S], k2[:, 0, :], 1.0 / W_SCALE).then_inc(kv_lo, 1)
                low(v2[:, 1].rearrange("p t n -> p (t n)"), ps_v[:, S:S + TT * XD],
                    v2[:, 0].rearrange("p t n -> p (t n)"), 1.0 / W_SCALE).then_inc(kv_lo, 1)

            def q2_low(b):
                dve.wait_ge(q2_hi, count(b, 1, 1))
                low(q2[:, 1, :], ps_x[0:XD, 0:S], q2[:, 0, :], 1.0 / W_SCALE).then_inc(q2_lo, 1)

            def masked(b):
                dve.wait_ge(s2_mm, count(b, 1, 1))
                dve.wait_ge(mask_done, count(b, 1, 1))
                past(dve, t2_mm, count(b, 1))
                vec.scalar_tensor_tensor(out=p2[:, :, :], in0=ps_x[:, :].rearrange("p (t k) -> p t k", t=TT), scalar=SCORE,
                                         in1=mask_add[:, :, :], op0=ALU.mult, op1=ALU.add).then_inc(s2_dve, 1)
                dve.wait_ge(s2_dve, count(b, 3, 1))
                vec.tensor_reduce(m2[:, :], p2[:, :, :], AX.X, ALU.max).then_inc(s2_dve, 1)
                dve.wait_ge(s2_dve, count(b, 3, 2))
                vec.tensor_scalar(n2[:, :], m2[:, :], -1.0, None, ALU.mult).then_inc(s2_dve, 1)

            def row_scales2(b):
                dve.wait_ge(e2_done, count(b, 1, 1))
                vec.reciprocal(rden2[:, :], den2[:, :]).then_inc(r2_done, 1)

            def turned2_lo(b):
                dve.wait_ge(t2_hi, count(b, 1, 1))
                low(p2T[:, 1].rearrange("p c n -> p (c n)"), ps_x[:, :], p2T[:, 0].rearrange("p c n -> p (c n)"),
                    P_SCALE).then_inc(t2_lo, 1)

            def o2_low(b):
                dve.wait_ge(o2_hi, count(b, 1, 1))
                low(o2[:, 1, :], ps_x[0:XD, 0:S], o2[:, 0, :], 1.0 / P_SCALE).then_inc(o2_lo, 1)

            def residual2(b, t):
                dve.wait_ge(out2_mm, count(b, TT, t + 1))
                if t == 0:
                    dve.wait_ge(x1b_done, count(b, 1, 1))
                vec.scalar_tensor_tensor(out=x1[:, t, :], in0=ps_x[:, :], scalar=1.0 / W_SCALE, in1=z[:, t, :],
                                         op0=ALU.mult, op1=ALU.add).then_inc(ln2, 1)

            def norm2(b):
                for t in range(TT):
                    if t == 0:
                        dve.wait_ge(ln2_rstd, count(b, 1, 1))
                        past(dve, x2t_mm, count(b, TT))
                        past(dve, st_x2, count(b, 32))
                    vec.tensor_scalar(x2[:, t, :], x1[:, t, :], mv2[:, t, 0:1], rstd2[:, t:t + 1],
                                      ALU.subtract, ALU.mult).then_inc(x2_done, 1)

            def step(b, n):
                past(dve, rt, count(b, RT, n))

            def gate_max(b):
                wait_apart(dve, gate_mm, count(b, 1, 1), s_constv, N_CONSTV)
                for t in range(TT):
                    vec.max(top_l[:, t, :], ps_gate[:, t, :]).then_inc(rt, 1)
                step(b, 2)
                vec.tensor_scalar(neg_l[:, :], top_l[:, :, 0], -1.0, None, ALU.mult).then_inc(rt, 1)

            def choose(b):
                by_row = lambda ap: ap.unsqueeze(2).to_broadcast([P, TT, NX])
                dve.wait_ge(rt_exp, count(b, 1, 1))
                vec.reciprocal(rden_l[:, :], den_l[:, :]).then_inc(rt, 1)
                step(b, 4)
                vec.tensor_tensor(pr[:, :, :], ex[:, :, :], by_row(rden_l[:, :]), ALU.mult).then_inc(rt, 1)
                wait_apart(dve, rt, count(b, RT, 5), s_constv, N_CONSTV)
                for t in range(TT):
                    vec.max(top_p[:, t, :], pr[:, t, :]).then_inc(rt, 1)
                wait_apart(dve, rt, count(b, RT, 7), s_constv, N_CONSTV)
                for t in range(TT):
                    vec.match_replace(left[:, t, :], top_p[:, t, :], pr[:, t, :], -1.0).then_inc(rt, 1)
                step(b, 9)
                vec.tensor_scalar(sel[:, :, :], left[:, :, :], -1.0, None, ALU.is_equal).then_inc(rt, 1)
                step(b, 10)
                vec.tensor_tensor(sel_sum[:, 1, :], sel_sum[:, 0, :], sel[:, 0, :], ALU.add).then_inc(rt, 1)
                vec.tensor_reduce(w_sum[:, :], top_p[:, :, :], AX.X, ALU.add).then_inc(rt, 1)
                step(b, 12)
                vec.reciprocal(w_rsum[:, :], w_sum[:, :]).then_inc(rt, 1)
                step(b, 13)
                vec.scalar_tensor_tensor(out=w32[:, :, :], in0=pr[:, :, :], scalar=G_SCALE, in1=by_row(w_rsum[:, :]),
                                         op0=ALU.mult, op1=ALU.mult).then_inc(rt, 1)
                step(b, 14)
                vec.tensor_copy(w_hi[:, :, :], w32[:, :, :]).then_inc(rt, 1)
                step(b, 15)
                vec.tensor_tensor(w_lo[:, :, :], w32[:, :, :], w_hi[:, :, :], ALU.subtract).then_inc(rt, 1)

            G = TT * NX

            def places(b):
                dve.wait_ge(pos_mm, count(b, 1, 1))
                vec.tensor_tensor(sel_sum[:, 0, :], sel_sum[:, 1, :], sel[:, 1, :], ALU.add).then_inc(rt, 1)
                vec.tensor_tensor(ge[:, :, 1:CC + 1], ps_pos[:, :].unsqueeze(2).to_broadcast([P, G, CC]),
                                  thr[:, :].unsqueeze(1).to_broadcast([P, G, CC]), ALU.is_ge).then_inc(rt, 1)
                step(b, 18)
                vec.tensor_reduce(n_ge[:, :], ge[:, :, 1:CC], AX.X, ALU.add).then_inc(rt, 1)
                step(b, 19)
                vec.scalar_tensor_tensor(out=pos_in[:, :], in0=n_ge[:, :], scalar=-float(P), in1=ps_pos[:, :],
                                         op0=ALU.mult, op1=ALU.add).then_inc(rt, 1)
                vec.tensor_tensor(in_chunk[:, :, :], ge[:, :, 0:CC], ge[:, :, 1:CC + 1], ALU.subtract).then_inc(rt, 1)

            def tell(b):
                by_choice = lambda ap: ap.rearrange("p t e -> p (t e)").unsqueeze(2).to_broadcast([P, G, CC])
                step(b, 21)
                vec.tensor_tensor(chosen[:, :, :], in_chunk[:, :, :], by_choice(sel[:, :, :]), ALU.mult).then_inc(rt, 1)
                step(b, 22)
                past(dve, slot_mm, count(b, 2))
                vec.tensor_scalar(said[:, :, 0, :], chosen[:, :, :], row1[:, 0:1], None, ALU.mult).then_inc(rt, 1)
                vec.tensor_tensor(said[:, :, 1, :].rearrange("p (t e) c -> p t e c", t=TT),
                                  chosen[:, :, :].rearrange("p (t e) c -> p t e c", t=TT),
                                  tile_no[:, :].unsqueeze(2).unsqueeze(3).to_broadcast([P, TT, NX, CC]), ALU.mult).then_inc(rt, 1)
                vec.tensor_tensor(said[:, :, 2, :], chosen[:, :, :], by_choice(w_hi[:, :, :]), ALU.mult).then_inc(rt, 1)
                vec.tensor_tensor(said[:, :, 3, :], chosen[:, :, :], by_choice(w_lo[:, :, :]), ALU.mult).then_inc(rt, 1)
                step(b, 24)
                vec.tensor_scalar(tile_no[:, :], tile_no[:, :], float(TT), None, ALU.add).then_inc(rt, 1)

            def slot_onehot(b, k, t):
                step(b, 20)
                past(dve, slot_mm, count(b, 2, k))
                vec.tensor_tensor(onehot[:, t, :, :], iota[:, :].unsqueeze(1).to_broadcast([P, HX, P]),
                                  pos_in[:, t * NX + k * HX:t * NX + (k + 1) * HX].unsqueeze(2).to_broadcast([P, HX, P]),
                                  ALU.is_equal).then_inc(oh_done, 1)

            def add_slots(b, k):
                dve.wait_ge(slot_mm, count(b, 2, k + 1))
                past(dve, slot_done, count(b, 2, k - 1))
                half = slots[:, k * HX:(k + 1) * HX, :, :].rearrange("p e a c -> p (e a c)")
                vec.tensor_tensor(half, half, ps_slot[:, :], ALU.add).then_inc(slot_done, 1)

            def weights_lo(e, k):
                dve.wait_ge(ew_hi, count(e, 1, 1))
                past(dve, y_mm, count(e, CC, -CC))
                low(ew[:, k, 1, 0:WGU], stage[:, k, 0:WGU], ew[:, k, 0, 0:WGU], W_SCALE).then_inc(ew_lo_gu, 1)
                low(ew[:, k, 1, WGU:NW], stage[:, k, WGU:NW], ew[:, k, 0, WGU:NW], W_SCALE).then_inc(ew_lo_dn, 1)

            def work(r, head, tail, route, fill):
                b, t, u, f = r, r - 1, r - 2, r - 3
                pair = pairs(r, head, tail)

                def step(s, between=()):
                    pair(maxima, s - 2)
                    pair(turned_lo, s - 3)
                    for on, run in between:
                        if on:
                            run()
                    pair(row_scales, s - 2)

                if route:
                    masked(u)
                if head and not (isinstance(r, int) and r == 0):
                    split_x(b)
                step(0, [(fill, lambda: add_slots(f, 0)), (fill, lambda: slot_onehot(f, 1, 0))])
                if route:
                    row_scales2(u)
                if head:
                    values_lo(b, 0)
                step(1, [(fill, lambda: slot_onehot(f, 1, 1))])
                if route:
                    turned2_lo(u)
                    o2_low(u)
                if head:
                    values_lo(b, 1)
                step(2)
                if route:
                    residual2(u, 0)
                if fill:
                    add_slots(f, 1)
                if route:
                    residual2(u, 1)
                    moments(u, x1, stats2, mv2, ve2, ln2, ln2_rstd)
                step(3, [(route, lambda: norm2(u))])
                if head:
                    values_lo(b, 2)
                if isinstance(r, int) and r == 0:
                    low_w(3, flat(wo[:, 1]), stage[:, 1, 0:4096], flat(wo[:, 0]))
                    low_w(4, wx[:, 1].rearrange("p k c n -> p (k c n)"), stage[:, 0, 0:3 * DC * XD],
                          wx[:, 0].rearrange("p k c n -> p (k c n)"))
                    low_w(5, wxo[:, 1, :], stage[0:XD, 1, 0:D], wxo[:, 0, :])
                step(4)
                if tail:
                    residual1(t, 0)
                    split_ctx(t)
                    residual1(t, 1)
                    moments(t, z, stats1, mv1, ve1, ln1, ln1_rstd)
                step(5, [(route, lambda: gate_max(u))])
                if tail:
                    norm1(t)
                if route:
                    choose(u)
                if head:
                    values_lo(b, 3)
                step(6, [(route, lambda: places(u))])
                if tail:
                    x1_lo(t, 0)
                if route:
                    tell(u)
                if tail:
                    x1_lo(t, 1)
                step(7, [(route, lambda: slot_onehot(u, 0, 0))])
                if tail:
                    kv2_lo(t)
                    q2_low(t)
                if route:
                    slot_onehot(u, 0, 1)
                if isinstance(r, int) and r == B:
                    weights_lo(0, 0)

            dve.wait_ge(s_constv, N_CONSTV)
            dve.wait_ge(ld_small, 96)
            dve.wait_ge(st_zero, 16)
            rounds(dve, work)

            dve.wait_ge(slot_done, B * 2)
            vec.scalar_tensor_tensor(out=tok[:, :, :], in0=slots[:, :, 1, :], scalar=float(P), in1=slots[:, :, 0, :],
                                     op0=ALU.mult, op1=ALU.add).then_inc(table, 1)
            vec.tensor_scalar(empty[:, :, :], slots[:, :, 0, :], 0.0, None, ALU.is_equal).then_inc(table, 1)
            dve.wait_ge(table, 2)
            vec.tensor_scalar(tok0[:, :, :], tok[:, :, :], -1.0, 0.0, ALU.add, ALU.max).then_inc(table, 1)
            dve.wait_ge(table, 3)
            vec.tensor_tensor(tok[:, :, :], empty[:, :, :], spare[:, :].unsqueeze(1).to_broadcast([P, NX, CC]), ALU.mult)\
               .then_inc(table, 1)
            dve.wait_ge(table, 4)
            vec.tensor_copy(idx_from[:, :, :], tok0[:, :, :]).then_inc(table, 1)
            vec.tensor_tensor(idx_to[:, :, :], tok0[:, :, :], tok[:, :, :], ALU.add).then_inc(table, 1)
            vec.tensor_tensor(w_slot[:, :, :], slots[:, :, 2, :], slots[:, :, 3, :], ALU.add).then_inc(table, 1)
            dve.wait_ge(table, 7)
            vec.tensor_scalar(w_slot[:, :, :], w_slot[:, :, :], 1.0 / (G_SCALE * W_SCALE), None, ALU.mult).then_inc(table, 1)

            def tokens_lo(e):
                for c in range(CC):
                    dve.wait_ge(xg_hi, count(e, CC, c + 1))
                    low(xgT[:, 1, :, c * P:(c + 1) * P], ps_xg[c % 2][:, :].rearrange("p (d n) -> p d n", d=DC),
                        xgT[:, 0, :, c * P:(c + 1) * P]).then_inc(xg_lo, 1)

            def expert(e, k, ahead):
                for f in range(FC):
                    n = FC * k + f
                    dve.wait_ge(u_mm, count(e, FC, f + 1))
                    dve.wait_ge(silu_done, count(e, FC, f + 1))
                    past(dve, h_lo, count(e, FC, f - 1))
                    vec.scalar_tensor_tensor(out=h32[:, n % 2, :], in0=ps_h[n % 2][1][:, :], scalar=1.0 / W_SCALE,
                                             in1=silu[:, n % 2, :], op0=ALU.mult, op1=ALU.mult).then_inc(h_f32, 1)
                    if f == 0:
                        past(dve, y_mm, count(e, CC))
                    dve.wait_ge(h_f32, count(e, FC, f + 1))
                    vec.tensor_copy(hT[:, 0, f, :], h32[:, n % 2, :]).then_inc(h_hi, 1)
                    dve.wait_ge(h_hi, count(e, FC, f + 1))
                    vec.tensor_tensor(hT[:, 1, f, :], h32[:, n % 2, :], hT[:, 0, f, :], ALU.subtract).then_inc(h_lo, 1)
                    if f == 1 and ahead:
                        weights_lo(e + 1, 1 - k)
                if ahead:
                    tokens_lo(e + 1)

            tokens_lo(0)
            expert(0, 0, True)
            expert(1, 1, True)
            with dve.Fori(2, NX - 3, 2) as e:
                expert(e, 0, True)
                expert(e + 1, 1, True)
            expert(NX - 2, 0, True)
            expert(NX - 1, 1, False)

            def final(g, k, loads):
                LN = 9
                dve.wait_ge(ld_acc[k], loads)
                for t in range(4):
                    vec.bn_stats(stats3[:, k, t, :], y[:, k, t, :]).then_inc(ln3, 1)
                for t in range(4):
                    wait_apart(dve, ln3, count(g, LN, t + 1), s_constv, N_CONSTV)
                    vec.bn_aggr(mv3[:, k, t, :], stats3[:, k, t, :]).then_inc(ln3, 1)
                dve.wait_ge(ln3, count(g, LN, 8))
                vec.tensor_scalar(ve3[:, k, :], mv3[:, k, :, 1], EPS, None, ALU.add).then_inc(ln3, 1)

            def final_norm(g, k, stores):
                dve.wait_ge(ln3_rstd, count(g, 1, 1))
                past(dve, st_out[k], stores)
                for t in range(4):
                    vec.tensor_scalar(xg[:, k, t, :], y[:, k, t, :], mv3[:, k, t, 0:1], rstd3[:, k, t:t + 1],
                                      ALU.subtract, ALU.mult).then_inc(out_done, 1)

            def final_pair(m, g, loads, stores):
                final(g, 0, loads)
                final(g + 1, 1, loads)
                final_norm(g, 0, stores)
                final_norm(g + 1, 1, stores)

            final_pair(0, 0, 16, 0)
            with dve.Fori(1, N // (8 * P)) as m:
                final_pair(m, m * 2, count(m, 16, 16), count(m, 16))

        @block.gpsimd
        def _(pool):
            gp = nc.gpsimd
            gp.memset(ident[:, :], 0.0).then_inc(s_const, 1)
            gp.memset(before_f32[:, :], 1.0).then_inc(s_const, 1)
            gp.memset(ones[:, :], 1.0).then_inc(s_const, 1)
            gp.memset(neg_half[:, :], -0.5).then_inc(s_const, 1)
            gp.iota(iota_i[:, :], [[1, P]], base=0, channel_multiplier=0).then_inc(s_const, 1)
            gp.iota(row_i[:, :], [[0, 1]], base=1, channel_multiplier=1).then_inc(s_const, 1)
            gp.iota(thr_i[:, :], [[P, CC]], base=P, channel_multiplier=0).then_inc(s_const, 1)
            gp.iota(spare_i[:, :], [[P, CC]], base=N, channel_multiplier=1).then_inc(s_const, 1)
            gp.memset(tile_no[:, 0:1], 0.0).then_inc(s_const, 1)
            gp.memset(tile_no[:, 1:2], 1.0).then_inc(s_const, 1)
            pool.wait_ge(s_const, 10)
            gp.affine_select(out=ident[:, :], in_=ident[:, :], compare_op=ALU.not_equal, fill=1.0, base=0,
                             pattern=[[-1, P]], channel_multiplier=1).then_inc(s_const, 1)
            gp.affine_select(out=before_f32[:, :], in_=before_f32[:, :], compare_op=ALU.is_ge, fill=0.0, base=-1,
                             pattern=[[1, P]], channel_multiplier=-1).then_inc(s_const, 1)
            pool.wait_ge(s_constv, N_CONSTV)
            pool.dma_start(acc_rows[N:N + CAP, :].rearrange("(c p) n -> p c n", p=P),
                           slots[:, :, :, :].rearrange("p e a c -> p (e a c)").unsqueeze(1).to_broadcast([P, CC, D])).then_inc(st_zero, 16)
            pool.wait_ge(ld_small, 96)

            def qk_low(b, j):
                past(pool, s_mm, count(b, EC, j - 1))
                pool.wait_ge(qk_hi, count(b, EC, j + 1))
                gp.tensor_tensor(qk[:, j % 2, 1, :], qk32[:, j % 2, :], qk[:, j % 2, 0, :], ALU.subtract).then_inc(qk_lo, 1)

            def normalise(b, j):
                pool.wait_ge(r_done, count(b, EC, j + 1))
                rows = probs[:, j % 2].rearrange("p h t k -> p (h t) k")
                gp.tensor_tensor(rows, rows, s_rden[:, j % 2, :].unsqueeze(2).to_broadcast([P, 4, S]), ALU.mult)\
                  .then_inc(p_done, 1)

            def heads_lo(b, j):
                pool.wait_ge(o_hi, count(b, EC, j + 1))
                gp.tensor_tensor(o[:, 1, j, :], o32[:, j % 2, :], o[:, 0, j, :], ALU.subtract).then_inc(o_lo, 1)

            def add_bias(b):
                pool.wait_ge(ld_row, count(b, 16, 16))
                gp.tensor_tensor(xr[:, :, :], xr[:, :, :], bo_row[:, :].unsqueeze(1).to_broadcast([P, TT, D]), ALU.add)\
                  .then_inc(xb_done, 1)

            def mask_rows(b):
                wait_apart(pool, ld_mask, count(b, 16, 16), s_const, N_CONST)
                gp.tensor_scalar(mask_add[:, :, :], mask_i[:, :, :], -1.0e9, None, ALU.mult).then_inc(mask_done, 1)

            def rstd(b, ln, dst, ve, done, read):
                pool.wait_ge(ln, count(b, 7, 7))
                past(pool, read, count(b, TT))
                gp.tensor_tensor(dst[:, :], ve[:, :], neg_half[:, 0:TT], ALU.pow).then_inc(done, 1)

            def add_bias2(b):
                pool.wait_ge(x1_done, count(b, TT, TT))
                gp.tensor_tensor(z[:, :, :], x1[:, :, :], xbo_row[:, :].unsqueeze(1).to_broadcast([P, TT, D]), ALU.add)\
                  .then_inc(x1b_done, 1)

            def normalise2(b):
                pool.wait_ge(r2_done, count(b, 1, 1))
                gp.tensor_tensor(p2[:, :, :], p2[:, :, :], rden2[:, :].unsqueeze(2).to_broadcast([P, TT, S]), ALU.mult)\
                  .then_inc(p2_done, 1)

            def work(r, head, tail, route, fill):
                b, t, u = r, r - 1, r - 2
                pair = pairs(r, head, tail)

                def step(s):
                    pair(normalise, s - 2)
                    if s != 4:
                        pair(heads_lo, s - 4)
                    if head:
                        qk_low(b, s)

                step(0)
                if route:
                    normalise2(u)
                step(1)
                if tail:
                    add_bias(t)
                step(2)
                if route:
                    rstd(u, ln2, rstd2, ve2, ln2_rstd, x2_done)
                step(3)
                step(4)
                pair(heads_lo, 0)
                if tail:
                    rstd(t, ln1, rstd1, ve1, ln1_rstd, x1_done)
                step(5)
                if tail:
                    add_bias2(t)
                step(6)
                if tail:
                    mask_rows(t)
                step(7)

            rounds(pool, work)

            def columns(e, k):
                at = bass.ds(e, 1)
                for dst, src in ((cur_from, idx_from), (cur_to, idx_to), (cur_w, w_slot)):
                    ins = gp.tensor_copy(dst[:, k, :], src[:, at, :].rearrange("p a c -> p (a c)"))
                    ins.then_inc(cur_done, 1)

            def gather(e, k):
                wait_apart(pool, cur_done, count(e, 3, 3), s_const, N_CONST)
                for c in range(CC):
                    gp.indirect_dma_start(xg[:, k, c, :], None, x2_rows,
                                          bass.IndirectOffsetOnAxis(ap=cur_from[:, k, c:c + 1], axis=0)).then_inc(ld_xg[k], 16)

            def scatter(e, k):
                for c in range(CC):
                    wait_apart(pool, y_done, count(e, CC, c + 1), s_const, N_CONST)
                    gp.indirect_dma_start(acc_rows, bass.IndirectOffsetOnAxis(ap=cur_to[:, k, c:c + 1], axis=0),
                                          y[:, k, c, :], None, compute_op=ALU.add).then_inc(st_y, 16)

            def expert(e, k, ahead):
                past(pool, st_y, count(e, 64))
                if ahead:
                    past(pool, y_done, count(e, CC))
                    past(pool, xg_mm, count(e, CC))
                    columns(e + 1, 1 - k)
                    gather(e + 1, 1 - k)
                scatter(e, k)

            pool.wait_ge(table, 8)
            columns(0, 0)
            pool.wait_ge(st_x2, B * 32)
            pool.wait_ge(st_zero, 16)
            pool.wait_ge(pt_lo, B * 2 * EC)
            pool.wait_ge(pv_mm, B * EC)
            gather(0, 0)
            expert(0, 0, True)
            expert(1, 1, True)
            with pool.Fori(2, NX - 3, 2) as e:
                expert(e, 0, True)
                expert(e + 1, 1, True)
            expert(NX - 2, 0, True)
            expert(NX - 1, 1, False)

            def rstd_final(g, k):
                pool.wait_ge(ln3, count(g, 9, 9))
                gp.tensor_tensor(rstd3[:, k, :], ve3[:, k, :], neg_half[:, :], ALU.pow).then_inc(ln3_rstd, 1)

            with pool.Fori(0, N // (4 * P) - 1, 2) as g:
                rstd_final(g, 0)
                rstd_final(g + 1, 1)


INS = ["xT", "x_rows", "ctxT", "mask", "wqT", "wkT", "wvT", "woT", "bq", "bk", "bv", "bo",
       "x_wv", "x_wk", "x_wq", "x_wo", "x_bo", "gateT", "wguT", "wdnT"]


def kernel(x, ctx_1024, mask_BxSxS2_ik1, L0_attn_Wq, L0_attn_bq, L0_attn_Wk, L0_attn_bk, L0_attn_Wv, L0_attn_bv,
           L0_attn_Wo, L0_attn_bo, L0_xattn_Wv, L0_xattn_Wk, L0_xattn_Wq, L0_xattn_Wo, L0_xattn_bo,
           L0_ffn_gate_weight, L0_ffn_gate_up_proj, L0_ffn_down_proj):
    import numpy as np
    import concourse.bacc as bacc
    from concourse.bass_utils import run_bass_kernel_spmd

    a = np.asarray
    rows = lambda m: a(m).reshape(N, -1)
    cols = lambda m: a(m).reshape(EC, P).T
    given = {
        "xT": rows(x).T, "x_rows": rows(x), "ctxT": rows(ctx_1024).T, "mask": rows(mask_BxSxS2_ik1),
        "wqT": a(L0_attn_Wq).T, "wkT": a(L0_attn_Wk).T, "wvT": a(L0_attn_Wv).T, "woT": a(L0_attn_Wo).T,
        "bq": cols(L0_attn_bq), "bk": cols(L0_attn_bk), "bv": cols(L0_attn_bv), "bo": a(L0_attn_bo),
        "x_wv": a(L0_xattn_Wv), "x_wk": a(L0_xattn_Wk), "x_wq": a(L0_xattn_Wq), "x_wo": a(L0_xattn_Wo),
        "x_bo": a(L0_xattn_bo), "gateT": a(L0_ffn_gate_weight).T,
        "wguT": a(L0_ffn_gate_up_proj).transpose(0, 2, 1), "wdnT": a(L0_ffn_down_proj).transpose(0, 2, 1),
    }
    given = {k: np.ascontiguousarray(m) for k, m in given.items()}
    nc = bacc.Bacc("TRN2", target_bir_lowering=False, num_devices=1)
    args = [nc.dram_tensor(k, given[k].shape, mybir.dt.from_np(given[k].dtype), kind="ExternalInput").ap() for k in INS]
    out = nc.dram_tensor("out", [N, D], F32, kind="ExternalOutput").ap()
    build(nc, *args, out)
    r = run_bass_kernel_spmd(nc, [given], core_ids=[0])
    return r.results[0]["out"].reshape(B, S, D)
```

```python
import concourse.bass as bass
from concourse import mybir
from contextlib import ExitStack


F32 = mybir.dt.float32
F16 = mybir.dt.float16
I32 = mybir.dt.int32
ALU = mybir.AluOpType
ACT = mybir.ActivationFunctionType
AX = mybir.AxisListType

P = 128
B, S, D = 16, 256, 512
N = B * S
H, DK = 16, 64
E = H * DK
DC = D // P
EC = E // P
TT = S // P
NX, TOP, CAP, F = 32, 8, 512, 384
FC = F // P
CC = CAP // P
XD = 64
WGU = DC * 2 * F
WDN = FC * D
EPS = 1e-5
SCORE = 1.0 / 8.0
W_SCALE = 256.0
P_SCALE = 4096.0
G_SCALE = 256.0
PARTS = ((0, 0), (0, 1), (1, 0))


def count(b, per, c=0):
    return b * per + c


def past(eng, sem, value):
    if isinstance(value, int) and value <= 0:
        return
    eng.wait_ge(sem, value)


def wait_apart(eng, sem, value, held, times):
    if not isinstance(value, int):
        value = eng.snap(eng.to_reg(value))
    eng.wait_ge(held, times)
    past(eng, sem, value)


def build(nc, xT, x_rows, ctxT, mask, wqT, wkT, wvT, woT, bq, bk, bv, bo,
          x_wv, x_wk, x_wq, x_wo, x_bo, gateT, wguT, wdnT, out):
    ctx = ExitStack()
    with ctx:
        def sb(name, shape, dt=F32):
            return ctx.enter_context(nc.sbuf_tensor(name, shape, dt))

        def sem(name):
            return ctx.enter_context(nc.semaphore(name))

        x2_rows = nc.dram_tensor("x2_rows", [N, D], F32, kind="Internal").ap()
        acc_rows = nc.dram_tensor("acc_rows", [N + CAP, D], F32, kind="Internal").ap()

        arena_wo = sb("arena_wo", [P, 3 * 2 * DC * E + 2 * EC * D], F16)
        arena_w = arena_wo[:, 0:3 * 2 * DC * E]
        arena_o = arena_wo[:, 3 * 2 * DC * E:]
        wqkv = arena_w[:, :].rearrange("p (w s c n) -> p w s c n", w=3, s=2, c=DC)
        wo = arena_o[:, :].rearrange("p (s c n) -> p s c n", s=2, c=EC)
        wx = sb("wx", [P, 2, 3, DC, XD], F16)
        wxo = sb("wxo", [XD, 2, D], F16)
        gate_w = sb("gate_w", [P, DC, NX])
        stage = sb("stage", [P, 2, WGU + WDN])
        bqkv = sb("bqkv", [P, 3, EC])
        bo_row = sb("bo_row", [P, D])
        xbo_row = sb("xbo_row", [P, D])

        ident = sb("ident", [P, P])
        before = sb("before", [P, P], F16)
        ones = sb("ones", [P, P], F16)
        iota = sb("iota", [P, P])
        row_i = sb("row_i", [P, 1], I32)
        row1 = sb("row1", [P, 1])
        thr_i = sb("thr_i", [P, CC], I32)
        thr = sb("thr", [P, CC])
        spare_i = sb("spare_i", [P, CC], I32)
        spare = sb("spare", [P, CC])
        neg_half = sb("neg_half", [P, 4])

        xt32 = sb("xt32", [P, DC, S])
        xt = sb("xt", [P, 2, DC, S], F16)
        qk32 = sb("qk32", [P, 2, 2 * S])
        qk = sb("qk", [P, 2, 2, 2 * S], F16)
        arena_v = sb("arena_v", [P, 2 * TT * E], F16)
        v = arena_v[:, :].rearrange("p (s t e) -> p s t e", s=2, t=TT)
        arena_p = sb("arena_p", [P, 4096])
        probs = arena_p[:, 0:2048].rearrange("p (b h q k) -> p b h q k", b=2, h=2, q=TT)
        pT = arena_p[:, 2048:4096].bitcast(F16).rearrange("p (b s h n) -> p b s h n", b=2, s=2, h=2)
        s_max = sb("s_max", [P, 2, 4])
        s_neg = sb("s_neg", [P, 2, 4])
        s_den = sb("s_den", [P, 2, 4])
        s_rden = sb("s_rden", [P, 2, 4])
        o32 = sb("o32", [P, 2, S])
        arena_a = sb("arena_a", [P, 2 * EC * S], F16)
        o = arena_a[:, :].rearrange("p (s j n) -> p s j n", s=2, j=EC)

        xr = sb("xr", [P, TT, D])
        z = sb("z", [P, TT, D])
        before_f32 = z[:, 0, 0:P]
        iota_i = z[:, 0, P:2 * P].bitcast(I32)
        x1 = sb("x1", [P, TT, D])
        x2 = sb("x2", [P, TT, D])
        stats1 = sb("stats1", [P, TT, 6])
        mv1 = sb("mv1", [P, TT, 2])
        ve1 = sb("ve1", [P, TT])
        rstd1 = sb("rstd1", [P, TT])
        stats2 = sb("stats2", [P, TT, 6])
        mv2 = sb("mv2", [P, TT, 2])
        ve2 = sb("ve2", [P, TT])
        rstd2 = sb("rstd2", [P, TT])

        ct32 = stage[:, 1, 0:1024].rearrange("p (c n) -> p c n", c=DC)
        ct = sb("ct", [P, 2, DC, S], F16)
        mask_i = sb("mask_i", [P, TT, S], I32)
        mask_add = stage[:, 1, 4096:4608].rearrange("p (t n) -> p t n", t=TT)
        x1T = sb("x1T", [P, 2, DC, S], F16)
        q2 = sb("q2", [XD, 2, S], F16)
        k2 = sb("k2", [XD, 2, S], F16)
        v2 = sb("v2", [P, 2, TT, XD], F16)
        p2 = sb("p2", [P, TT, S])
        m2 = sb("m2", [P, TT])
        n2 = sb("n2", [P, TT])
        den2 = sb("den2", [P, TT])
        rden2 = sb("rden2", [P, TT])
        p2T = sb("p2T", [P, 2, 2, S], F16)
        o2 = sb("o2", [XD, 2, S], F16)

        x2T = stage[:, 1, 1024:2048].rearrange("p (c n) -> p c n", c=DC)
        top_l = sb("top_l", [P, TT, 8])
        neg_l = sb("neg_l", [P, TT])
        ex = sb("ex", [P, TT, NX])
        den_l = sb("den_l", [P, TT])
        rden_l = sb("rden_l", [P, TT])
        pr = sb("pr", [P, TT, NX])
        top_p = sb("top_p", [P, TT, 8])
        left = sb("left", [P, TT, NX])
        sel = sb("sel", [P, TT, NX], F16)
        sel_sum = sb("sel_sum", [P, 2, NX], F16)
        w_sum = sb("w_sum", [P, TT])
        w_rsum = sb("w_rsum", [P, TT])
        w32 = sb("w32", [P, TT, NX])
        w_hi = sb("w_hi", [P, TT, NX], F16)
        w_lo = sb("w_lo", [P, TT, NX], F16)
        ge = sb("ge", [P, TT * NX, CC + 1])
        n_ge = sb("n_ge", [P, TT * NX])
        pos_in = sb("pos_in", [P, TT * NX])
        in_chunk = sb("in_chunk", [P, TT * NX, CC])
        chosen = sb("chosen", [P, TT * NX, CC])
        tile_no = sb("tile_no", [P, TT])
        said = sb("said", [P, TT * NX, 4, CC], F16)
        onehot = stage[:, 1, 2048:4096].bitcast(F16).rearrange("p (t e n) -> p t e n", t=TT, e=NX // 2)
        slots = sb("slots", [P, NX, 4, CC])
        tok, tok0, empty = in_chunk[:, 0:NX, :], in_chunk[:, NX:2 * NX, :], chosen[:, 0:NX, :]
        idx_from = sb("idx_from", [P, NX, CC], I32)
        idx_to = sb("idx_to", [P, NX, CC], I32)
        w_slot = sb("w_slot", [P, NX, CC])
        cur_from = sb("cur_from", [P, 2, CC], I32)
        cur_to = sb("cur_to", [P, 2, CC], I32)
        cur_w = sb("cur_w", [P, 2, CC])
        GT = 4
        GROUPS = N // (GT * P)
        per3 = xr[:, :, :].rearrange("p t n -> p (t n)")
        stats3 = per3[:, 0:6 * GROUPS * GT].rearrange("p (g t k) -> p g t k", g=GROUPS, t=GT)
        mv3 = per3[:, 6 * GROUPS * GT:8 * GROUPS * GT].rearrange("p (g t k) -> p g t k", g=GROUPS, t=GT)
        ve3, neg_mean3, rstd3, shift3 = (per3[:, k * GROUPS * GT:(k + 1) * GROUPS * GT]
                                         .rearrange("p (g t) -> p g t", g=GROUPS) for k in range(8, 12))

        NW = WGU + WDN
        ew = arena_w[:, 0:4 * NW].rearrange("p (b s n) -> p b s n", b=2, s=2)
        ew_gu = ew[:, :, :, 0:WGU].rearrange("p b s (c f) -> p b s c f", c=DC)
        ew_dn = ew[:, :, :, WGU:NW].rearrange("p b s (c n) -> p b s c n", c=FC)
        hT = arena_w[:, 4 * NW:4 * NW + 2 * FC * CAP].rearrange("p (s f n) -> p s f n", s=2, f=FC)
        y = arena_o[:, :].bitcast(F32).rearrange("p (b c n) -> p b c n", b=2, c=CC)
        xg = arena_p[:, :].rearrange("p (b c n) -> p b c n", b=2, c=CC)
        xgT = arena_v[:, :].rearrange("p (s c n) -> p s c n", s=2, c=DC)
        act32 = arena_a[:, :].bitcast(F32).rearrange("p (k b n) -> p k b n", k=2, b=2)
        silu, h32 = act32[:, 0], act32[:, 1]
        rows3 = arena_wo[:, :].bitcast(F32).rearrange("p (g t n) -> p g t n", g=GROUPS, t=GT)

        bank = [ctx.enter_context(nc.psum_tensor(f"bank{i}", [P, 512], F32)) for i in range(8)]
        ps_qk = bank[0]
        ps_v = bank[1]
        ps_s = bank[2:4]
        ps_t = bank[4:6]
        ps_o = bank[6]
        ps_x = bank[7]
        ps_gate = bank[7][:, 0:TT * NX].rearrange("p (t e) -> p t e", t=TT)
        ps_pos = bank[7][:, 0:TT * NX]
        ps_slot = bank[1][:, 0:256]
        ps_h = (bank[0:2], bank[2:4])
        ps_xg = bank[4:6]
        ps_y = bank[6:8]

        HX = NX // 2

        s_const = sem("s_const")
        s_constv = sem("s_constv")
        ld_w = [sem("ld_w0"), sem("ld_w1")]
        ld_setup = [sem(f"ld_setup{k}") for k in range(4)]
        ld_bias, ld_small = sem("ld_bias"), sem("ld_small")
        w_split_hi = sem("w_split_hi")
        w_split_lo = sem("w_split_lo")
        ld_x, ld_row, ld_ctx, ld_mask = sem("ld_x"), sem("ld_row"), sem("ld_ctx"), sem("ld_mask")
        xt_hi, xt_lo = sem("xt_hi"), sem("xt_lo")
        qk_mm, qk_hi, qk_lo = sem("qk_mm"), sem("qk_hi"), sem("qk_lo")
        s_mm, s_maxd, s_negd = sem("s_mm"), sem("s_maxd"), sem("s_negd")
        e_done, r_done, p_done = sem("e_done"), sem("r_done"), sem("p_done")
        t_mm, pt_hi, pt_lo = sem("t_mm"), sem("pt_hi"), sem("pt_lo")
        v_mm, v_hi, v_lo = sem("v_mm"), sem("v_hi"), sem("v_lo")
        pv_mm, o_hi, o_lo = sem("pv_mm"), sem("o_hi"), sem("o_lo")
        wo_mm, xb_done = sem("wo_mm"), sem("xb_done")
        ln1, ln1_rstd, x1_done, x1b_done = sem("ln1"), sem("ln1_rstd"), sem("x1_done"), sem("x1b_done")
        x1t_mm, x1t_hi, x1t_lo = sem("x1t_mm"), sem("x1t_hi"), sem("x1t_lo")
        ct_hi, ct_lo = sem("ct_hi"), sem("ct_lo")
        kv_mm, kv_hi, kv_lo = sem("kv_mm"), sem("kv_hi"), sem("kv_lo")
        q2_mm, q2_hi, q2_lo = sem("q2_mm"), sem("q2_hi"), sem("q2_lo")
        s2_mm, mask_done, s2_dve = sem("s2_mm"), sem("mask_done"), sem("s2_dve")
        e2_done, r2_done, p2_done = sem("e2_done"), sem("r2_done"), sem("p2_done")
        t2_mm, t2_hi, t2_lo = sem("t2_mm"), sem("t2_hi"), sem("t2_lo")
        pv2_mm, o2_hi, o2_lo = sem("pv2_mm"), sem("o2_hi"), sem("o2_lo")
        out2_mm = sem("out2_mm")
        ln2, ln2_rstd, x2_done = sem("ln2"), sem("ln2_rstd"), sem("x2_done")
        st_x2 = sem("st_x2")
        x2t_mm, x2t_done = sem("x2t_mm"), sem("x2t_done")
        gate_mm, rt_exp, rt = sem("gate_mm"), sem("rt_exp"), sem("rt")
        pos_mm, oh_done, slot_mm, slot_done = sem("pos_mm"), sem("oh_done"), sem("slot_mm"), sem("slot_done")
        table = sem("table")
        cur_done = sem("cur_done")
        ld_xg = [sem("ld_xg0"), sem("ld_xg1")]
        xg_mm, xg_hi, xg_lo = sem("xg_mm"), sem("xg_hi"), sem("xg_lo")
        ew_hi, ew_lo_gu, ew_lo_dn = sem("ew_hi"), sem("ew_lo_gu"), sem("ew_lo_dn")
        g_mm, u_mm, silu_done = sem("g_mm"), sem("u_mm"), sem("silu_done")
        h_f32, h_hi, h_lo = sem("h_f32"), sem("h_hi"), sem("h_lo")
        y_mm, y_done = sem("y_mm"), sem("y_done")
        st_y = sem("st_y")
        st_zero = sem("st_zero")
        HALF = GROUPS // 2
        ld_acc = [sem(f"ld_acc{k}") for k in range(HALF)]
        ln3, ln3_rstd, out_done = sem("ln3"), sem("ln3_rstd"), sem("out_done")
        st_out = sem("st_out")

        RT = 27
        N_CONST, N_CONSTV = 12, 8

        Q0, K0, V0, V1, Q1, K1, O0, O1, X3, XO = range(10)
        SETUP = 10
        EH = E // 2

        def piece_place(n):
            at = stage[:, :, :].rearrange("p k n -> p (k n)")[:, n % 4 * DC * EH:(n % 4 + 1) * DC * EH]
            if n == X3:
                return at[:, 0:3 * DC * XD].rearrange("p (c n) -> p c n", c=3 * DC)
            if n == XO:
                return at[0:XD, 0:D].unsqueeze(1)
            return at.rearrange("p (c n) -> p c n", c=DC)

        def piece_split(n, part):
            if n in (O0, O1):
                return wo[:, part, (n - O0) * DC:(n - O0 + 1) * DC, :]
            if n == X3:
                return wx[:, part].rearrange("p k c n -> p (k c) n")
            if n == XO:
                return wxo[:, part, :].unsqueeze(1)
            w, half = {Q0: (0, 0), Q1: (0, 1), K0: (1, 0), K1: (1, 1), V0: (2, 0), V1: (2, 1)}[n]
            return wqkv[:, w, part, :, half * EH:(half + 1) * EH]

        def piece_loaded(n):
            return 16 * (n // 4 + (3 if n == X3 else 1))

        def rounds(eng, work):
            work(0, True, False, False, False)
            work(1, True, True, False, False)
            work(2, True, True, True, False)
            work(3, True, True, True, True)
            with eng.Fori(4, B) as r:
                work(r, True, True, True, True)
            work(B, False, True, True, True)
            work(B + 1, False, False, True, True)
            work(B + 2, False, False, False, True)

        def pairs(b, head, tail):
            def call(stage_of, j):
                if j >= 0 and head:
                    stage_of(b, j)
                elif j < 0 and tail:
                    stage_of(b - 1, j + EC)
            return call

        def cols(r):
            return bass.ds(r * S, S)

        def rows_of(ap, b):
            return ap[bass.ds(b * S, S), :].rearrange("(t p) n -> p t n", p=P)

        block = ctx.enter_context(nc.Block())

        @block.sync
        def _(sp):
            def piece(n, src):
                if n >= 4:
                    sp.wait_ge(w_split_hi, n - 3)
                    sp.wait_ge(w_split_lo, n - 3)
                for k, one in enumerate(src):
                    place = piece_place(n)[:, k * DC:(k + 1) * DC, :] if n == X3 else piece_place(n)
                    sp.dma_start(place, one).then_inc(ld_setup[n % 4], 16)

            def columns(w, half):
                return [w[:, half * EH:(half + 1) * EH].rearrange("(c p) n -> p c n", p=P)]

            def o_rows(half):
                return [woT[half * EH:(half + 1) * EH, :].rearrange("(c p) n -> p c n", p=P)]

            piece(Q0, columns(wqT, 0))
            sp.dma_start(xt32[:, :, :], xT[:, 0:S].rearrange("(c p) n -> p c n", p=P)).then_inc(ld_x, 16)
            piece(K0, columns(wkT, 0))
            for k, src in enumerate((bq, bk, bv)):
                sp.dma_start(bqkv[:, k, :], src).then_inc(ld_bias, 16)
            piece(V0, columns(wvT, 0))
            piece(V1, columns(wvT, 1))
            piece(Q1, columns(wqT, 1))
            piece(K1, columns(wkT, 1))
            piece(O0, o_rows(0))
            piece(O1, o_rows(1))
            sp.dma_start(bo_row[:, :], bo.partition_broadcast(P)).then_inc(ld_small, 16)
            sp.dma_start(xbo_row[:, :], x_bo.partition_broadcast(P)).then_inc(ld_small, 16)
            sp.dma_start(gate_w[:, :, :], gateT.rearrange("(c p) n -> p c n", p=P)).then_inc(ld_small, 16)
            piece(X3, [w.rearrange("(c p) n -> p c n", p=P) for w in (x_wq, x_wk, x_wv)])
            piece(XO, [x_wo.unsqueeze(1)])

            def load_expert(e, place):
                sp.dma_start(stage[:, place, 0:WGU].rearrange("p (c f) -> p c f", c=DC),
                             wguT[e].rearrange("(c p) f -> p c f", p=P)).then_inc(ld_w[place], 16)
                sp.dma_start(stage[:, place, WGU:NW].rearrange("p (c n) -> p c n", c=FC),
                             wdnT[e].rearrange("(c p) n -> p c n", p=P)).then_inc(ld_w[place], 16)

            def work(r, head, tail, route, fill):
                if head and not (isinstance(r, int) and r == 0):
                    sp.wait_ge(xt_hi, count(r, 1))
                    sp.wait_ge(xt_lo, count(r, 1))
                    sp.dma_start(xt32[:, :, :], xT[:, cols(r)].rearrange("(c p) n -> p c n", p=P)).then_inc(ld_x, 16)
                if tail:
                    t = r - 1
                    if isinstance(r, int) and r == 1:
                        sp.wait_ge(w_split_hi, SETUP)
                        sp.wait_ge(w_split_lo, SETUP)
                    past(sp, ct_hi, count(t, 1))
                    past(sp, ct_lo, count(t, 1))
                    sp.dma_start(ct32[:, :, :], ctxT[:, cols(t)].rearrange("(c p) n -> p c n", p=P)).then_inc(ld_ctx, 16)
                    past(sp, mask_done, count(t, 1))
                    sp.dma_start(mask_i[:, :, :], rows_of(mask, t)).then_inc(ld_mask, 16)
                    past(sp, ln1, count(t, 7))
                    sp.dma_start(xr[:, :, :], rows_of(x_rows, t)).then_inc(ld_row, 16)
                if route:
                    t = r - 2
                    sp.wait_ge(x2_done, count(t, TT, TT))
                    sp.dma_start(rows_of(x2_rows, t), x2[:, :, :]).then_inc(st_x2, 16)
                    sp.dma_start(rows_of(acc_rows, t), x2[:, :, :]).then_inc(st_x2, 16)
                if isinstance(r, int) and r == 1:
                    load_expert(0, 0)
                if isinstance(r, int) and r == B + 1:
                    sp.wait_ge(ew_lo_gu, 1)
                    sp.wait_ge(ew_lo_dn, 1)
                    load_expert(1, 0)

            rounds(sp, work)
            sp.wait_ge(slot_mm, B * 2)
            sp.wait_ge(ld_xg[0], 64)
            load_expert(2, 1)

            def next_but_one(e, place):
                sp.wait_ge(ew_lo_gu, count(e, 1, 1))
                sp.wait_ge(ew_lo_dn, count(e, 1, 1))
                load_expert(e + 2, place)

            with sp.Fori(1, NX - 4, 2) as e:
                next_but_one(e, 0)
                next_but_one(e + 1, 1)
            next_but_one(NX - 3, 0)

            sp.wait_ge(st_y, NX * 64)
            sp.wait_ge(y_done, NX * CC)

            def group_rows(ap, g):
                return ap[bass.ds(g * GT * P, GT * P), :].rearrange("(t p) n -> p t n", p=P)

            for g in range(GROUPS):
                if g >= HALF:
                    sp.wait_ge(ld_acc[g % HALF], 16)
                sp.dma_start(rows3[:, g], group_rows(acc_rows, g)).then_inc(ld_acc[g % HALF], 16)
            for g in range(GROUPS):
                sp.wait_ge(out_done, (g + 1) * GT)
                sp.dma_start(group_rows(out, g), rows3[:, g]).then_inc(st_out, 16)
            sp.wait_ge(st_out, GROUPS * 16)

        @block.tensor
        def _(pe):
            def split_mm(out_ap, lhs, rhs, chunks):
                for n, (a, c) in enumerate(PARTS):
                    for i in range(chunks):
                        mm = pe.matmul(out_ap, lhs(a, i), rhs(c, i),
                                       start=(n == 0 and i == 0), stop=(n == 2 and i == chunks - 1))
                return mm

            def qk_pair(b, j):
                if j == 0:
                    pe.wait_ge(xt_lo, count(b, 1, 1))
                if isinstance(b, int) and b == 0 and j == 0:
                    pe.wait_ge(w_split_lo, K0 + 1)
                if isinstance(b, int) and b == 0 and j == EC // 2:
                    pe.wait_ge(w_split_lo, K1 + 1)
                past(pe, qk_hi, count(b, EC, j))
                for w in range(2):
                    mm = split_mm(ps_qk[:, w * S:(w + 1) * S],
                                  lambda a, i: wqkv[:, w, a, i, j * P:(j + 1) * P],
                                  lambda c, i: xt[:, c, i, :], DC)
                mm.then_inc(qk_mm, 1)

            def scores(b, j):
                past(pe, e_done, count(b, EC, j))
                pe.wait_ge(qk_lo, count(b, EC, j + 1))
                pe.wait_ge(s_const, N_CONST)
                for n, (a, c) in enumerate(PARTS):
                    for t in range(TT):
                        for h in range(2):
                            hp = slice(h * DK, (h + 1) * DK)
                            mm = pe.matmul(ps_s[h][:, t * S:(t + 1) * S],
                                           qk[hp, j % 2, a, t * P:(t + 1) * P], qk[hp, j % 2, c, S:2 * S],
                                           start=(n == 0 and t == 0), stop=(n == 2 and t == TT - 1),
                                           skip_group_check=True)
                mm.then_inc(s_mm, 1)

            def values(b, g, tail, fill):
                half, t = g // 2, g % 2
                if isinstance(b, int) and b == 0 and t == 0:
                    pe.wait_ge(w_split_lo, (V0, V1)[half] + 1)
                if g == 0 and fill:
                    pe.wait_ge(slot_done, count(b - 3, 2, 1))
                elif g == 0 and tail:
                    past(pe, kv_lo, count(b - 1, 2))
                if g:
                    pe.wait_ge(v_lo, count(b, 4, g))
                if g == 2 and fill:
                    pe.wait_ge(slot_done, count(b - 3, 2, 2))
                split_mm(ps_v[:, :],
                         lambda a, i: xt[:, a, i, t * P:(t + 1) * P],
                         lambda c, i: wqkv[:, 2, c, i, half * 512:(half + 1) * 512], DC).then_inc(v_mm, 1)

            def turn(b, j):
                pe.wait_ge(p_done, count(b, EC, j + 1))
                past(pe, pt_lo, count(b, 2 * EC, 2 * j))
                for h in range(2):
                    for c in range(2):
                        for t in range(TT):
                            mm = pe.transpose(ps_t[h][:, c * S + t * P:c * S + (t + 1) * P],
                                              probs[:, j % 2, h, t, c * P:(c + 1) * P], ident[:, :])
                    mm.then_inc(t_mm, 1)

            def weigh(b, j):
                past(pe, o_hi, count(b, EC, j))
                if j in (0, EC // 2):
                    pe.wait_ge(v_lo, count(b, 4, 2 if j == 0 else 4))
                pe.wait_ge(pt_lo, count(b, 2 * EC, 2 * j + 2))
                for n, (a, c) in enumerate(PARTS):
                    for i in range(2):
                        for h in range(2):
                            mm = pe.matmul(ps_o[h * DK:(h + 1) * DK, 0:S],
                                           v[:, a, i, (2 * j + h) * DK:(2 * j + h + 1) * DK],
                                           pT[:, j % 2, c, h, i * S:(i + 1) * S],
                                           start=(n == 0 and i == 0), stop=(n == 2 and i == 1),
                                           skip_group_check=True)
                mm.then_inc(pv_mm, 1)

            def project(b, t, route):
                if t == 0:
                    if isinstance(b, int) and b == 0:
                        pe.wait_ge(w_split_lo, SETUP)
                    pe.wait_ge(o_lo, count(b, EC, EC))
                    if route:
                        pe.wait_ge(x2t_done, count(b - 1, TT, TT))
                else:
                    pe.wait_ge(ln1, count(b, 7, t))
                split_mm(ps_x[:, :], lambda a, i: o[:, a, i, t * P:(t + 1) * P],
                         lambda c, i: wo[:, c, i, :], EC).then_inc(wo_mm, 1)

            def turn_x1(b, t, head, route, fill):
                pe.wait_ge(x1_done, count(b, TT, t + 1))
                if t == 0 and head:
                    pe.wait_ge(v_lo, count(b + 1, 4, 4))
                elif t == 0 and fill:
                    pe.wait_ge(slot_done, count(b - 2, 2, 2))
                elif t and route:
                    pe.wait_ge(rt, count(b - 1, RT, 20))
                into = (ps_v, ps_x)[t]
                for c in range(DC):
                    mm = pe.transpose(into[:, c * P:(c + 1) * P], x1[:, t, c * P:(c + 1) * P], ident[:, :])
                mm.then_inc(x1t_mm, 1)

            def ctx_kv(b):
                pe.wait_ge(ct_lo, count(b, 1, 1))
                pe.wait_ge(x1t_lo, count(b, TT, 1))
                split_mm(ps_v[0:XD, 0:S], lambda a, i: wx[:, a, 1, i, :], lambda c, i: ct[:, c, i, :], DC)
                for t in range(TT):
                    mm = split_mm(ps_v[:, S + t * XD:S + (t + 1) * XD],
                                  lambda a, i: ct[:, a, i, t * P:(t + 1) * P], lambda c, i: wx[:, c, 2, i, :], DC)
                mm.then_inc(kv_mm, 1)

            def cross_q(b):
                pe.wait_ge(x1t_lo, count(b, TT, TT))
                split_mm(ps_x[0:XD, 0:S], lambda a, i: wx[:, a, 0, i, :], lambda c, i: x1T[:, c, i, :], DC)\
                    .then_inc(q2_mm, 1)

            def cross_scores(b):
                pe.wait_ge(q2_lo, count(b, 1, 1))
                pe.wait_ge(kv_lo, count(b, 2, 1))
                pe.wait_ge(s_const, N_CONST)
                for t in range(TT):
                    mm = split_mm(ps_x[:, t * S:(t + 1) * S], lambda a, i: q2[:, a, t * P:(t + 1) * P],
                                  lambda c, i: k2[:, c, :], 1)
                mm.then_inc(s2_mm, 1)

            def cross_turn(b):
                pe.wait_ge(p2_done, count(b, 1, 1))
                for c in range(2):
                    for t in range(TT):
                        mm = pe.transpose(ps_x[:, c * S + t * P:c * S + (t + 1) * P],
                                          p2[:, t, c * P:(c + 1) * P], ident[:, :])
                mm.then_inc(t2_mm, 1)

            def cross_weigh(b):
                pe.wait_ge(t2_lo, count(b, 1, 1))
                split_mm(ps_x[0:XD, 0:S], lambda a, i: v2[:, a, i, :], lambda c, i: p2T[:, c, i, :], 2)\
                    .then_inc(pv2_mm, 1)

            def cross_project(b, t):
                if t == 0:
                    pe.wait_ge(o2_lo, count(b, 1, 1))
                else:
                    pe.wait_ge(ln2, count(b, 7, t))
                pe.wait_ge(s_const, N_CONST)
                split_mm(ps_x[:, :], lambda a, i: o2[:, a, t * P:(t + 1) * P], lambda c, i: wxo[:, c, :], 1)\
                    .then_inc(out2_mm, 1)

            def turn_x2(b, t):
                pe.wait_ge(x2_done, count(b, TT, t + 1))
                if t:
                    pe.wait_ge(x2t_done, count(b, TT, t))
                for c in range(DC):
                    mm = pe.transpose(ps_x[:, c * P:(c + 1) * P], x2[:, t, c * P:(c + 1) * P], ident[:, :])
                mm.then_inc(x2t_mm, 1)

            def gate(b, tail):
                pe.wait_ge(x2t_done, count(b, TT, TT))
                if tail:
                    pe.wait_ge(ln1, count(b + 1, 7, TT))
                for t in range(TT):
                    for c in range(DC):
                        mm = pe.matmul(ps_gate[:, t, :], x2T[:, c, t * P:(t + 1) * P], gate_w[:, c, :],
                                       start=(c == 0), stop=(c == DC - 1))
                mm.then_inc(gate_mm, 1)

            def positions(b):
                pe.wait_ge(rt, count(b, RT, 11))
                for t in range(TT):
                    pe.matmul(ps_pos[:, t * NX:(t + 1) * NX], before[:, :], sel[:, t, :], start=True, stop=False)
                    mm = pe.matmul(ps_pos[:, t * NX:(t + 1) * NX], ones[:, :], sel_sum[:, t, :],
                                   start=False, stop=True)
                mm.then_inc(pos_mm, 1)

            def fill_slots(b, k, head):
                pe.wait_ge(oh_done, count(b, 2 * TT, TT * (k + 1)))
                past(pe, slot_done, count(b, 2, k))
                if k == 0:
                    pe.wait_ge(rt, count(b, RT, 26))
                    pe.wait_ge(kv_lo, count(min(b + 2, B) if isinstance(b, int) else b + 2, 2))
                elif head:
                    pe.wait_ge(v_lo, count(b + 3, 4, 2))
                for e in range(HX):
                    for t in range(TT):
                        mm = pe.matmul(ps_slot[:, e * 16:(e + 1) * 16], onehot[:, t, e, :],
                                       said[:, t * NX + k * HX + e, :, :].rearrange("p a c -> p (a c)"),
                                       start=(t == 0), stop=(t == TT - 1))
                mm.then_inc(slot_mm, 1)

            def work(r, head, tail, route, fill):
                b, t, u, f = r, r - 1, r - 2, r - 3
                pair = pairs(r, head, tail)

                def step(s, between=()):
                    pair(scores, s - 2)
                    pair(turn, s - 3)
                    for on, run in between:
                        if on:
                            run()
                    pair(weigh, s - 4)
                    if head:
                        qk_pair(b, s)

                step(0, [(fill, lambda: fill_slots(f, 0, head))])
                if head:
                    values(b, 0, tail, fill)
                step(1, [(route, lambda: cross_turn(u))])
                if route:
                    cross_weigh(u)
                if head:
                    values(b, 1, tail, fill)
                step(2, [(route, lambda: cross_project(u, 0)), (fill, lambda: fill_slots(f, 1, head))])
                if route:
                    cross_project(u, 1)
                step(3)
                if route:
                    turn_x2(u, 0)
                if head:
                    values(b, 2, tail, fill)
                if route:
                    turn_x2(u, 1)
                step(4, [(tail, lambda: project(t, 0, route))])
                if tail:
                    project(t, 1, route)
                step(5, [(route, lambda: gate(u, tail))])
                if head:
                    values(b, 3, tail, fill)
                step(6, [(tail, lambda: turn_x1(t, 0, head, route, fill)), (route, lambda: positions(u))])
                if tail:
                    turn_x1(t, 1, head, route, fill)
                step(7, [(tail, lambda: ctx_kv(t)), (tail, lambda: cross_q(t))])
                if tail:
                    cross_scores(t)

            rounds(pe, work)

            def up_gate(e, k):
                pe.wait_ge(xg_lo, count(e, CC, CC))
                pe.wait_ge(ew_lo_gu, count(e, 1, 1))
                for f in range(FC):
                    n = FC * k + f
                    past(pe, h_f32, count(e, FC, f - 1))
                    split_mm(ps_h[n % 2][0][:, :], lambda a, i: ew_gu[:, k, a, i, f * P:(f + 1) * P],
                             lambda c, i: xgT[:, c, i, :], DC).then_inc(g_mm, 1)
                    split_mm(ps_h[n % 2][1][:, :], lambda a, i: ew_gu[:, k, a, i, F + f * P:F + (f + 1) * P],
                             lambda c, i: xgT[:, c, i, :], DC).then_inc(u_mm, 1)

            def turn_xg(e, k, c):
                past(pe, xg_lo, count(e, CC, c - 1))
                for d in range(DC):
                    mm = pe.transpose(ps_xg[c % 2][:, d * P:(d + 1) * P], xg[:, k, c, d * P:(d + 1) * P], ident[:, :])
                mm.then_inc(xg_mm, 1)

            def down(e, k, ahead):
                pe.wait_ge(ew_lo_dn, count(e, 1, 1))
                for c in range(CC):
                    past(pe, y_done, count(e, CC, c - 1))
                    for f in range(FC):
                        if c == 0:
                            pe.wait_ge(h_lo, count(e, FC, f + 1))
                        for n, (a, w) in enumerate(PARTS):
                            mm = pe.matmul(ps_y[c % 2][:, :], hT[:, a, f, c * P:(c + 1) * P], ew_dn[:, k, w, f, :],
                                           start=(f == 0 and n == 0), stop=(f == FC - 1 and n == 2))
                    mm.then_inc(y_mm, 1)
                    if ahead and c + 2 < CC:
                        turn_xg(e + 1, 1 - k, c + 2)

            def expert(e, k, ahead, landed):
                up_gate(e, k)
                if ahead:
                    pe.wait_ge(ld_xg[1 - k], landed)
                    turn_xg(e + 1, 1 - k, 0)
                    turn_xg(e + 1, 1 - k, 1)
                down(e, k, ahead)

            pe.wait_ge(ld_xg[0], 64)
            for c in range(CC):
                turn_xg(0, 0, c)
            expert(0, 0, True, 64)
            expert(1, 1, True, 128)
            with pe.Fori(1, NX // 2 - 1) as m:
                expert(m * 2, 0, True, count(m, 64, 64))
                expert(m * 2 + 1, 1, True, count(m, 64, 128))
            expert(NX - 2, 0, True, NX // 2 * 64)
            expert(NX - 1, 1, False, 0)

        @block.scalar
        def _(act):
            def piece_hi(n):
                act.wait_ge(ld_setup[n % 4], piece_loaded(n))
                nc.scalar.activation(piece_split(n, 0), piece_place(n), ACT.Copy, scale=W_SCALE).then_inc(w_split_hi, 1)

            def split_x(b):
                act.wait_ge(ld_x, count(b, 16, 16))
                past(act, qk_mm, count(b, EC))
                past(act, v_mm, count(b, 4))
                nc.scalar.activation(xt[:, 0, :, :], xt32[:, :, :], ACT.Copy).then_inc(xt_hi, 1)

            piece_hi(Q0)
            split_x(0)
            for n in (K0, V0, V1):
                piece_hi(n)

            def qk_out(b, j):
                past(act, s_mm, count(b, EC, j - 1))
                act.wait_ge(qk_mm, count(b, EC, j + 1))
                for w in range(2):
                    at = slice(w * S, (w + 1) * S)
                    nc.scalar.activation(qk32[:, j % 2, at], ps_qk[:, at], ACT.Identity,
                                         bias=bqkv[:, w, j:j + 1], scale=1.0 / W_SCALE)
                    ins = nc.scalar.activation(qk[:, j % 2, 0, at], ps_qk[:, at], ACT.Identity,
                                               bias=bqkv[:, w, j:j + 1], scale=1.0 / W_SCALE)
                ins.then_inc(qk_hi, 1)

            def heads_out(b, j):
                past(act, o_lo, count(b, EC, j - 1))
                if j == 0:
                    past(act, wo_mm, count(b, TT))
                act.wait_ge(pv_mm, count(b, EC, j + 1))
                for dst in (o32[:, j % 2, :], o[:, 0, j, :]):
                    ins = nc.scalar.activation(dst, ps_o[:, 0:S], ACT.Identity, bias=bqkv[:, 2, j:j + 1],
                                               scale=1.0 / P_SCALE)
                ins.then_inc(o_hi, 1)

            def exps(b, j):
                past(act, t_mm, count(b, 2 * EC, 2 * j - 2))
                act.wait_ge(s_negd, count(b, EC, j + 1))
                for h in range(2):
                    for t in range(TT):
                        n = 2 * h + t
                        ins = nc.scalar.activation(probs[:, j % 2, h, t, :], ps_s[h][:, t * S:(t + 1) * S], ACT.Exp,
                                                   bias=s_neg[:, j % 2, n:n + 1], scale=SCORE,
                                                   accum_out=s_den[:, j % 2, n:n + 1])
                ins.then_inc(e_done, 1)

            def values_hi(b, g):
                half, t = g // 2, g % 2
                if t == 0:
                    past(act, pv_mm, count(b, EC, half * EC // 2 - EC // 2))
                act.wait_ge(v_mm, count(b, 4, g + 1))
                nc.scalar.activation(v[:, 0, t, half * 512:(half + 1) * 512], ps_v[:, :], ACT.Copy,
                                     scale=1.0 / W_SCALE).then_inc(v_hi, 1)

            def turned_hi(b, j):
                past(act, pv_mm, count(b, EC, j - 1))
                for h in range(2):
                    act.wait_ge(t_mm, count(b, 2 * EC, 2 * j + h + 1))
                    nc.scalar.activation(pT[:, j % 2, 0, h, :], ps_t[h][:, :], ACT.Copy,
                                         scale=P_SCALE).then_inc(pt_hi, 1)

            def x1_hi(b, t):
                act.wait_ge(x1t_mm, count(b, TT, t + 1))
                past(act, q2_mm, count(b, 1))
                nc.scalar.activation(x1T[:, 0, :, t * P:(t + 1) * P],
                                     (ps_v, ps_x)[t][:, :].rearrange("p (c n) -> p c n", c=DC), ACT.Copy).then_inc(x1t_hi, 1)

            def split_ctx(b):
                act.wait_ge(ld_ctx, count(b, 16, 16))
                past(act, kv_mm, count(b, 1))
                nc.scalar.activation(ct[:, 0, :, :], ct32[:, :, :], ACT.Copy).then_inc(ct_hi, 1)

            def kv2_hi(b):
                act.wait_ge(kv_mm, count(b, 1, 1))
                past(act, pv2_mm, count(b, 1))
                nc.scalar.activation(k2[:, 0, :], ps_v[0:XD, 0:S], ACT.Copy, scale=1.0 / W_SCALE).then_inc(kv_hi, 1)
                nc.scalar.activation(v2[:, 0].rearrange("p t n -> p (t n)"), ps_v[:, S:S + TT * XD], ACT.Copy,
                                     scale=1.0 / W_SCALE).then_inc(kv_hi, 1)

            def q2_high(b):
                act.wait_ge(q2_mm, count(b, 1, 1))
                past(act, s2_mm, count(b, 1))
                nc.scalar.activation(q2[:, 0, :], ps_x[0:XD, 0:S], ACT.Copy, scale=1.0 / W_SCALE).then_inc(q2_hi, 1)

            def exp2(b):
                act.wait_ge(s2_dve, count(b, 3, 3))
                for t in range(TT):
                    ins = nc.scalar.activation(p2[:, t, :], p2[:, t, :], ACT.Exp, bias=n2[:, t:t + 1],
                                               accum_out=den2[:, t:t + 1])
                ins.then_inc(e2_done, 1)

            def turned2_hi(b):
                act.wait_ge(t2_mm, count(b, 1, 1))
                past(act, pv2_mm, count(b, 1))
                nc.scalar.activation(p2T[:, 0].rearrange("p c n -> p (c n)"), ps_x[:, :], ACT.Copy,
                                     scale=P_SCALE).then_inc(t2_hi, 1)

            def o2_high(b):
                act.wait_ge(pv2_mm, count(b, 1, 1))
                past(act, out2_mm, count(b, TT))
                nc.scalar.activation(o2[:, 0, :], ps_x[0:XD, 0:S], ACT.Copy, scale=1.0 / P_SCALE).then_inc(o2_hi, 1)

            W0 = 32 + 48
            W1 = 48

            GU, DN = slice(0, WGU), slice(WGU, NW)

            def weights_hi(e, k, part, place, loads):
                if part == GU:
                    act.wait_ge(ld_w[place], loads)
                    past(act, y_mm, count(e, CC, -CC))
                nc.scalar.activation(ew[:, k, 0, part], stage[:, place, part], ACT.Copy, scale=W_SCALE).then_inc(ew_hi, 1)

            def x2_turned(b, t):
                act.wait_ge(x2t_mm, count(b, TT, t + 1))
                past(act, gate_mm, count(b, 1))
                nc.scalar.activation(x2T[:, :, t * P:(t + 1) * P],
                                     ps_x[:, :].rearrange("p (c n) -> p c n", c=DC), ACT.Copy).then_inc(x2t_done, 1)

            def gate_exp(b):
                act.wait_ge(rt, count(b, RT, 3))
                for t in range(TT):
                    ins = nc.scalar.activation(ex[:, t, :], ps_gate[:, t, :], ACT.Exp, bias=neg_l[:, t:t + 1],
                                               accum_out=den_l[:, t:t + 1])
                ins.then_inc(rt_exp, 1)

            def work(r, head, tail, route, fill):
                b, t, u = r, r - 1, r - 2
                pair = pairs(r, head, tail)

                def step(s, between=(), first=()):
                    pair(turned_hi, s - 3)
                    for on, run in first:
                        if on:
                            run()
                    pair(exps, s - 2)
                    for on, run in between:
                        if on:
                            run()
                    if s != 4:
                        pair(heads_out, s - 4)
                    if head:
                        qk_out(b, s)

                if head and not (isinstance(r, int) and r == 0):
                    split_x(b)
                if isinstance(r, int) and r == 0:
                    act.wait_ge(ld_bias, 48)
                step(0, first=[(route, lambda: exp2(u))])
                if head:
                    values_hi(b, 0)
                if isinstance(r, int) and r == 0:
                    piece_hi(Q1)
                step(1, [(route, lambda: turned2_hi(u))])
                if route:
                    o2_high(u)
                if head:
                    values_hi(b, 1)
                step(2, first=[(isinstance(r, int) and r == 0, lambda: piece_hi(K1))])
                step(3)
                if route:
                    x2_turned(u, 0)
                if head:
                    values_hi(b, 2)
                if route:
                    x2_turned(u, 1)
                step(4)
                if tail:
                    split_ctx(t)
                if isinstance(r, int) and r == B:
                    act.wait_ge(qk_mm, B * EC)
                    act.wait_ge(v_mm, B * 4)
                    weights_hi(0, 0, GU, 0, 32)
                    weights_hi(0, 0, DN, 0, 32)
                if isinstance(r, int) and r == 0:
                    piece_hi(O0)
                pair(heads_out, 0)
                step(5, [(route, lambda: gate_exp(u))])
                if isinstance(r, int) and r == 0:
                    piece_hi(O1)
                if head:
                    values_hi(b, 3)
                step(6, [(tail, lambda: x1_hi(t, 0))])
                if tail:
                    x1_hi(t, 1)
                if isinstance(r, int) and r == 0:
                    piece_hi(X3)
                    piece_hi(XO)
                step(7, [(tail, lambda: kv2_hi(t)), (tail, lambda: q2_high(t))])

            rounds(act, work)

            def tokens_hi(e, c):
                if c == 0:
                    past(act, u_mm, count(e, FC))
                act.wait_ge(xg_mm, count(e, CC, c + 1))
                nc.scalar.activation(xgT[:, 0, :, c * P:(c + 1) * P],
                                     ps_xg[c % 2][:, :].rearrange("p (d n) -> p d n", d=DC), ACT.Copy).then_inc(xg_hi, 1)

            def expert(e, k, ahead, loads):
                if ahead:
                    weights_hi(e + 1, 1 - k, GU, k, loads)
                for f in range(FC):
                    n = FC * k + f
                    act.wait_ge(g_mm, count(e, FC, f + 1))
                    past(act, h_f32, count(e, FC, f - 1))
                    nc.scalar.activation(silu[:, n % 2, :], ps_h[n % 2][0][:, :], ACT.Silu, scale=1.0 / W_SCALE)\
                      .then_inc(silu_done, 1)
                    if f == 0 and ahead:
                        weights_hi(e + 1, 1 - k, DN, k, loads)
                if ahead:
                    tokens_hi(e + 1, 0)
                    tokens_hi(e + 1, 1)
                for c in range(CC):
                    act.wait_ge(y_mm, count(e, CC, c + 1))
                    if c == 0:
                        act.wait_ge(cur_done, count(e, 3, 3))
                        past(act, st_y, count(e, 64, -64))
                    nc.scalar.activation(y[:, k, c, :], ps_y[c % 2][:, :], ACT.Copy,
                                         scale=cur_w[:, k, c:c + 1]).then_inc(y_done, 1)
                    if ahead and c + 2 < CC:
                        tokens_hi(e + 1, c + 2)

            for c in range(CC):
                tokens_hi(0, c)
            expert(0, 0, True, 64)
            expert(1, 1, True, 32)
            with act.Fori(1, NX // 2 - 1) as m:
                expert(m * 2, 0, True, count(m, 32, 64))
                expert(m * 2 + 1, 1, True, count(m, 32, 32))
            expert(NX - 2, 0, True, count(NX // 2 - 1, 32, 64))
            expert(NX - 1, 1, False, 0)

            for g in range(GROUPS):
                act.wait_ge(ln3_rstd, 2 * (g + 1))
                for t in range(GT):
                    nc.scalar.activation(rows3[:, g, t, :], rows3[:, g, t, :], ACT.Identity, bias=shift3[:, g, t:t + 1],
                                         scale=rstd3[:, g, t:t + 1]).then_inc(out_done, 1)

        @block.vector
        def _(dve):
            vec = nc.vector

            def low(dst, src, hi, scale=1.0):
                return vec.scalar_tensor_tensor(out=dst, in0=src, scalar=scale, in1=hi, op0=ALU.mult, op1=ALU.subtract)

            dve.wait_ge(s_const, N_CONST)
            vec.tensor_copy(before[:, :], before_f32[:, :]).then_inc(s_constv, 1)
            vec.tensor_copy(iota[:, :], iota_i[:, :]).then_inc(s_constv, 1)
            vec.tensor_copy(row1[:, :], row_i[:, :]).then_inc(s_constv, 1)
            vec.tensor_copy(thr[:, :], thr_i[:, :]).then_inc(s_constv, 1)
            vec.tensor_copy(spare[:, :], spare_i[:, :]).then_inc(s_constv, 1)
            vec.memset(sel_sum[:, :, :], 0.0).then_inc(s_constv, 1)
            vec.memset(ge[:, :, 0:1], 1.0).then_inc(s_constv, 1)
            vec.memset(slots[:, :, :, :], 0.0).then_inc(s_constv, 1)

            def piece_lo(n):
                dve.wait_ge(w_split_hi, n + 1)
                low(piece_split(n, 1), piece_place(n), piece_split(n, 0), W_SCALE).then_inc(w_split_lo, 1)

            def split_x(b):
                dve.wait_ge(xt_hi, count(b, 1, 1))
                low(xt[:, 1, :, :], xt32[:, :, :], xt[:, 0, :, :]).then_inc(xt_lo, 1)

            piece_lo(Q0)
            split_x(0)
            for n in (K0, V0, V1):
                piece_lo(n)

            def maxima(b, j):
                dve.wait_ge(s_mm, count(b, EC, j + 1))
                past(dve, e_done, count(b, EC, j - 1))
                for h in range(2):
                    vec.tensor_reduce(s_max[:, j % 2, 2 * h:2 * h + 2], ps_s[h][:, :].rearrange("p (t k) -> p t k", t=TT),
                                      AX.X, ALU.max).then_inc(s_maxd, 1)
                dve.wait_ge(s_maxd, count(b, 2 * EC, 2 * j + 2))
                vec.tensor_scalar(s_neg[:, j % 2, :], s_max[:, j % 2, :], -SCORE, None, ALU.mult).then_inc(s_negd, 1)

            def row_scales(b, j):
                past(dve, p_done, count(b, EC, j - 1))
                dve.wait_ge(e_done, count(b, EC, j + 1))
                vec.reciprocal(s_rden[:, j % 2, :], s_den[:, j % 2, :]).then_inc(r_done, 1)

            def values_lo(b, g):
                half, t = g // 2, g % 2
                cs = slice(half * 512, (half + 1) * 512)
                dve.wait_ge(v_hi, count(b, 4, g + 1))
                low(v[:, 1, t, cs], ps_v[:, :], v[:, 0, t, cs], 1.0 / W_SCALE).then_inc(v_lo, 1)

            def turned_lo(b, j):
                for h in range(2):
                    dve.wait_ge(pt_hi, count(b, 2 * EC, 2 * j + h + 1))
                    low(pT[:, j % 2, 1, h, :], ps_t[h][:, :], pT[:, j % 2, 0, h, :], P_SCALE).then_inc(pt_lo, 1)

            def residual1(b, t):
                dve.wait_ge(wo_mm, count(b, TT, t + 1))
                if t == 0:
                    dve.wait_ge(xb_done, count(b, 1, 1))
                    past(dve, x1b_done, count(b, 1))
                    past(dve, ln2, count(b, 7))
                vec.scalar_tensor_tensor(out=z[:, t, :], in0=ps_x[:, :], scalar=1.0 / W_SCALE, in1=xr[:, t, :],
                                         op0=ALU.mult, op1=ALU.add).then_inc(ln1, 1)

            def moments(b, rows, stats, mv, ve, ln, before_it):
                for t in range(TT):
                    dve.wait_ge(ln, count(b, 7, t + 1))
                    vec.bn_stats(stats[:, t, :], rows[:, t, :]).then_inc(ln, 1)
                for t in range(TT):
                    wait_apart(dve, ln, count(b, 7, TT + t + 1), s_constv, N_CONSTV)
                    vec.bn_aggr(mv[:, t, :], stats[:, t, :]).then_inc(ln, 1)
                past(dve, before_it, count(b, 1))
                dve.wait_ge(ln, count(b, 7, 6))
                vec.tensor_scalar(ve[:, :], mv[:, :, 1], EPS, None, ALU.add).then_inc(ln, 1)

            def norm1(b):
                for t in range(TT):
                    if t == 0:
                        dve.wait_ge(ln1_rstd, count(b, 1, 1))
                        past(dve, x2_done, count(b, TT))
                    vec.tensor_scalar(x1[:, t, :], z[:, t, :], mv1[:, t, 0:1], rstd1[:, t:t + 1],
                                      ALU.subtract, ALU.mult).then_inc(x1_done, 1)

            def x1_lo(b, t):
                dve.wait_ge(x1t_hi, count(b, TT, t + 1))
                low(x1T[:, 1, :, t * P:(t + 1) * P], (ps_v, ps_x)[t][:, :].rearrange("p (c n) -> p c n", c=DC),
                    x1T[:, 0, :, t * P:(t + 1) * P]).then_inc(x1t_lo, 1)

            def split_ctx(b):
                dve.wait_ge(ct_hi, count(b, 1, 1))
                low(ct[:, 1, :, :], ct32[:, :, :], ct[:, 0, :, :]).then_inc(ct_lo, 1)

            def kv2_lo(b):
                dve.wait_ge(kv_hi, count(b, 2, 2))
                low(k2[:, 1, :], ps_v[0:XD, 0:S], k2[:, 0, :], 1.0 / W_SCALE).then_inc(kv_lo, 1)
                low(v2[:, 1].rearrange("p t n -> p (t n)"), ps_v[:, S:S + TT * XD],
                    v2[:, 0].rearrange("p t n -> p (t n)"), 1.0 / W_SCALE).then_inc(kv_lo, 1)

            def q2_low(b):
                dve.wait_ge(q2_hi, count(b, 1, 1))
                low(q2[:, 1, :], ps_x[0:XD, 0:S], q2[:, 0, :], 1.0 / W_SCALE).then_inc(q2_lo, 1)

            def masked(b):
                dve.wait_ge(s2_mm, count(b, 1, 1))
                dve.wait_ge(mask_done, count(b, 1, 1))
                past(dve, t2_mm, count(b, 1))
                vec.scalar_tensor_tensor(out=p2[:, :, :], in0=ps_x[:, :].rearrange("p (t k) -> p t k", t=TT), scalar=SCORE,
                                         in1=mask_add[:, :, :], op0=ALU.mult, op1=ALU.add).then_inc(s2_dve, 1)
                dve.wait_ge(s2_dve, count(b, 3, 1))
                vec.tensor_reduce(m2[:, :], p2[:, :, :], AX.X, ALU.max).then_inc(s2_dve, 1)
                dve.wait_ge(s2_dve, count(b, 3, 2))
                vec.tensor_scalar(n2[:, :], m2[:, :], -1.0, None, ALU.mult).then_inc(s2_dve, 1)

            def row_scales2(b):
                dve.wait_ge(e2_done, count(b, 1, 1))
                vec.reciprocal(rden2[:, :], den2[:, :]).then_inc(r2_done, 1)

            def turned2_lo(b):
                dve.wait_ge(t2_hi, count(b, 1, 1))
                low(p2T[:, 1].rearrange("p c n -> p (c n)"), ps_x[:, :], p2T[:, 0].rearrange("p c n -> p (c n)"),
                    P_SCALE).then_inc(t2_lo, 1)

            def o2_low(b):
                dve.wait_ge(o2_hi, count(b, 1, 1))
                low(o2[:, 1, :], ps_x[0:XD, 0:S], o2[:, 0, :], 1.0 / P_SCALE).then_inc(o2_lo, 1)

            def residual2(b, t):
                dve.wait_ge(out2_mm, count(b, TT, t + 1))
                if t == 0:
                    dve.wait_ge(x1b_done, count(b, 1, 1))
                vec.scalar_tensor_tensor(out=x1[:, t, :], in0=ps_x[:, :], scalar=1.0 / W_SCALE, in1=z[:, t, :],
                                         op0=ALU.mult, op1=ALU.add).then_inc(ln2, 1)

            def norm2(b):
                for t in range(TT):
                    if t == 0:
                        dve.wait_ge(ln2_rstd, count(b, 1, 1))
                        past(dve, x2t_mm, count(b, TT))
                        past(dve, st_x2, count(b, 32))
                    vec.tensor_scalar(x2[:, t, :], x1[:, t, :], mv2[:, t, 0:1], rstd2[:, t:t + 1],
                                      ALU.subtract, ALU.mult).then_inc(x2_done, 1)

            def step(b, n):
                past(dve, rt, count(b, RT, n))

            def gate_max(b):
                wait_apart(dve, gate_mm, count(b, 1, 1), s_constv, N_CONSTV)
                for t in range(TT):
                    vec.max(top_l[:, t, :], ps_gate[:, t, :]).then_inc(rt, 1)
                step(b, 2)
                vec.tensor_scalar(neg_l[:, :], top_l[:, :, 0], -1.0, None, ALU.mult).then_inc(rt, 1)

            def choose(b):
                by_row = lambda ap: ap.unsqueeze(2).to_broadcast([P, TT, NX])
                dve.wait_ge(rt_exp, count(b, 1, 1))
                vec.reciprocal(rden_l[:, :], den_l[:, :]).then_inc(rt, 1)
                step(b, 4)
                vec.tensor_tensor(pr[:, :, :], ex[:, :, :], by_row(rden_l[:, :]), ALU.mult).then_inc(rt, 1)
                wait_apart(dve, rt, count(b, RT, 5), s_constv, N_CONSTV)
                for t in range(TT):
                    vec.max(top_p[:, t, :], pr[:, t, :]).then_inc(rt, 1)
                wait_apart(dve, rt, count(b, RT, 7), s_constv, N_CONSTV)
                for t in range(TT):
                    vec.match_replace(left[:, t, :], top_p[:, t, :], pr[:, t, :], -1.0).then_inc(rt, 1)
                step(b, 9)
                vec.tensor_scalar(sel[:, :, :], left[:, :, :], -1.0, None, ALU.is_equal).then_inc(rt, 1)
                step(b, 10)
                vec.tensor_tensor(sel_sum[:, 1, :], sel_sum[:, 0, :], sel[:, 0, :], ALU.add).then_inc(rt, 1)
                vec.tensor_reduce(w_sum[:, :], top_p[:, :, :], AX.X, ALU.add).then_inc(rt, 1)
                step(b, 12)
                vec.reciprocal(w_rsum[:, :], w_sum[:, :]).then_inc(rt, 1)
                step(b, 13)
                vec.scalar_tensor_tensor(out=w32[:, :, :], in0=pr[:, :, :], scalar=G_SCALE, in1=by_row(w_rsum[:, :]),
                                         op0=ALU.mult, op1=ALU.mult).then_inc(rt, 1)
                step(b, 14)
                vec.tensor_copy(w_hi[:, :, :], w32[:, :, :]).then_inc(rt, 1)
                step(b, 15)
                vec.tensor_tensor(w_lo[:, :, :], w32[:, :, :], w_hi[:, :, :], ALU.subtract).then_inc(rt, 1)

            G = TT * NX

            def places(b):
                dve.wait_ge(pos_mm, count(b, 1, 1))
                vec.tensor_tensor(sel_sum[:, 0, :], sel_sum[:, 1, :], sel[:, 1, :], ALU.add).then_inc(rt, 1)
                vec.tensor_tensor(ge[:, :, 1:CC + 1], ps_pos[:, :].unsqueeze(2).to_broadcast([P, G, CC]),
                                  thr[:, :].unsqueeze(1).to_broadcast([P, G, CC]), ALU.is_ge).then_inc(rt, 1)
                step(b, 18)
                vec.tensor_reduce(n_ge[:, :], ge[:, :, 1:CC], AX.X, ALU.add).then_inc(rt, 1)
                step(b, 19)
                vec.scalar_tensor_tensor(out=pos_in[:, :], in0=n_ge[:, :], scalar=-float(P), in1=ps_pos[:, :],
                                         op0=ALU.mult, op1=ALU.add).then_inc(rt, 1)
                vec.tensor_tensor(in_chunk[:, :, :], ge[:, :, 0:CC], ge[:, :, 1:CC + 1], ALU.subtract).then_inc(rt, 1)

            def tell(b):
                by_choice = lambda ap: ap.rearrange("p t e -> p (t e)").unsqueeze(2).to_broadcast([P, G, CC])
                step(b, 21)
                vec.tensor_tensor(chosen[:, :, :], in_chunk[:, :, :], by_choice(sel[:, :, :]), ALU.mult).then_inc(rt, 1)
                step(b, 22)
                past(dve, slot_mm, count(b, 2))
                vec.tensor_scalar(said[:, :, 0, :], chosen[:, :, :], row1[:, 0:1], None, ALU.mult).then_inc(rt, 1)
                vec.tensor_tensor(said[:, :, 1, :].rearrange("p (t e) c -> p t e c", t=TT),
                                  chosen[:, :, :].rearrange("p (t e) c -> p t e c", t=TT),
                                  tile_no[:, :].unsqueeze(2).unsqueeze(3).to_broadcast([P, TT, NX, CC]), ALU.mult).then_inc(rt, 1)
                vec.tensor_tensor(said[:, :, 2, :], chosen[:, :, :], by_choice(w_hi[:, :, :]), ALU.mult).then_inc(rt, 1)
                vec.tensor_tensor(said[:, :, 3, :], chosen[:, :, :], by_choice(w_lo[:, :, :]), ALU.mult).then_inc(rt, 1)
                step(b, 24)
                vec.tensor_scalar(tile_no[:, :], tile_no[:, :], float(TT), None, ALU.add).then_inc(rt, 1)

            def slot_onehot(b, k, t):
                step(b, 20)
                past(dve, slot_mm, count(b, 2, k))
                vec.tensor_tensor(onehot[:, t, :, :], iota[:, :].unsqueeze(1).to_broadcast([P, HX, P]),
                                  pos_in[:, t * NX + k * HX:t * NX + (k + 1) * HX].unsqueeze(2).to_broadcast([P, HX, P]),
                                  ALU.is_equal).then_inc(oh_done, 1)

            def add_slots(b, k):
                dve.wait_ge(slot_mm, count(b, 2, k + 1))
                if isinstance(b, int) and b == 0 and k == 0:
                    dve.wait_ge(st_zero, 16)
                past(dve, slot_done, count(b, 2, k - 1))
                half = slots[:, k * HX:(k + 1) * HX, :, :].rearrange("p e a c -> p (e a c)")
                vec.tensor_tensor(half, half, ps_slot[:, :], ALU.add).then_inc(slot_done, 1)

            def tables(k):
                at = slice(k * HX, (k + 1) * HX)
                dve.wait_ge(slot_done, count(B - 1, 2, k + 1))
                vec.scalar_tensor_tensor(out=tok[:, at, :], in0=slots[:, at, 1, :], scalar=float(P), in1=slots[:, at, 0, :],
                                         op0=ALU.mult, op1=ALU.add).then_inc(table, 1)
                vec.tensor_scalar(empty[:, at, :], slots[:, at, 0, :], 0.0, None, ALU.is_equal).then_inc(table, 1)
                dve.wait_ge(table, count(k, 8, 2))
                vec.tensor_scalar(tok0[:, at, :], tok[:, at, :], -1.0, 0.0, ALU.add, ALU.max).then_inc(table, 1)
                dve.wait_ge(table, count(k, 8, 3))
                vec.tensor_tensor(tok[:, at, :], empty[:, at, :], spare[:, :].unsqueeze(1).to_broadcast([P, HX, CC]), ALU.mult)\
                   .then_inc(table, 1)
                vec.tensor_copy(idx_from[:, at, :], tok0[:, at, :]).then_inc(table, 1)
                dve.wait_ge(table, count(k, 8, 4))
                vec.tensor_tensor(idx_to[:, at, :], tok0[:, at, :], tok[:, at, :], ALU.add).then_inc(table, 1)
                vec.tensor_tensor(w_slot[:, at, :], slots[:, at, 2, :], slots[:, at, 3, :], ALU.add).then_inc(table, 1)
                dve.wait_ge(table, count(k, 8, 7))
                vec.tensor_scalar(w_slot[:, at, :], w_slot[:, at, :], 1.0 / (G_SCALE * W_SCALE), None, ALU.mult).then_inc(table, 1)

            def weights_lo(e, k, part, place, n, done):
                dve.wait_ge(ew_hi, count(e, 2, n))
                if n == 1:
                    past(dve, y_mm, count(e, CC, -CC))
                low(ew[:, k, 1, part], stage[:, place, part], ew[:, k, 0, part], W_SCALE).then_inc(done, 1)

            def gate_up_lo(e, k, place):
                weights_lo(e, k, slice(0, WGU), place, 1, ew_lo_gu)

            def down_lo(e, k, place):
                weights_lo(e, k, slice(WGU, NW), place, 2, ew_lo_dn)

            def work(r, head, tail, route, fill):
                b, t, u, f = r, r - 1, r - 2, r - 3
                pair = pairs(r, head, tail)

                def step(s, between=()):
                    pair(maxima, s - 2)
                    pair(turned_lo, s - 3)
                    for on, run in between:
                        if on:
                            run()
                    pair(row_scales, s - 2)

                if route:
                    masked(u)
                if head and not (isinstance(r, int) and r == 0):
                    split_x(b)
                step(0, [(route, lambda: row_scales2(u)), (fill, lambda: add_slots(f, 0)),
                         (isinstance(r, int) and r == B + 2, lambda: tables(0)),
                         (fill, lambda: slot_onehot(f, 1, 0))])
                if head:
                    values_lo(b, 0)
                if isinstance(r, int) and r == 0:
                    piece_lo(Q1)
                step(1, [(fill, lambda: slot_onehot(f, 1, 1))])
                if route:
                    turned2_lo(u)
                    o2_low(u)
                if head:
                    values_lo(b, 1)
                step(2, [(isinstance(r, int) and r == 0, lambda: piece_lo(K1))])
                if route:
                    residual2(u, 0)
                if fill:
                    add_slots(f, 1)
                if isinstance(r, int) and r == B + 2:
                    tables(1)
                if route:
                    residual2(u, 1)
                    moments(u, x1, stats2, mv2, ve2, ln2, ln2_rstd)
                step(3, [(route, lambda: norm2(u))])
                if head:
                    values_lo(b, 2)
                if isinstance(r, int) and r == B + 1:
                    down_lo(0, 0, 0)
                step(4)
                if isinstance(r, int) and r == 0:
                    piece_lo(O0)
                if tail:
                    residual1(t, 0)
                    split_ctx(t)
                    if isinstance(r, int) and r == B:
                        gate_up_lo(0, 0, 0)
                    residual1(t, 1)
                    moments(t, z, stats1, mv1, ve1, ln1, ln1_rstd)
                step(5, [(route, lambda: gate_max(u))])
                if tail:
                    norm1(t)
                if route:
                    choose(u)
                if isinstance(r, int) and r == 0:
                    piece_lo(O1)
                if head:
                    values_lo(b, 3)
                step(6, [(route, lambda: places(u))])
                if tail:
                    x1_lo(t, 0)
                if route:
                    tell(u)
                if tail:
                    x1_lo(t, 1)
                if isinstance(r, int) and r == 0:
                    piece_lo(X3)
                    piece_lo(XO)
                step(7, [(route, lambda: slot_onehot(u, 0, 0))])
                if tail:
                    kv2_lo(t)
                    q2_low(t)
                if route:
                    slot_onehot(u, 0, 1)

            dve.wait_ge(s_constv, N_CONSTV)
            rounds(dve, work)

            def tokens_lo(e):
                for c in range(CC):
                    dve.wait_ge(xg_hi, count(e, CC, c + 1))
                    low(xgT[:, 1, :, c * P:(c + 1) * P], ps_xg[c % 2][:, :].rearrange("p (d n) -> p d n", d=DC),
                        xgT[:, 0, :, c * P:(c + 1) * P]).then_inc(xg_lo, 1)

            def expert(e, k, ahead):
                if ahead:
                    gate_up_lo(e + 1, 1 - k, k)
                for f in range(FC):
                    n = FC * k + f
                    dve.wait_ge(u_mm, count(e, FC, f + 1))
                    dve.wait_ge(silu_done, count(e, FC, f + 1))
                    past(dve, h_lo, count(e, FC, f - 1))
                    vec.scalar_tensor_tensor(out=h32[:, n % 2, :], in0=ps_h[n % 2][1][:, :], scalar=1.0 / W_SCALE,
                                             in1=silu[:, n % 2, :], op0=ALU.mult, op1=ALU.mult).then_inc(h_f32, 1)
                    if f == 0:
                        past(dve, y_mm, count(e, CC))
                    dve.wait_ge(h_f32, count(e, FC, f + 1))
                    vec.tensor_copy(hT[:, 0, f, :], h32[:, n % 2, :]).then_inc(h_hi, 1)
                    dve.wait_ge(h_hi, count(e, FC, f + 1))
                    vec.tensor_tensor(hT[:, 1, f, :], h32[:, n % 2, :], hT[:, 0, f, :], ALU.subtract).then_inc(h_lo, 1)
                    if f == 0 and ahead:
                        down_lo(e + 1, 1 - k, k)
                if ahead:
                    tokens_lo(e + 1)

            tokens_lo(0)
            expert(0, 0, True)
            expert(1, 1, True)
            with dve.Fori(2, NX - 3, 2) as e:
                expert(e, 0, True)
                expert(e + 1, 1, True)
            expert(NX - 2, 0, True)
            expert(NX - 1, 1, False)

            LN = 2 * GT + 2
            for g in range(GROUPS):
                dve.wait_ge(ld_acc[g % HALF], 16 * (g // HALF + 1))
                for t in range(GT):
                    vec.bn_stats(stats3[:, g, t, :], rows3[:, g, t, :]).then_inc(ln3, 1)
                for t in range(GT):
                    dve.wait_ge(ln3, count(g, LN, t + 1))
                    vec.bn_aggr(mv3[:, g, t, :], stats3[:, g, t, :]).then_inc(ln3, 1)
                dve.wait_ge(ln3, count(g, LN, 2 * GT))
                vec.tensor_scalar(ve3[:, g, :], mv3[:, g, :, 1], EPS, None, ALU.add).then_inc(ln3, 1)
                vec.tensor_scalar(neg_mean3[:, g, :], mv3[:, g, :, 0], -1.0, None, ALU.mult).then_inc(ln3, 1)

        @block.gpsimd
        def _(pool):
            gp = nc.gpsimd
            gp.memset(ident[:, :], 0.0).then_inc(s_const, 1)
            gp.memset(before_f32[:, :], 1.0).then_inc(s_const, 1)
            gp.memset(ones[:, :], 1.0).then_inc(s_const, 1)
            gp.memset(neg_half[:, :], -0.5).then_inc(s_const, 1)
            gp.iota(iota_i[:, :], [[1, P]], base=0, channel_multiplier=0).then_inc(s_const, 1)
            gp.iota(row_i[:, :], [[0, 1]], base=1, channel_multiplier=1).then_inc(s_const, 1)
            gp.iota(thr_i[:, :], [[P, CC]], base=P, channel_multiplier=0).then_inc(s_const, 1)
            gp.iota(spare_i[:, :], [[P, CC]], base=N, channel_multiplier=1).then_inc(s_const, 1)
            gp.memset(tile_no[:, 0:1], 0.0).then_inc(s_const, 1)
            gp.memset(tile_no[:, 1:2], 1.0).then_inc(s_const, 1)
            pool.wait_ge(s_const, 10)
            gp.affine_select(out=ident[:, :], in_=ident[:, :], compare_op=ALU.not_equal, fill=1.0, base=0,
                             pattern=[[-1, P]], channel_multiplier=1).then_inc(s_const, 1)
            gp.affine_select(out=before_f32[:, :], in_=before_f32[:, :], compare_op=ALU.is_ge, fill=0.0, base=-1,
                             pattern=[[1, P]], channel_multiplier=-1).then_inc(s_const, 1)

            def qk_low(b, j):
                past(pool, s_mm, count(b, EC, j - 1))
                pool.wait_ge(qk_hi, count(b, EC, j + 1))
                gp.tensor_tensor(qk[:, j % 2, 1, :], qk32[:, j % 2, :], qk[:, j % 2, 0, :], ALU.subtract).then_inc(qk_lo, 1)

            def normalise(b, j):
                pool.wait_ge(r_done, count(b, EC, j + 1))
                rows = probs[:, j % 2].rearrange("p h t k -> p (h t) k")
                gp.tensor_tensor(rows, rows, s_rden[:, j % 2, :].unsqueeze(2).to_broadcast([P, 4, S]), ALU.mult)\
                  .then_inc(p_done, 1)

            def heads_lo(b, j):
                pool.wait_ge(o_hi, count(b, EC, j + 1))
                gp.tensor_tensor(o[:, 1, j, :], o32[:, j % 2, :], o[:, 0, j, :], ALU.subtract).then_inc(o_lo, 1)

            def add_bias(b):
                pool.wait_ge(ld_row, count(b, 16, 16))
                gp.tensor_tensor(xr[:, :, :], xr[:, :, :], bo_row[:, :].unsqueeze(1).to_broadcast([P, TT, D]), ALU.add)\
                  .then_inc(xb_done, 1)

            def mask_rows(b):
                wait_apart(pool, ld_mask, count(b, 16, 16), s_const, N_CONST)
                gp.tensor_scalar(mask_add[:, :, :], mask_i[:, :, :], -1.0e9, None, ALU.mult).then_inc(mask_done, 1)

            def rstd(b, ln, dst, ve, done, read):
                pool.wait_ge(ln, count(b, 7, 7))
                past(pool, read, count(b, TT))
                gp.tensor_tensor(dst[:, :], ve[:, :], neg_half[:, 0:TT], ALU.pow).then_inc(done, 1)

            def add_bias2(b):
                pool.wait_ge(x1_done, count(b, TT, TT))
                gp.tensor_tensor(z[:, :, :], x1[:, :, :], xbo_row[:, :].unsqueeze(1).to_broadcast([P, TT, D]), ALU.add)\
                  .then_inc(x1b_done, 1)

            def normalise2(b):
                pool.wait_ge(r2_done, count(b, 1, 1))
                gp.tensor_tensor(p2[:, :, :], p2[:, :, :], rden2[:, :].unsqueeze(2).to_broadcast([P, TT, S]), ALU.mult)\
                  .then_inc(p2_done, 1)

            def work(r, head, tail, route, fill):
                b, t, u = r, r - 1, r - 2
                pair = pairs(r, head, tail)

                def step(s):
                    pair(normalise, s - 2)
                    if s != 4:
                        pair(heads_lo, s - 4)
                    if head:
                        qk_low(b, s)

                if route:
                    normalise2(u)
                step(0)
                step(1)
                if isinstance(r, int) and r == 1:
                    pool.wait_ge(s_constv, N_CONSTV)
                    pool.dma_start(acc_rows[N:N + CAP, :].rearrange("(c p) n -> p c n", p=P),
                                   slots[:, :, :, :].rearrange("p e a c -> p (e a c)").unsqueeze(1)
                                   .to_broadcast([P, CC, D])).then_inc(st_zero, 16)
                    pool.wait_ge(ld_small, 48)
                if tail:
                    add_bias(t)
                step(2)
                if route:
                    rstd(u, ln2, rstd2, ve2, ln2_rstd, x2_done)
                step(3)
                step(4)
                pair(heads_lo, 0)
                if tail:
                    rstd(t, ln1, rstd1, ve1, ln1_rstd, x1_done)
                step(5)
                if tail:
                    add_bias2(t)
                step(6)
                if tail:
                    mask_rows(t)
                step(7)

            rounds(pool, work)

            def columns(e, k):
                at = bass.ds(e, 1)
                for dst, src in ((cur_from, idx_from), (cur_to, idx_to), (cur_w, w_slot)):
                    ins = gp.tensor_copy(dst[:, k, :], src[:, at, :].rearrange("p a c -> p (a c)"))
                    ins.then_inc(cur_done, 1)

            def gather(e, k):
                wait_apart(pool, cur_done, count(e, 3, 3), s_const, N_CONST)
                for c in range(CC):
                    gp.indirect_dma_start(xg[:, k, c, :], None, x2_rows,
                                          bass.IndirectOffsetOnAxis(ap=cur_from[:, k, c:c + 1], axis=0)).then_inc(ld_xg[k], 16)

            def scatter(e, k):
                for c in range(CC):
                    wait_apart(pool, y_done, count(e, CC, c + 1), s_const, N_CONST)
                    gp.indirect_dma_start(acc_rows, bass.IndirectOffsetOnAxis(ap=cur_to[:, k, c:c + 1], axis=0),
                                          y[:, k, c, :], None, compute_op=ALU.add).then_inc(st_y, 16)

            def expert(e, k, ahead):
                past(pool, st_y, count(e, 64))
                if ahead:
                    past(pool, y_done, count(e, CC))
                    past(pool, xg_mm, count(e, CC))
                    columns(e + 1, 1 - k)
                    gather(e + 1, 1 - k)
                scatter(e, k)

            pool.wait_ge(table, 8)
            columns(0, 0)
            pool.wait_ge(st_x2, B * 32)
            pool.wait_ge(st_zero, 16)
            pool.wait_ge(pt_lo, B * 2 * EC)
            pool.wait_ge(pv_mm, B * EC)
            gather(0, 0)
            pool.wait_ge(table, 16)
            expert(0, 0, True)
            expert(1, 1, True)
            with pool.Fori(2, NX - 3, 2) as e:
                expert(e, 0, True)
                expert(e + 1, 1, True)
            expert(NX - 2, 0, True)
            expert(NX - 1, 1, False)

            for g in range(GROUPS):
                pool.wait_ge(ln3, (g + 1) * (2 * GT + 2))
                gp.tensor_tensor(rstd3[:, g, :], ve3[:, g, :], neg_half[:, :], ALU.pow).then_inc(ln3_rstd, 1)
                pool.wait_ge(ln3_rstd, 2 * g + 1)
                gp.tensor_tensor(shift3[:, g, :], neg_mean3[:, g, :], rstd3[:, g, :], ALU.mult).then_inc(ln3_rstd, 1)


INS = ["xT", "x_rows", "ctxT", "mask", "wqT", "wkT", "wvT", "woT", "bq", "bk", "bv", "bo",
       "x_wv", "x_wk", "x_wq", "x_wo", "x_bo", "gateT", "wguT", "wdnT"]


def kernel(x, ctx_1024, mask_BxSxS2_ik1, L0_attn_Wq, L0_attn_bq, L0_attn_Wk, L0_attn_bk, L0_attn_Wv, L0_attn_bv,
           L0_attn_Wo, L0_attn_bo, L0_xattn_Wv, L0_xattn_Wk, L0_xattn_Wq, L0_xattn_Wo, L0_xattn_bo,
           L0_ffn_gate_weight, L0_ffn_gate_up_proj, L0_ffn_down_proj):
    import numpy as np
    import concourse.bacc as bacc
    from concourse.bass_utils import run_bass_kernel_spmd

    a = np.asarray
    rows = lambda m: a(m).reshape(N, -1)
    cols = lambda m: a(m).reshape(EC, P).T
    given = {
        "xT": rows(x).T, "x_rows": rows(x), "ctxT": rows(ctx_1024).T, "mask": rows(mask_BxSxS2_ik1),
        "wqT": a(L0_attn_Wq).T, "wkT": a(L0_attn_Wk).T, "wvT": a(L0_attn_Wv).T, "woT": a(L0_attn_Wo).T,
        "bq": cols(L0_attn_bq), "bk": cols(L0_attn_bk), "bv": cols(L0_attn_bv), "bo": a(L0_attn_bo),
        "x_wv": a(L0_xattn_Wv), "x_wk": a(L0_xattn_Wk), "x_wq": a(L0_xattn_Wq), "x_wo": a(L0_xattn_Wo),
        "x_bo": a(L0_xattn_bo), "gateT": a(L0_ffn_gate_weight).T,
        "wguT": a(L0_ffn_gate_up_proj).transpose(0, 2, 1), "wdnT": a(L0_ffn_down_proj).transpose(0, 2, 1),
    }
    given = {k: np.ascontiguousarray(m) for k, m in given.items()}
    nc = bacc.Bacc("TRN2", target_bir_lowering=False, num_devices=1)
    args = [nc.dram_tensor(k, given[k].shape, mybir.dt.from_np(given[k].dtype), kind="ExternalInput").ap() for k in INS]
    out = nc.dram_tensor("out", [N, D], F32, kind="ExternalOutput").ap()
    build(nc, *args, out)
    r = run_bass_kernel_spmd(nc, [given], core_ids=[0])
    return r.results[0]["out"].reshape(B, S, D)
```

```python
import concourse.bass as bass
from concourse import mybir
from contextlib import ExitStack


F32 = mybir.dt.float32
F16 = mybir.dt.float16
I32 = mybir.dt.int32
ALU = mybir.AluOpType
ACT = mybir.ActivationFunctionType
AX = mybir.AxisListType

P = 128
B, S, D = 16, 256, 512
N = B * S
H, DK = 16, 64
E = H * DK
DC = D // P
EC = E // P
TT = S // P
NX, TOP, CAP, F = 32, 8, 512, 384
FC = F // P
CC = CAP // P
XD = 64
WGU = DC * 2 * F
WDN = FC * D
EPS = 1e-5
SCORE = 1.0 / 8.0
W_SCALE = 256.0
P_SCALE = 4096.0
G_SCALE = 256.0
PARTS = ((0, 0), (0, 1), (1, 0))


def count(b, per, c=0):
    return b * per + c


def past(eng, sem, value):
    if isinstance(value, int) and value <= 0:
        return
    eng.wait_ge(sem, value)


def wait_apart(eng, sem, value, held, times):
    if not isinstance(value, int):
        value = eng.snap(eng.to_reg(value))
    eng.wait_ge(held, times)
    past(eng, sem, value)


def build(nc, xT, x_rows, ctxT, mask, wqT, wkT, wvT, woT, bq, bk, bv, bo,
          x_wv, x_wk, x_wq, x_wo, x_bo, gateT, wguT, wdnT, out):
    ctx = ExitStack()
    with ctx:
        def sb(name, shape, dt=F32):
            return ctx.enter_context(nc.sbuf_tensor(name, shape, dt))

        def sem(name):
            return ctx.enter_context(nc.semaphore(name))

        x2_rows = nc.dram_tensor("x2_rows", [N, D], F32, kind="Internal").ap()
        acc_rows = nc.dram_tensor("acc_rows", [N + CAP, D], F32, kind="Internal").ap()

        XQ, XK, XV = slice(0, XD), slice(XD, 3 * XD), slice(3 * XD, 4 * XD)
        XG = slice(4 * XD, 4 * XD + NX)
        arena_wo = sb("arena_wo", [P, 3 * 2 * DC * E + 2 * EC * D], F16)
        arena_w = arena_wo[:, 0:3 * 2 * DC * E]
        arena_o = arena_wo[:, 3 * 2 * DC * E:]
        wqkv = arena_w[:, :].rearrange("p (w s c n) -> p w s c n", w=3, s=2, c=DC)
        wo = arena_o[:, :].rearrange("p (s c n) -> p s c n", s=2, c=EC)
        wx = sb("wx", [P, 2, DC, 4 * XD + NX], F16)
        wxo = sb("wxo", [P, 2, D], F16)
        stage = sb("stage", [P, 2, WGU + WDN])
        bqkv = sb("bqkv", [P, 3, EC])
        bo_row = sb("bo_row", [P, D])
        xbo_row = sb("xbo_row", [P, D])

        ident = sb("ident", [P, P])
        before = sb("before", [P, P], F16)
        ones = sb("ones", [P, P], F16)
        iota = sb("iota", [P, P])
        row_i = sb("row_i", [P, 1], I32)
        row1 = sb("row1", [P, 1])
        thr_i = sb("thr_i", [P, CC], I32)
        thr = sb("thr", [P, CC])
        spare_i = sb("spare_i", [P, CC], I32)
        spare = sb("spare", [P, CC])
        neg_half = sb("neg_half", [P, 4])

        xt32 = sb("xt32", [P, DC, S])
        xt = sb("xt", [P, 2, DC, S], F16)
        qk32 = sb("qk32", [P, 2, 2 * S])
        qk = sb("qk", [P, 2, 2, 2 * S], F16)
        arena_v = sb("arena_v", [P, 2 * TT * E], F16)
        v = arena_v[:, :].rearrange("p (s t e) -> p s t e", s=2, t=TT)
        arena_p = sb("arena_p", [P, 4096])
        probs = arena_p[:, 0:2048].rearrange("p (b h q k) -> p b h q k", b=2, h=2, q=TT)
        pT = arena_p[:, 2048:4096].bitcast(F16).rearrange("p (b s h n) -> p b s h n", b=2, s=2, h=2)
        s_max = sb("s_max", [P, 2, 4])
        s_neg = sb("s_neg", [P, 2, 4])
        s_den = sb("s_den", [P, 2, 4])
        s_rden = sb("s_rden", [P, 2, 4])
        o32 = sb("o32", [P, 2, S])
        arena_a = sb("arena_a", [P, 2 * EC * S], F16)
        o = arena_a[:, :].rearrange("p (s j n) -> p s j n", s=2, j=EC)

        xr = sb("xr", [P, TT, D])
        z = sb("z", [P, TT, D])
        before_f32 = z[:, 0, 0:P]
        iota_i = z[:, 0, P:2 * P].bitcast(I32)
        x1 = sb("x1", [P, TT, D])
        x2 = sb("x2", [P, TT, D])
        stats1 = sb("stats1", [P, TT, 6])
        mv1 = sb("mv1", [P, TT, 2])
        ve1 = sb("ve1", [P, TT])
        rstd1 = sb("rstd1", [P, TT])
        stats2 = sb("stats2", [P, TT, 6])
        mv2 = sb("mv2", [P, TT, 2])
        ve2 = sb("ve2", [P, TT])
        rstd2 = sb("rstd2", [P, TT])

        ct32 = stage[:, 1, 0:1024].rearrange("p (c n) -> p c n", c=DC)
        ct = sb("ct", [P, 2, DC, S], F16)
        mask_i = sb("mask_i", [P, TT, S], I32)
        mask_add = stage[:, 1, 4096:4608].rearrange("p (t n) -> p t n", t=TT)
        x1T = sb("x1T", [P, 2, DC, S], F16)
        q2 = sb("q2", [P, 2, S], F16)
        k2 = sb("k2", [P, 2, S], F16)
        v2 = sb("v2", [P, 2, TT, XD], F16)
        p2 = sb("p2", [P, TT, S])
        m2 = sb("m2", [P, TT])
        n2 = sb("n2", [P, TT])
        den2 = sb("den2", [P, TT])
        rden2 = sb("rden2", [P, TT])
        p2T = sb("p2T", [P, 2, 2, S], F16)
        o2 = sb("o2", [P, 2, S], F16)

        x2T = stage[:, 1, 1024:2048].bitcast(F16).rearrange("p (s c n) -> p s c n", s=2, c=DC)
        top_l = sb("top_l", [P, TT, 8])
        neg_l = sb("neg_l", [P, TT])
        ex = sb("ex", [P, TT, NX])
        den_l = sb("den_l", [P, TT])
        rden_l = sb("rden_l", [P, TT])
        pr = sb("pr", [P, TT, NX])
        top_p = sb("top_p", [P, TT, 8])
        left = sb("left", [P, TT, NX])
        sel = sb("sel", [P, TT, NX], F16)
        sel_sum = sb("sel_sum", [P, 2, NX], F16)
        w_sum = sb("w_sum", [P, TT])
        w_rsum = sb("w_rsum", [P, TT])
        w32 = sb("w32", [P, TT, NX])
        w_hi = sb("w_hi", [P, TT, NX], F16)
        w_lo = sb("w_lo", [P, TT, NX], F16)
        ge = sb("ge", [P, TT * NX, CC + 1])
        n_ge = sb("n_ge", [P, TT * NX])
        pos_in = sb("pos_in", [P, TT * NX])
        in_chunk = sb("in_chunk", [P, TT * NX, CC])
        chosen = sb("chosen", [P, TT * NX, CC])
        tile_no = sb("tile_no", [P, TT])
        said = sb("said", [P, TT * NX, 4, CC], F16)
        onehot = stage[:, 1, 2048:4096].bitcast(F16).rearrange("p (t e n) -> p t e n", t=TT, e=NX // 2)
        slots = sb("slots", [P, NX, 4, CC])
        tok, tok0, empty = in_chunk[:, 0:NX, :], in_chunk[:, NX:2 * NX, :], chosen[:, 0:NX, :]
        idx_from = sb("idx_from", [P, NX, CC], I32)
        idx_to = sb("idx_to", [P, NX, CC], I32)
        w_slot = sb("w_slot", [P, NX, CC])
        cur_from = sb("cur_from", [P, 2, CC], I32)
        cur_to = sb("cur_to", [P, 2, CC], I32)
        cur_w = sb("cur_w", [P, 2, CC])
        GT = 4
        GROUPS = N // (GT * P)
        per3 = xr[:, :, :].rearrange("p t n -> p (t n)")
        stats3 = per3[:, 0:6 * GROUPS * GT].rearrange("p (g t k) -> p g t k", g=GROUPS, t=GT)
        mv3 = per3[:, 6 * GROUPS * GT:8 * GROUPS * GT].rearrange("p (g t k) -> p g t k", g=GROUPS, t=GT)
        ve3, neg_mean3, rstd3, shift3 = (per3[:, k * GROUPS * GT:(k + 1) * GROUPS * GT]
                                         .rearrange("p (g t) -> p g t", g=GROUPS) for k in range(8, 12))

        NW = WGU + WDN
        ew = arena_w[:, 0:4 * NW].rearrange("p (b s n) -> p b s n", b=2, s=2)
        ew_gu = ew[:, :, :, 0:WGU].rearrange("p b s (c f) -> p b s c f", c=DC)
        ew_dn = ew[:, :, :, WGU:NW].rearrange("p b s (c n) -> p b s c n", c=FC)
        hT = arena_w[:, 4 * NW:4 * NW + 2 * FC * CAP].rearrange("p (s f n) -> p s f n", s=2, f=FC)
        y = arena_o[:, :].bitcast(F32).rearrange("p (b c n) -> p b c n", b=2, c=CC)
        xg = arena_p[:, :].rearrange("p (b c n) -> p b c n", b=2, c=CC)
        xgT = arena_v[:, :].rearrange("p (s c n) -> p s c n", s=2, c=DC)
        act32 = arena_a[:, :].bitcast(F32).rearrange("p (k b n) -> p k b n", k=2, b=2)
        silu, h32 = act32[:, 0], act32[:, 1]
        rows3 = arena_wo[:, :].bitcast(F32).rearrange("p (g t n) -> p g t n", g=GROUPS, t=GT)

        bank = [ctx.enter_context(nc.psum_tensor(f"bank{i}", [P, 512], F32)) for i in range(8)]
        ps_qk = bank[0]
        ps_v = bank[1]
        ps_s = bank[2:4]
        ps_t = bank[4:6]
        ps_o = bank[6]
        ps_x = bank[7]
        ps_gate = bank[7][:, 0:TT * NX].rearrange("p (t e) -> p t e", t=TT)
        ps_pos = bank[7][:, 0:TT * NX]
        ps_slot = bank[1][:, 0:256]
        ps_h = (bank[0:2], bank[2:4])
        ps_xg = bank[4:6]
        ps_y = bank[6:8]

        HX = NX // 2
        LAST = (slice(0, 2), slice(2, HX), slice(HX, NX))
        ps_last = (ps_slot, ps_slot, bank[6][:, 0:256])
        ps_warm = bank[3]
        WARM_START = 16
        WARM_ROUTE = (12, 8, 3, 3, 8)
        WARM = (10, 6, 2)
        FILLS = B * 2 + 1
        EARLIER = (B - 1) * 2

        s_const = sem("s_const")
        s_constv = sem("s_constv")
        ld_w = [sem("ld_w0"), sem("ld_w1")]
        ld_setup = [sem(f"ld_setup{k}") for k in range(4)]
        ld_bias, ld_small = sem("ld_bias"), sem("ld_small")
        w_split_hi = sem("w_split_hi")
        w_split_lo = sem("w_split_lo")
        ld_x, ld_row, ld_ctx, ld_mask = sem("ld_x"), sem("ld_row"), sem("ld_ctx"), sem("ld_mask")
        xt_hi, xt_lo = sem("xt_hi"), sem("xt_lo")
        qk_mm, qk_hi, qk_lo = sem("qk_mm"), sem("qk_hi"), sem("qk_lo")
        s_mm, s_maxd, s_negd = sem("s_mm"), sem("s_maxd"), sem("s_negd")
        e_done, r_done, p_done = sem("e_done"), sem("r_done"), sem("p_done")
        t_mm, pt_hi, pt_lo = sem("t_mm"), sem("pt_hi"), sem("pt_lo")
        v_mm, v_hi, v_lo = sem("v_mm"), sem("v_hi"), sem("v_lo")
        pv_mm, o_hi, o_lo = sem("pv_mm"), sem("o_hi"), sem("o_lo")
        wo_mm, xb_done = sem("wo_mm"), sem("xb_done")
        ln1, ln1_rstd, x1_done, x1b_done = sem("ln1"), sem("ln1_rstd"), sem("x1_done"), sem("x1b_done")
        x1t_mm, x1t_hi, x1t_lo = sem("x1t_mm"), sem("x1t_hi"), sem("x1t_lo")
        ct_hi, ct_lo = sem("ct_hi"), sem("ct_lo")
        kv_mm, kv_hi, kv_lo = sem("kv_mm"), sem("kv_hi"), sem("kv_lo")
        q2_mm, q2_hi, q2_lo = sem("q2_mm"), sem("q2_hi"), sem("q2_lo")
        s2_mm, mask_done, s2_dve = sem("s2_mm"), sem("mask_done"), sem("s2_dve")
        e2_done, r2_done, p2_done = sem("e2_done"), sem("r2_done"), sem("p2_done")
        t2_mm, t2_hi, t2_lo = sem("t2_mm"), sem("t2_hi"), sem("t2_lo")
        pv2_mm, o2_hi, o2_lo = sem("pv2_mm"), sem("o2_hi"), sem("o2_lo")
        out2_mm = sem("out2_mm")
        ln2, ln2_rstd, x2_done = sem("ln2"), sem("ln2_rstd"), sem("x2_done")
        st_x2 = sem("st_x2")
        x2t_mm, x2t_hi, x2t_lo = sem("x2t_mm"), sem("x2t_hi"), sem("x2t_lo")
        gate_mm, rt_exp, rt = sem("gate_mm"), sem("rt_exp"), sem("rt")
        pos_mm, oh_done, slot_mm, slot_done = sem("pos_mm"), sem("oh_done"), sem("slot_mm"), sem("slot_done")
        warm = sem("warm")
        table = sem("table")
        from_done, cur_done = sem("from_done"), sem("cur_done")
        ld_xg = [sem("ld_xg0"), sem("ld_xg1")]
        xg_mm, xg_hi, xg_lo = sem("xg_mm"), sem("xg_hi"), sem("xg_lo")
        ew_hi, ew_lo_gu, ew_lo_dn = sem("ew_hi"), sem("ew_lo_gu"), sem("ew_lo_dn")
        g_mm, u_mm, silu_done = sem("g_mm"), sem("u_mm"), sem("silu_done")
        h_f32, h_hi, h_lo = sem("h_f32"), sem("h_hi"), sem("h_lo")
        y_mm, y_done = sem("y_mm"), sem("y_done")
        st_y = sem("st_y")
        st_zero = sem("st_zero")
        HALF = GROUPS // 2
        ld_acc = [sem(f"ld_acc{k}") for k in range(HALF)]
        ln3, ln3_rstd, out_done = sem("ln3"), sem("ln3_rstd"), sem("out_done")
        st_out = sem("st_out")

        RT = 27
        N_CONST, N_CONSTV = 12, 8

        Q0, K0, V0, Q1, K1, V1, Q2, K2, O0, O1, X3, XO = range(12)
        SETUP = 12
        EH, EQ = E // 2, E // 4
        PIECES = {Q0: (0, 0, EQ), Q1: (0, EQ, EQ), Q2: (0, EH, EH), K0: (1, 0, EQ), K1: (1, EQ, EQ), K2: (1, EH, EH),
                  V0: (2, 0, EH), V1: (2, EH, EH)}

        def piece_place(n):
            at = stage[:, :, :].rearrange("p k n -> p (k n)")[:, n % 4 * DC * EH:(n % 4 + 1) * DC * EH]
            if n == XO:
                return at[:, 0:D].unsqueeze(1)
            width = 4 * XD + NX if n == X3 else PIECES[n][2] if n in PIECES else D
            return at[:, 0:DC * width].rearrange("p (c n) -> p c n", c=DC)

        def piece_split(n, part):
            if n in (O0, O1):
                return wo[:, part, (n - O0) * DC:(n - O0 + 1) * DC, :]
            if n == X3:
                return wx[:, part]
            if n == XO:
                return wxo[:, part, :].unsqueeze(1)
            w, at, width = PIECES[n]
            return wqkv[:, w, part, :, at:at + width]

        def piece_loaded(n):
            return 16 * (n // 4 + {X3: 5, XO: 2}.get(n, 1))

        def rounds(eng, work):
            work(0, True, False, False, False)
            work(1, True, True, False, False)
            work(2, True, True, True, False)
            work(3, True, True, True, True)
            with eng.Fori(4, B) as r:
                work(r, True, True, True, True)
            work(B, False, True, True, True)
            work(B + 1, False, False, True, True)
            work(B + 2, False, False, False, True)

        def last_tail(r):
            return isinstance(r, int) and r == B

        def wo_bank(t, last):
            return ps_s[t] if last else ps_x

        def x1_bank(t, last):
            return ps_s[t] if last else (ps_v, ps_x)[t]

        def pairs(b, head, tail):
            def call(stage_of, j):
                if j >= 0 and head:
                    stage_of(b, j)
                elif j < 0 and tail:
                    stage_of(b - 1, j + EC)
            return call

        def cols(r):
            return bass.ds(r * S, S)

        def rows_of(ap, b):
            return ap[bass.ds(b * S, S), :].rearrange("(t p) n -> p t n", p=P)

        block = ctx.enter_context(nc.Block())

        @block.sync
        def _(sp):
            def piece(n, src):
                if n >= 4:
                    sp.wait_ge(w_split_hi, n - 3)
                    sp.wait_ge(w_split_lo, n - 3)
                for dst, one in src:
                    sp.dma_start(dst, one).then_inc(ld_setup[n % 4], 16)

            def columns(n):
                w, at, width = PIECES[n]
                piece(n, [(piece_place(n), (wqT, wkT, wvT)[w][:, at:at + width].rearrange("(c p) n -> p c n", p=P))])

            def o_rows(n):
                half = woT[(n - O0) * EH:(n - O0 + 1) * EH, :]
                piece(n, [(piece_place(n), half.rearrange("(c p) n -> p c n", p=P))])

            columns(Q0)
            sp.dma_start(xt32[:, :, :], xT[:, 0:S].rearrange("(c p) n -> p c n", p=P)).then_inc(ld_x, 16)
            columns(K0)
            for k, src in enumerate((bq, bk, bv)):
                sp.dma_start(bqkv[:, k, :], src).then_inc(ld_bias, 16)
            for n in (V0, Q1, K1, V1, Q2, K2):
                columns(n)
            o_rows(O0)
            o_rows(O1)
            sp.dma_start(bo_row[:, :], bo.partition_broadcast(P)).then_inc(ld_small, 16)
            sp.dma_start(xbo_row[:, :], x_bo.partition_broadcast(P)).then_inc(ld_small, 16)
            piece(X3, [(piece_place(X3)[:, :, k * XD:(k + 1) * XD], w.rearrange("(c p) n -> p c n", p=P))
                       for k, w in enumerate((x_wq, x_wk, x_wk, x_wv))]
                  + [(piece_place(X3)[:, :, XG], gateT.rearrange("(c p) n -> p c n", p=P))])
            piece(XO, [(piece_place(XO)[h * XD:(h + 1) * XD], x_wo.unsqueeze(1)) for h in range(2)])

            def load_expert(e, place):
                sp.dma_start(stage[:, place, 0:WGU].rearrange("p (c f) -> p c f", c=DC),
                             wguT[e].rearrange("(c p) f -> p c f", p=P)).then_inc(ld_w[place], 16)
                sp.dma_start(stage[:, place, WGU:NW].rearrange("p (c n) -> p c n", c=FC),
                             wdnT[e].rearrange("(c p) n -> p c n", p=P)).then_inc(ld_w[place], 16)

            def work(r, head, tail, route, fill):
                if head and not (isinstance(r, int) and r == 0):
                    sp.wait_ge(xt_hi, count(r, 1))
                    sp.wait_ge(xt_lo, count(r, 1))
                    sp.dma_start(xt32[:, :, :], xT[:, cols(r)].rearrange("(c p) n -> p c n", p=P)).then_inc(ld_x, 16)
                if tail:
                    t = r - 1
                    if isinstance(r, int) and r == 1:
                        sp.dma_start(xr[:, :, :], rows_of(x_rows, t)).then_inc(ld_row, 16)
                        sp.wait_ge(w_split_hi, SETUP)
                        sp.wait_ge(w_split_lo, SETUP)
                    past(sp, ct_hi, count(t, 1))
                    past(sp, ct_lo, count(t, 1))
                    sp.dma_start(ct32[:, :, :], ctxT[:, cols(t)].rearrange("(c p) n -> p c n", p=P)).then_inc(ld_ctx, 16)
                    past(sp, mask_done, count(t, 1))
                    sp.dma_start(mask_i[:, :, :], rows_of(mask, t)).then_inc(ld_mask, 16)
                    if not (isinstance(r, int) and r == 1):
                        past(sp, ln1, count(t, 7))
                        sp.dma_start(xr[:, :, :], rows_of(x_rows, t)).then_inc(ld_row, 16)
                if route:
                    t = r - 2
                    sp.wait_ge(x2_done, count(t, TT, TT))
                    sp.dma_start(rows_of(x2_rows, t), x2[:, :, :]).then_inc(st_x2, 16)
                    sp.dma_start(rows_of(acc_rows, t), x2[:, :, :]).then_inc(st_x2, 16)
                if isinstance(r, int) and r == 1:
                    load_expert(0, 0)
                if isinstance(r, int) and r == B:
                    sp.wait_ge(ew_lo_gu, 1)
                    sp.wait_ge(ew_lo_dn, 1)
                    load_expert(1, 0)

            rounds(sp, work)
            sp.wait_ge(slot_mm, FILLS)
            sp.wait_ge(ld_xg[0], 64)
            load_expert(2, 1)

            def next_but_one(e, place):
                sp.wait_ge(ew_lo_gu, count(e, 1, 1))
                sp.wait_ge(ew_lo_dn, count(e, 1, 1))
                load_expert(e + 2, place)

            with sp.Fori(1, NX - 4, 2) as e:
                next_but_one(e, 0)
                next_but_one(e + 1, 1)
            next_but_one(NX - 3, 0)

            sp.wait_ge(st_y, NX * 64)
            sp.wait_ge(y_done, NX * CC)

            def group_rows(ap, g):
                return ap[bass.ds(g * GT * P, GT * P), :].rearrange("(t p) n -> p t n", p=P)

            for g in range(GROUPS):
                if g >= HALF:
                    sp.wait_ge(ld_acc[g % HALF], 16)
                sp.dma_start(rows3[:, g], group_rows(acc_rows, g)).then_inc(ld_acc[g % HALF], 16)
            for g in range(GROUPS):
                sp.wait_ge(out_done, (g + 1) * GT)
                sp.dma_start(group_rows(out, g), rows3[:, g]).then_inc(st_out, 16)
            sp.wait_ge(st_out, GROUPS * 16)

        @block.tensor
        def _(pe):
            def split_mm(out_ap, lhs, rhs, chunks):
                for n, (a, c) in enumerate(PARTS):
                    for i in range(chunks):
                        mm = pe.matmul(out_ap, lhs(a, i), rhs(c, i),
                                       start=(n == 0 and i == 0), stop=(n == 2 and i == chunks - 1))
                return mm

            def half_mm(bank, lhs, rhs, chunks):
                per = chunks // 2
                for n, (a, c) in enumerate(PARTS):
                    for i in range(per):
                        for h in range(2):
                            mm = pe.matmul(bank[h * XD:(h + 1) * XD, 0:S], lhs(a, h * per + i), rhs(c, h * per + i),
                                           start=(n == 0 and i == 0), stop=(n == 2 and i == per - 1),
                                           skip_group_check=True)
                return mm

            def qk_pair(b, j):
                if j == 0:
                    pe.wait_ge(xt_lo, count(b, 1, 1))
                if isinstance(b, int) and b == 0 and j == 0:
                    pe.wait_ge(w_split_lo, K0 + 1)
                if isinstance(b, int) and b == 0 and j in (EC // 4, EC // 2):
                    pe.wait_ge(w_split_lo, (K1 if j == EC // 4 else K2) + 1)
                past(pe, qk_hi, count(b, EC, j))
                for w in range(2):
                    mm = split_mm(ps_qk[:, w * S:(w + 1) * S],
                                  lambda a, i: wqkv[:, w, a, i, j * P:(j + 1) * P],
                                  lambda c, i: xt[:, c, i, :], DC)
                mm.then_inc(qk_mm, 1)

            def scores(b, j):
                past(pe, e_done, count(b, EC, j))
                pe.wait_ge(qk_lo, count(b, EC, j + 1))
                pe.wait_ge(s_const, N_CONST)
                for n, (a, c) in enumerate(PARTS):
                    for t in range(TT):
                        for h in range(2):
                            hp = slice(h * DK, (h + 1) * DK)
                            mm = pe.matmul(ps_s[h][:, t * S:(t + 1) * S],
                                           qk[hp, j % 2, a, t * P:(t + 1) * P], qk[hp, j % 2, c, S:2 * S],
                                           start=(n == 0 and t == 0), stop=(n == 2 and t == TT - 1),
                                           skip_group_check=True)
                mm.then_inc(s_mm, 1)

            def values(b, g, tail, fill):
                half, t = g // 2, g % 2
                if isinstance(b, int) and b == 0 and t == 0:
                    pe.wait_ge(w_split_lo, (V0, V1)[half] + 1)
                if g == 0 and fill:
                    pe.wait_ge(slot_done, count(b - 3, 2, 1))
                elif g == 0 and tail:
                    past(pe, kv_lo, count(b - 1, 2))
                if g:
                    pe.wait_ge(v_lo, count(b, 4, g))
                if g == 2 and fill:
                    pe.wait_ge(slot_done, count(b - 3, 2, 2))
                split_mm(ps_v[:, :],
                         lambda a, i: xt[:, a, i, t * P:(t + 1) * P],
                         lambda c, i: wqkv[:, 2, c, i, half * 512:(half + 1) * 512], DC).then_inc(v_mm, 1)

            def turn(b, j):
                pe.wait_ge(p_done, count(b, EC, j + 1))
                past(pe, pt_lo, count(b, 2 * EC, 2 * j))
                for h in range(2):
                    for c in range(2):
                        for t in range(TT):
                            mm = pe.transpose(ps_t[h][:, c * S + t * P:c * S + (t + 1) * P],
                                              probs[:, j % 2, h, t, c * P:(c + 1) * P], ident[:, :])
                    mm.then_inc(t_mm, 1)

            def weigh(b, j):
                past(pe, o_hi, count(b, EC, j))
                if j in (0, EC // 2):
                    pe.wait_ge(v_lo, count(b, 4, 2 if j == 0 else 4))
                pe.wait_ge(pt_lo, count(b, 2 * EC, 2 * j + 2))
                for n, (a, c) in enumerate(PARTS):
                    for i in range(2):
                        for h in range(2):
                            mm = pe.matmul(ps_o[h * DK:(h + 1) * DK, 0:S],
                                           v[:, a, i, (2 * j + h) * DK:(2 * j + h + 1) * DK],
                                           pT[:, j % 2, c, h, i * S:(i + 1) * S],
                                           start=(n == 0 and i == 0), stop=(n == 2 and i == 1),
                                           skip_group_check=True)
                mm.then_inc(pv_mm, 1)

            def project(b, t, route, last=False):
                if t == 0:
                    if isinstance(b, int) and b == 0:
                        pe.wait_ge(w_split_lo, SETUP)
                    pe.wait_ge(o_lo, count(b, EC, EC))
                if last:
                    pe.wait_ge(e_done, count(b, EC, EC))
                elif t:
                    pe.wait_ge(ln1, count(b, 7, t))
                elif route:
                    pe.wait_ge(x2t_lo, count(b - 1, TT, TT))
                split_mm(wo_bank(t, last)[:, :], lambda a, i: o[:, a, i, t * P:(t + 1) * P],
                         lambda c, i: wo[:, c, i, :], EC).then_inc(wo_mm, 1)

            def turn_x1(b, t, head, route, fill, last=False):
                pe.wait_ge(x1_done, count(b, TT, t + 1))
                if last:
                    pass
                elif t == 0 and head:
                    pe.wait_ge(v_lo, count(b + 1, 4, 4))
                elif t and route:
                    pe.wait_ge(rt, count(b - 1, RT, 20))
                into = x1_bank(t, last)
                for c in range(DC):
                    mm = pe.transpose(into[:, c * P:(c + 1) * P], x1[:, t, c * P:(c + 1) * P], ident[:, :])
                mm.then_inc(x1t_mm, 1)

            def ctx_kv(b, last=False):
                pe.wait_ge(ct_lo, count(b, 1, 1))
                if last:
                    pe.wait_ge(slot_done, count(b - 2, 2, 2))
                else:
                    pe.wait_ge(x1t_lo, count(b, TT, 1))
                split_mm(ps_v[:, 0:S], lambda a, i: wx[:, a, i, XK],
                         lambda c, i: ct[:, c, i, :], DC)
                for t in range(TT):
                    mm = split_mm(ps_v[:, S + t * XD:S + (t + 1) * XD],
                                  lambda a, i: ct[:, a, i, t * P:(t + 1) * P], lambda c, i: wx[:, c, i, XV], DC)
                mm.then_inc(kv_mm, 1)

            def cross_q(b, last=False):
                pe.wait_ge(x1t_lo, count(b, TT, TT))
                if last:
                    pe.wait_ge(rt, count(b - 1, RT, 20))
                half_mm(ps_x, lambda a, i: wx[:, a, i, XQ], lambda c, i: x1T[:, c, i, :], DC).then_inc(q2_mm, 1)

            def cross_scores(b):
                pe.wait_ge(q2_lo, count(b, 1, 1))
                pe.wait_ge(kv_lo, count(b, 2, 1))
                pe.wait_ge(s_const, N_CONST)
                for t in range(TT):
                    mm = split_mm(ps_x[:, t * S:(t + 1) * S], lambda a, i: q2[:, a, t * P:(t + 1) * P],
                                  lambda c, i: k2[:, c, :], 1)
                mm.then_inc(s2_mm, 1)

            def cross_turn(b):
                pe.wait_ge(p2_done, count(b, 1, 1))
                for c in range(2):
                    for t in range(TT):
                        mm = pe.transpose(ps_x[:, c * S + t * P:c * S + (t + 1) * P],
                                          p2[:, t, c * P:(c + 1) * P], ident[:, :])
                mm.then_inc(t2_mm, 1)

            def cross_weigh(b):
                pe.wait_ge(t2_lo, count(b, 1, 1))
                half_mm(ps_x, lambda a, i: v2[:, a, i, :], lambda c, i: p2T[:, c, i, :], 2).then_inc(pv2_mm, 1)

            def cross_project(b, t):
                if t == 0:
                    pe.wait_ge(o2_lo, count(b, 1, 1))
                else:
                    pe.wait_ge(ln2, count(b, 7, t))
                pe.wait_ge(s_const, N_CONST)
                split_mm(ps_x[:, :], lambda a, i: o2[:, a, t * P:(t + 1) * P], lambda c, i: wxo[:, c, :], 1)\
                    .then_inc(out2_mm, 1)

            def turn_x2(b, t):
                pe.wait_ge(x2_done, count(b, TT, t + 1))
                if t:
                    pe.wait_ge(x2t_lo, count(b, TT, t))
                for c in range(DC):
                    mm = pe.transpose(ps_x[:, c * P:(c + 1) * P], x2[:, t, c * P:(c + 1) * P], ident[:, :])
                mm.then_inc(x2t_mm, 1)

            def gate(b, tail):
                pe.wait_ge(x2t_lo, count(b, TT, TT))
                if tail:
                    pe.wait_ge(ln1, count(b + 1, 7, TT))
                for t in range(TT):
                    mm = split_mm(ps_gate[:, t, :], lambda a, i: x2T[:, a, i, t * P:(t + 1) * P],
                                  lambda c, i: wx[:, c, i, XG], DC)
                mm.then_inc(gate_mm, 1)

            def positions(b):
                pe.wait_ge(rt, count(b, RT, 11))
                for t in range(TT):
                    pe.matmul(ps_pos[:, t * NX:(t + 1) * NX], before[:, :], sel[:, t, :], start=True, stop=False)
                    mm = pe.matmul(ps_pos[:, t * NX:(t + 1) * NX], ones[:, :], sel_sum[:, t, :],
                                   start=False, stop=True)
                mm.then_inc(pos_mm, 1)

            def fill_slots(b, k, head):
                pe.wait_ge(oh_done, count(b, 2 * TT, TT * (k + 1)))
                past(pe, slot_done, count(b, 2, k))
                if k == 0:
                    pe.wait_ge(rt, count(b, RT, 26))
                    pe.wait_ge(kv_lo, count(min(b + 2, B) if isinstance(b, int) else b + 2, 2))
                elif head:
                    pe.wait_ge(v_lo, count(b + 3, 4, 2))
                for e in range(HX):
                    for t in range(TT):
                        mm = pe.matmul(ps_slot[:, e * 16:(e + 1) * 16], onehot[:, t, e, :],
                                       said[:, t * NX + k * HX + e, :, :].rearrange("p a c -> p (a c)"),
                                       start=(t == 0), stop=(t == TT - 1))
                mm.then_inc(slot_mm, 1)

            def fill_last(n):
                pe.wait_ge(oh_done, (EARLIER + n + 1) * TT)
                pe.wait_ge(slot_done, EARLIER + min(n, 1))
                pe.wait_ge(rt, count(B - 1, RT, 26))
                for e in range(LAST[n].start, LAST[n].stop):
                    for t in range(TT):
                        mm = pe.matmul(ps_last[n][:, e % HX * 16:(e % HX + 1) * 16], onehot[:, t, e % HX, :],
                                       said[:, t * NX + e, :, :].rearrange("p a c -> p (a c)"),
                                       start=(t == 0), stop=(t == TT - 1))
                mm.then_inc(slot_mm, 1)

            def keep_warm(times):
                for _ in range(times):
                    pe.matmul(ps_warm[:, :], ones[:, :], ones[:, :].unsqueeze(1).to_broadcast([P, 4, P]),
                              start=True, stop=True).then_inc(warm, 1)

            def work(r, head, tail, route, fill):
                b, t, u, f = r, r - 1, r - 2, r - 3
                pair = pairs(r, head, tail)

                def step(s, between=()):
                    pair(scores, s - 2)
                    pair(turn, s - 3)
                    for on, run in between:
                        if on:
                            run()
                    pair(weigh, s - 4)
                    if head:
                        qk_pair(b, s)

                last = last_tail(r)
                late_fill = isinstance(r, int) and r == B + 1
                if isinstance(r, int) and r == B + 2:
                    fill_last(0)
                    keep_warm(WARM[0])
                    fill_last(1)
                    keep_warm(WARM[1])
                    return

                step(0, [(fill and not late_fill, lambda: fill_slots(f, 0, head))])
                if head:
                    values(b, 0, tail, fill)
                step(1, [(route, lambda: cross_turn(u))])
                if route:
                    cross_weigh(u)
                if head:
                    values(b, 1, tail, fill)
                step(2, [(late_fill, lambda: fill_slots(f, 0, head)), (route, lambda: cross_project(u, 0)),
                         (fill and not last and not late_fill, lambda: fill_slots(f, 1, head))])
                if route:
                    cross_project(u, 1)
                if late_fill:
                    keep_warm(WARM_ROUTE[1])
                step(3)
                if last:
                    project(t, 0, route, last)
                    turn_x2(u, 0)
                    project(t, 1, route, last)
                    turn_x2(u, 1)
                    gate(u, False)
                    turn_x1(t, 0, head, route, fill, last)
                    turn_x1(t, 1, head, route, fill, last)
                    fill_slots(f, 1, head)
                    positions(u)
                    ctx_kv(t, last)
                    cross_q(t, last)
                    cross_scores(t)
                    keep_warm(WARM_ROUTE[0])
                    return
                if route:
                    turn_x2(u, 0)
                if late_fill:
                    keep_warm(WARM_ROUTE[2])
                if head:
                    values(b, 2, tail, fill)
                if route:
                    turn_x2(u, 1)
                if late_fill:
                    keep_warm(WARM_ROUTE[3])
                step(4, [(tail, lambda: project(t, 0, route))])
                if tail:
                    project(t, 1, route)
                step(5, [(route, lambda: gate(u, tail)), (late_fill, lambda: fill_slots(f, 1, head))])
                if head:
                    values(b, 3, tail, fill)
                step(6, [(tail, lambda: turn_x1(t, 0, head, route, fill)), (route, lambda: positions(u))])
                if late_fill:
                    keep_warm(WARM_ROUTE[4])
                if tail:
                    turn_x1(t, 1, head, route, fill)
                step(7, [(tail, lambda: ctx_kv(t)), (tail, lambda: cross_q(t))])
                if tail:
                    cross_scores(t)

            pe.wait_ge(s_const, N_CONST)
            keep_warm(WARM_START)
            pe.wait_ge(warm, WARM_START)
            rounds(pe, work)

            def up_gate(e, k):
                pe.wait_ge(xg_lo, count(e, CC, CC))
                pe.wait_ge(ew_lo_gu, count(e, 1, 1))
                for f in range(FC):
                    n = FC * k + f
                    past(pe, h_f32, count(e, FC, f - 1))
                    split_mm(ps_h[n % 2][0][:, :], lambda a, i: ew_gu[:, k, a, i, f * P:(f + 1) * P],
                             lambda c, i: xgT[:, c, i, :], DC).then_inc(g_mm, 1)
                    split_mm(ps_h[n % 2][1][:, :], lambda a, i: ew_gu[:, k, a, i, F + f * P:F + (f + 1) * P],
                             lambda c, i: xgT[:, c, i, :], DC).then_inc(u_mm, 1)
                    if isinstance(e, int) and e == 0 and f == 1:
                        fill_last(2)

            def turn_xg(e, k, c):
                past(pe, xg_lo, count(e, CC, c - 1))
                for d in range(DC):
                    mm = pe.transpose(ps_xg[c % 2][:, d * P:(d + 1) * P], xg[:, k, c, d * P:(d + 1) * P], ident[:, :])
                mm.then_inc(xg_mm, 1)

            def down(e, k, ahead):
                pe.wait_ge(ew_lo_dn, count(e, 1, 1))
                if isinstance(e, int) and e == 0:
                    pe.wait_ge(slot_done, FILLS)
                for c in range(CC):
                    past(pe, y_done, count(e, CC, c - 1))
                    for f in range(FC):
                        if c == 0:
                            pe.wait_ge(h_lo, count(e, FC, f + 1))
                        for n, (a, w) in enumerate(PARTS):
                            mm = pe.matmul(ps_y[c % 2][:, :], hT[:, a, f, c * P:(c + 1) * P], ew_dn[:, k, w, f, :],
                                           start=(f == 0 and n == 0), stop=(f == FC - 1 and n == 2))
                    mm.then_inc(y_mm, 1)
                    if ahead and c + 2 < CC:
                        turn_xg(e + 1, 1 - k, c + 2)

            def expert(e, k, ahead, landed):
                up_gate(e, k)
                if ahead:
                    pe.wait_ge(ld_xg[1 - k], landed)
                    turn_xg(e + 1, 1 - k, 0)
                    turn_xg(e + 1, 1 - k, 1)
                down(e, k, ahead)

            pe.wait_ge(ld_xg[0], 64)
            for c in range(CC):
                turn_xg(0, 0, c)
                if c % 2:
                    keep_warm(WARM[2])
            pe.wait_ge(warm, WARM_START + sum(WARM_ROUTE) + WARM[0] + WARM[1] + CC // 2 * WARM[2])
            expert(0, 0, True, 64)
            expert(1, 1, True, 128)
            with pe.Fori(1, NX // 2 - 1) as m:
                expert(m * 2, 0, True, count(m, 64, 64))
                expert(m * 2 + 1, 1, True, count(m, 64, 128))
            expert(NX - 2, 0, True, NX // 2 * 64)
            expert(NX - 1, 1, False, 0)

        @block.scalar
        def _(act):
            def piece_hi(n):
                act.wait_ge(ld_setup[n % 4], piece_loaded(n))
                nc.scalar.activation(piece_split(n, 0), piece_place(n), ACT.Copy, scale=W_SCALE).then_inc(w_split_hi, 1)

            def split_x(b):
                act.wait_ge(ld_x, count(b, 16, 16))
                past(act, qk_mm, count(b, EC))
                past(act, v_mm, count(b, 4))
                nc.scalar.activation(xt[:, 0, :, :], xt32[:, :, :], ACT.Copy).then_inc(xt_hi, 1)

            piece_hi(Q0)
            split_x(0)
            for n in (K0, V0):
                piece_hi(n)

            def qk_out(b, j):
                past(act, s_mm, count(b, EC, j - 1))
                act.wait_ge(qk_mm, count(b, EC, j + 1))
                for w in range(2):
                    at = slice(w * S, (w + 1) * S)
                    nc.scalar.activation(qk32[:, j % 2, at], ps_qk[:, at], ACT.Identity,
                                         bias=bqkv[:, w, j:j + 1], scale=1.0 / W_SCALE)
                    ins = nc.scalar.activation(qk[:, j % 2, 0, at], ps_qk[:, at], ACT.Identity,
                                               bias=bqkv[:, w, j:j + 1], scale=1.0 / W_SCALE)
                ins.then_inc(qk_hi, 1)

            def heads_out(b, j):
                past(act, o_lo, count(b, EC, j - 1))
                if j == 0:
                    past(act, wo_mm, count(b, TT))
                act.wait_ge(pv_mm, count(b, EC, j + 1))
                for dst in (o32[:, j % 2, :], o[:, 0, j, :]):
                    ins = nc.scalar.activation(dst, ps_o[:, 0:S], ACT.Identity, bias=bqkv[:, 2, j:j + 1],
                                               scale=1.0 / P_SCALE)
                ins.then_inc(o_hi, 1)

            def exps(b, j):
                past(act, t_mm, count(b, 2 * EC, 2 * j - 2))
                act.wait_ge(s_negd, count(b, EC, j + 1))
                for h in range(2):
                    for t in range(TT):
                        n = 2 * h + t
                        ins = nc.scalar.activation(probs[:, j % 2, h, t, :], ps_s[h][:, t * S:(t + 1) * S], ACT.Exp,
                                                   bias=s_neg[:, j % 2, n:n + 1], scale=SCORE,
                                                   accum_out=s_den[:, j % 2, n:n + 1])
                ins.then_inc(e_done, 1)

            def values_hi(b, g):
                half, t = g // 2, g % 2
                if t == 0:
                    past(act, pv_mm, count(b, EC, half * EC // 2 - EC // 2))
                act.wait_ge(v_mm, count(b, 4, g + 1))
                nc.scalar.activation(v[:, 0, t, half * 512:(half + 1) * 512], ps_v[:, :], ACT.Copy,
                                     scale=1.0 / W_SCALE).then_inc(v_hi, 1)

            def turned_hi(b, j):
                past(act, pv_mm, count(b, EC, j - 1))
                for h in range(2):
                    act.wait_ge(t_mm, count(b, 2 * EC, 2 * j + h + 1))
                    nc.scalar.activation(pT[:, j % 2, 0, h, :], ps_t[h][:, :], ACT.Copy,
                                         scale=P_SCALE).then_inc(pt_hi, 1)

            def x1_hi(b, t, last=False):
                act.wait_ge(x1t_mm, count(b, TT, t + 1))
                past(act, q2_mm, count(b, 1))
                nc.scalar.activation(x1T[:, 0, :, t * P:(t + 1) * P],
                                     x1_bank(t, last)[:, :].rearrange("p (c n) -> p c n", c=DC), ACT.Copy).then_inc(x1t_hi, 1)

            def split_ctx(b):
                act.wait_ge(ld_ctx, count(b, 16, 16))
                past(act, kv_mm, count(b, 1))
                nc.scalar.activation(ct[:, 0, :, :], ct32[:, :, :], ACT.Copy).then_inc(ct_hi, 1)

            def kv2_hi(b):
                act.wait_ge(kv_mm, count(b, 1, 1))
                past(act, pv2_mm, count(b, 1))
                nc.scalar.activation(k2[:, 0, :], ps_v[:, 0:S], ACT.Copy, scale=1.0 / W_SCALE).then_inc(kv_hi, 1)
                nc.scalar.activation(v2[:, 0].rearrange("p t n -> p (t n)"), ps_v[:, S:S + TT * XD], ACT.Copy,
                                     scale=1.0 / W_SCALE).then_inc(kv_hi, 1)

            def q2_high(b):
                act.wait_ge(q2_mm, count(b, 1, 1))
                past(act, s2_mm, count(b, 1))
                nc.scalar.activation(q2[:, 0, :], ps_x[:, 0:S], ACT.Copy, scale=1.0 / W_SCALE).then_inc(q2_hi, 1)

            def exp2(b):
                act.wait_ge(s2_dve, count(b, 3, 3))
                for t in range(TT):
                    ins = nc.scalar.activation(p2[:, t, :], p2[:, t, :], ACT.Exp, bias=n2[:, t:t + 1],
                                               accum_out=den2[:, t:t + 1])
                ins.then_inc(e2_done, 1)

            def turned2_hi(b):
                act.wait_ge(t2_mm, count(b, 1, 1))
                past(act, pv2_mm, count(b, 1))
                nc.scalar.activation(p2T[:, 0].rearrange("p c n -> p (c n)"), ps_x[:, :], ACT.Copy,
                                     scale=P_SCALE).then_inc(t2_hi, 1)

            def o2_high(b):
                act.wait_ge(pv2_mm, count(b, 1, 1))
                past(act, out2_mm, count(b, TT))
                nc.scalar.activation(o2[:, 0, :], ps_x[:, 0:S], ACT.Copy, scale=1.0 / P_SCALE).then_inc(o2_hi, 1)

            W0 = 32 + 48
            W1 = 48

            GU, DN = slice(0, WGU), slice(WGU, NW)

            def weights_hi(e, k, part, place, loads):
                if part == GU:
                    act.wait_ge(ld_w[place], loads)
                    past(act, y_mm, count(e, CC, -CC))
                nc.scalar.activation(ew[:, k, 0, part], stage[:, place, part], ACT.Copy, scale=W_SCALE).then_inc(ew_hi, 1)

            def x2_turned(b, t):
                act.wait_ge(x2t_mm, count(b, TT, t + 1))
                past(act, gate_mm, count(b, 1))
                nc.scalar.activation(x2T[:, 0, :, t * P:(t + 1) * P],
                                     ps_x[:, :].rearrange("p (c n) -> p c n", c=DC), ACT.Copy).then_inc(x2t_hi, 1)

            def gate_exp(b):
                act.wait_ge(rt, count(b, RT, 3))
                for t in range(TT):
                    ins = nc.scalar.activation(ex[:, t, :], ps_gate[:, t, :], ACT.Exp, bias=neg_l[:, t:t + 1], scale=1.0 / W_SCALE,
                                               accum_out=den_l[:, t:t + 1])
                ins.then_inc(rt_exp, 1)

            def work(r, head, tail, route, fill):
                b, t, u = r, r - 1, r - 2
                pair = pairs(r, head, tail)

                def step(s, between=(), first=(), late=()):
                    pair(turned_hi, s - 3)
                    for on, run in first:
                        if on:
                            run()
                    pair(exps, s - 2)
                    for on, run in between:
                        if on:
                            run()
                    if s != 4:
                        pair(heads_out, s - 4)
                    for on, run in late:
                        if on:
                            run()
                    if head and s < EC - 1:
                        qk_out(b, s)

                if head and not (isinstance(r, int) and r == 0):
                    split_x(b)
                if tail:
                    qk_out(t, EC - 1)
                if isinstance(r, int) and r == 0:
                    act.wait_ge(ld_bias, 48)
                step(0, first=[(route, lambda: exp2(u))])
                if head:
                    values_hi(b, 0)
                if isinstance(r, int) and r == 0:
                    piece_hi(Q1)
                    piece_hi(K1)
                step(1, first=[(route, lambda: turned2_hi(u))])
                if route:
                    o2_high(u)
                if head:
                    values_hi(b, 1)
                if isinstance(r, int) and r == 1:
                    piece_hi(O1)
                step(2, first=[(isinstance(r, int) and r == 0, lambda: piece_hi(V1))])
                step(3, first=[(isinstance(r, int) and r == 0, lambda: piece_hi(Q2))],
                     late=[(head and route, lambda: x2_turned(u, 0))])
                if last_tail(r):
                    split_ctx(t)
                    act.wait_ge(qk_mm, B * EC)
                    act.wait_ge(v_mm, B * 4)
                    weights_hi(0, 0, GU, 0, 32)
                    x2_turned(u, 0)
                    weights_hi(0, 0, DN, 0, 32)
                    x2_turned(u, 1)
                    gate_exp(u)
                    x1_hi(t, 0, True)
                    x1_hi(t, 1, True)
                    kv2_hi(t)
                    q2_high(t)
                    return
                if route and not head:
                    x2_turned(u, 0)
                if head:
                    values_hi(b, 2)
                if isinstance(r, int) and r == 0:
                    piece_hi(K2)
                if isinstance(r, int) and r == 1:
                    piece_hi(X3)
                    piece_hi(XO)
                if route:
                    x2_turned(u, 1)
                step(4)
                if tail:
                    split_ctx(t)
                pair(heads_out, 0)
                step(5, [(route, lambda: gate_exp(u))])
                if head:
                    values_hi(b, 3)
                if isinstance(r, int) and r == 0:
                    piece_hi(O0)
                step(6, [(tail, lambda: x1_hi(t, 0))])
                if tail:
                    x1_hi(t, 1)
                step(7, [(tail, lambda: kv2_hi(t)), (tail, lambda: q2_high(t))])

            rounds(act, work)

            def tokens_hi(e, c):
                if c == 0:
                    past(act, u_mm, count(e, FC))
                act.wait_ge(xg_mm, count(e, CC, c + 1))
                nc.scalar.activation(xgT[:, 0, :, c * P:(c + 1) * P],
                                     ps_xg[c % 2][:, :].rearrange("p (d n) -> p d n", d=DC), ACT.Copy).then_inc(xg_hi, 1)

            def expert(e, k, ahead, loads):
                if ahead and not (isinstance(e, int) and e == 0):
                    weights_hi(e + 1, 1 - k, GU, k, loads)
                for f in range(FC):
                    n = FC * k + f
                    act.wait_ge(g_mm, count(e, FC, f + 1))
                    past(act, h_f32, count(e, FC, f - 1))
                    nc.scalar.activation(silu[:, n % 2, :], ps_h[n % 2][0][:, :], ACT.Silu, scale=1.0 / W_SCALE)\
                      .then_inc(silu_done, 1)
                    if f == 0 and ahead:
                        weights_hi(e + 1, 1 - k, DN, k, loads)
                if ahead:
                    tokens_hi(e + 1, 0)
                    tokens_hi(e + 1, 1)
                for c in range(CC):
                    act.wait_ge(y_mm, count(e, CC, c + 1))
                    if c == 0:
                        act.wait_ge(cur_done, count(e, 2, 2))
                        past(act, st_y, count(e, 64, -64))
                    nc.scalar.activation(y[:, k, c, :], ps_y[c % 2][:, :], ACT.Copy,
                                         scale=cur_w[:, k, c:c + 1]).then_inc(y_done, 1)
                    if ahead and c + 2 < CC:
                        tokens_hi(e + 1, c + 2)

            weights_hi(1, 1, GU, 0, 64)
            for c in range(CC):
                tokens_hi(0, c)
            expert(0, 0, True, 64)
            expert(1, 1, True, 32)
            with act.Fori(1, NX // 2 - 1) as m:
                expert(m * 2, 0, True, count(m, 32, 64))
                expert(m * 2 + 1, 1, True, count(m, 32, 32))
            expert(NX - 2, 0, True, count(NX // 2 - 1, 32, 64))
            expert(NX - 1, 1, False, 0)

            for g in range(GROUPS):
                act.wait_ge(ln3_rstd, 2 * (g + 1))
                for t in range(GT):
                    nc.scalar.activation(rows3[:, g, t, :], rows3[:, g, t, :], ACT.Identity, bias=shift3[:, g, t:t + 1],
                                         scale=rstd3[:, g, t:t + 1]).then_inc(out_done, 1)

        @block.vector
        def _(dve):
            vec = nc.vector

            def low(dst, src, hi, scale=1.0):
                return vec.scalar_tensor_tensor(out=dst, in0=src, scalar=scale, in1=hi, op0=ALU.mult, op1=ALU.subtract)

            dve.wait_ge(s_const, N_CONST)
            vec.tensor_copy(before[:, :], before_f32[:, :]).then_inc(s_constv, 1)
            vec.tensor_copy(iota[:, :], iota_i[:, :]).then_inc(s_constv, 1)
            vec.tensor_copy(row1[:, :], row_i[:, :]).then_inc(s_constv, 1)
            vec.tensor_copy(thr[:, :], thr_i[:, :]).then_inc(s_constv, 1)
            vec.tensor_copy(spare[:, :], spare_i[:, :]).then_inc(s_constv, 1)
            vec.memset(sel_sum[:, :, :], 0.0).then_inc(s_constv, 1)
            vec.memset(ge[:, :, 0:1], 1.0).then_inc(s_constv, 1)
            vec.memset(slots[:, :, :, :], 0.0).then_inc(s_constv, 1)

            def piece_lo(n):
                dve.wait_ge(w_split_hi, n + 1)
                low(piece_split(n, 1), piece_place(n), piece_split(n, 0), W_SCALE).then_inc(w_split_lo, 1)

            def split_x(b):
                dve.wait_ge(xt_hi, count(b, 1, 1))
                low(xt[:, 1, :, :], xt32[:, :, :], xt[:, 0, :, :]).then_inc(xt_lo, 1)

            piece_lo(Q0)
            split_x(0)
            for n in (K0, V0):
                piece_lo(n)

            def maxima(b, j):
                dve.wait_ge(s_mm, count(b, EC, j + 1))
                past(dve, e_done, count(b, EC, j - 1))
                for h in range(2):
                    vec.tensor_reduce(s_max[:, j % 2, 2 * h:2 * h + 2], ps_s[h][:, :].rearrange("p (t k) -> p t k", t=TT),
                                      AX.X, ALU.max).then_inc(s_maxd, 1)
                dve.wait_ge(s_maxd, count(b, 2 * EC, 2 * j + 2))
                vec.tensor_scalar(s_neg[:, j % 2, :], s_max[:, j % 2, :], -SCORE, None, ALU.mult).then_inc(s_negd, 1)

            def row_scales(b, j):
                past(dve, p_done, count(b, EC, j - 1))
                dve.wait_ge(e_done, count(b, EC, j + 1))
                vec.reciprocal(s_rden[:, j % 2, :], s_den[:, j % 2, :]).then_inc(r_done, 1)

            def values_lo(b, g):
                half, t = g // 2, g % 2
                cs = slice(half * 512, (half + 1) * 512)
                dve.wait_ge(v_hi, count(b, 4, g + 1))
                low(v[:, 1, t, cs], ps_v[:, :], v[:, 0, t, cs], 1.0 / W_SCALE).then_inc(v_lo, 1)

            def turned_lo(b, j):
                for h in range(2):
                    dve.wait_ge(pt_hi, count(b, 2 * EC, 2 * j + h + 1))
                    low(pT[:, j % 2, 1, h, :], ps_t[h][:, :], pT[:, j % 2, 0, h, :], P_SCALE).then_inc(pt_lo, 1)

            def residual1(b, t, last=False):
                dve.wait_ge(wo_mm, count(b, TT, t + 1))
                if t == 0:
                    dve.wait_ge(xb_done, count(b, 1, 1))
                    past(dve, x1b_done, count(b, 1))
                    past(dve, ln2, count(b, 7))
                vec.scalar_tensor_tensor(out=z[:, t, :], in0=wo_bank(t, last)[:, :], scalar=1.0 / W_SCALE, in1=xr[:, t, :],
                                         op0=ALU.mult, op1=ALU.add).then_inc(ln1, 1)

            def moments(b, rows, stats, mv, ve, ln, before_it):
                for t in range(TT):
                    dve.wait_ge(ln, count(b, 7, t + 1))
                    vec.bn_stats(stats[:, t, :], rows[:, t, :]).then_inc(ln, 1)
                for t in range(TT):
                    wait_apart(dve, ln, count(b, 7, TT + t + 1), s_constv, N_CONSTV)
                    vec.bn_aggr(mv[:, t, :], stats[:, t, :]).then_inc(ln, 1)
                past(dve, before_it, count(b, 1))
                dve.wait_ge(ln, count(b, 7, 6))
                vec.tensor_scalar(ve[:, :], mv[:, :, 1], EPS, None, ALU.add).then_inc(ln, 1)

            def norm1(b):
                for t in range(TT):
                    if t == 0:
                        dve.wait_ge(ln1_rstd, count(b, 1, 1))
                        past(dve, x2_done, count(b, TT))
                    vec.tensor_scalar(x1[:, t, :], z[:, t, :], mv1[:, t, 0:1], rstd1[:, t:t + 1],
                                      ALU.subtract, ALU.mult).then_inc(x1_done, 1)

            def x1_lo(b, t, last=False):
                dve.wait_ge(x1t_hi, count(b, TT, t + 1))
                low(x1T[:, 1, :, t * P:(t + 1) * P], x1_bank(t, last)[:, :].rearrange("p (c n) -> p c n", c=DC),
                    x1T[:, 0, :, t * P:(t + 1) * P]).then_inc(x1t_lo, 1)

            def split_ctx(b):
                dve.wait_ge(ct_hi, count(b, 1, 1))
                low(ct[:, 1, :, :], ct32[:, :, :], ct[:, 0, :, :]).then_inc(ct_lo, 1)

            def kv2_lo(b):
                dve.wait_ge(kv_hi, count(b, 2, 2))
                low(k2[:, 1, :], ps_v[:, 0:S], k2[:, 0, :], 1.0 / W_SCALE).then_inc(kv_lo, 1)
                low(v2[:, 1].rearrange("p t n -> p (t n)"), ps_v[:, S:S + TT * XD],
                    v2[:, 0].rearrange("p t n -> p (t n)"), 1.0 / W_SCALE).then_inc(kv_lo, 1)

            def q2_low(b):
                dve.wait_ge(q2_hi, count(b, 1, 1))
                low(q2[:, 1, :], ps_x[:, 0:S], q2[:, 0, :], 1.0 / W_SCALE).then_inc(q2_lo, 1)

            def masked(b):
                dve.wait_ge(s2_mm, count(b, 1, 1))
                dve.wait_ge(mask_done, count(b, 1, 1))
                past(dve, t2_mm, count(b, 1))
                vec.scalar_tensor_tensor(out=p2[:, :, :], in0=ps_x[:, :].rearrange("p (t k) -> p t k", t=TT), scalar=SCORE,
                                         in1=mask_add[:, :, :], op0=ALU.mult, op1=ALU.add).then_inc(s2_dve, 1)
                dve.wait_ge(s2_dve, count(b, 3, 1))
                vec.tensor_reduce(m2[:, :], p2[:, :, :], AX.X, ALU.max).then_inc(s2_dve, 1)
                dve.wait_ge(s2_dve, count(b, 3, 2))
                vec.tensor_scalar(n2[:, :], m2[:, :], -1.0, None, ALU.mult).then_inc(s2_dve, 1)

            def row_scales2(b):
                dve.wait_ge(e2_done, count(b, 1, 1))
                vec.reciprocal(rden2[:, :], den2[:, :]).then_inc(r2_done, 1)

            def turned2_lo(b):
                dve.wait_ge(t2_hi, count(b, 1, 1))
                low(p2T[:, 1].rearrange("p c n -> p (c n)"), ps_x[:, :], p2T[:, 0].rearrange("p c n -> p (c n)"),
                    P_SCALE).then_inc(t2_lo, 1)

            def o2_low(b):
                dve.wait_ge(o2_hi, count(b, 1, 1))
                low(o2[:, 1, :], ps_x[:, 0:S], o2[:, 0, :], 1.0 / P_SCALE).then_inc(o2_lo, 1)

            def residual2(b, t):
                dve.wait_ge(out2_mm, count(b, TT, t + 1))
                if t == 0:
                    dve.wait_ge(x1b_done, count(b, 1, 1))
                vec.scalar_tensor_tensor(out=x1[:, t, :], in0=ps_x[:, :], scalar=1.0 / W_SCALE, in1=z[:, t, :],
                                         op0=ALU.mult, op1=ALU.add).then_inc(ln2, 1)

            def norm2(b):
                for t in range(TT):
                    if t == 0:
                        dve.wait_ge(ln2_rstd, count(b, 1, 1))
                        past(dve, x2t_mm, count(b, TT))
                        past(dve, st_x2, count(b, 32))
                    vec.tensor_scalar(x2[:, t, :], x1[:, t, :], mv2[:, t, 0:1], rstd2[:, t:t + 1],
                                      ALU.subtract, ALU.mult).then_inc(x2_done, 1)

            def step(b, n):
                past(dve, rt, count(b, RT, n))

            def x2_lo(b, t):
                dve.wait_ge(x2t_hi, count(b, TT, t + 1))
                low(x2T[:, 1, :, t * P:(t + 1) * P], ps_x[:, :].rearrange("p (c n) -> p c n", c=DC),
                    x2T[:, 0, :, t * P:(t + 1) * P]).then_inc(x2t_lo, 1)

            def gate_max(b):
                wait_apart(dve, gate_mm, count(b, 1, 1), s_constv, N_CONSTV)
                for t in range(TT):
                    vec.max(top_l[:, t, :], ps_gate[:, t, :]).then_inc(rt, 1)
                step(b, 2)
                vec.tensor_scalar(neg_l[:, :], top_l[:, :, 0], -1.0 / W_SCALE, None, ALU.mult).then_inc(rt, 1)

            def choose(b):
                by_row = lambda ap: ap.unsqueeze(2).to_broadcast([P, TT, NX])
                dve.wait_ge(rt_exp, count(b, 1, 1))
                vec.reciprocal(rden_l[:, :], den_l[:, :]).then_inc(rt, 1)
                step(b, 4)
                vec.tensor_tensor(pr[:, :, :], ex[:, :, :], by_row(rden_l[:, :]), ALU.mult).then_inc(rt, 1)
                wait_apart(dve, rt, count(b, RT, 5), s_constv, N_CONSTV)
                for t in range(TT):
                    vec.max(top_p[:, t, :], pr[:, t, :]).then_inc(rt, 1)
                wait_apart(dve, rt, count(b, RT, 7), s_constv, N_CONSTV)
                for t in range(TT):
                    vec.match_replace(left[:, t, :], top_p[:, t, :], pr[:, t, :], -1.0).then_inc(rt, 1)
                step(b, 9)
                vec.tensor_scalar(sel[:, :, :], left[:, :, :], -1.0, None, ALU.is_equal).then_inc(rt, 1)
                step(b, 10)
                vec.tensor_tensor(sel_sum[:, 1, :], sel_sum[:, 0, :], sel[:, 0, :], ALU.add).then_inc(rt, 1)
                vec.tensor_reduce(w_sum[:, :], top_p[:, :, :], AX.X, ALU.add).then_inc(rt, 1)
                step(b, 12)
                vec.reciprocal(w_rsum[:, :], w_sum[:, :]).then_inc(rt, 1)
                step(b, 13)
                vec.scalar_tensor_tensor(out=w32[:, :, :], in0=pr[:, :, :], scalar=G_SCALE, in1=by_row(w_rsum[:, :]),
                                         op0=ALU.mult, op1=ALU.mult).then_inc(rt, 1)
                step(b, 14)
                vec.tensor_copy(w_hi[:, :, :], w32[:, :, :]).then_inc(rt, 1)
                step(b, 15)
                vec.tensor_tensor(w_lo[:, :, :], w32[:, :, :], w_hi[:, :, :], ALU.subtract).then_inc(rt, 1)

            G = TT * NX

            def places(b):
                dve.wait_ge(pos_mm, count(b, 1, 1))
                vec.tensor_tensor(sel_sum[:, 0, :], sel_sum[:, 1, :], sel[:, 1, :], ALU.add).then_inc(rt, 1)
                vec.tensor_tensor(ge[:, :, 1:CC + 1], ps_pos[:, :].unsqueeze(2).to_broadcast([P, G, CC]),
                                  thr[:, :].unsqueeze(1).to_broadcast([P, G, CC]), ALU.is_ge).then_inc(rt, 1)
                step(b, 18)
                vec.tensor_reduce(n_ge[:, :], ge[:, :, 1:CC], AX.X, ALU.add).then_inc(rt, 1)
                step(b, 19)
                vec.scalar_tensor_tensor(out=pos_in[:, :], in0=n_ge[:, :], scalar=-float(P), in1=ps_pos[:, :],
                                         op0=ALU.mult, op1=ALU.add).then_inc(rt, 1)
                vec.tensor_tensor(in_chunk[:, :, :], ge[:, :, 0:CC], ge[:, :, 1:CC + 1], ALU.subtract).then_inc(rt, 1)

            def tell(b):
                by_choice = lambda ap: ap.rearrange("p t e -> p (t e)").unsqueeze(2).to_broadcast([P, G, CC])
                step(b, 21)
                vec.tensor_tensor(chosen[:, :, :], in_chunk[:, :, :], by_choice(sel[:, :, :]), ALU.mult).then_inc(rt, 1)
                step(b, 22)
                past(dve, slot_mm, count(b, 2))
                vec.tensor_scalar(said[:, :, 0, :], chosen[:, :, :], row1[:, 0:1], None, ALU.mult).then_inc(rt, 1)
                vec.tensor_tensor(said[:, :, 1, :].rearrange("p (t e) c -> p t e c", t=TT),
                                  chosen[:, :, :].rearrange("p (t e) c -> p t e c", t=TT),
                                  tile_no[:, :].unsqueeze(2).unsqueeze(3).to_broadcast([P, TT, NX, CC]), ALU.mult).then_inc(rt, 1)
                vec.tensor_tensor(said[:, :, 2, :], chosen[:, :, :], by_choice(w_hi[:, :, :]), ALU.mult).then_inc(rt, 1)
                vec.tensor_tensor(said[:, :, 3, :], chosen[:, :, :], by_choice(w_lo[:, :, :]), ALU.mult).then_inc(rt, 1)
                step(b, 24)
                vec.tensor_scalar(tile_no[:, :], tile_no[:, :], float(TT), None, ALU.add).then_inc(rt, 1)

            def slot_onehot(b, k, t):
                step(b, 20)
                past(dve, slot_mm, count(b, 2, k))
                vec.tensor_tensor(onehot[:, t, :, :], iota[:, :].unsqueeze(1).to_broadcast([P, HX, P]),
                                  pos_in[:, t * NX + k * HX:t * NX + (k + 1) * HX].unsqueeze(2).to_broadcast([P, HX, P]),
                                  ALU.is_equal).then_inc(oh_done, 1)

            def add_slots(b, k):
                dve.wait_ge(slot_mm, count(b, 2, k + 1))
                if isinstance(b, int) and b == 0 and k == 0:
                    dve.wait_ge(st_zero, 16)
                past(dve, slot_done, count(b, 2, k - 1))
                half = slots[:, k * HX:(k + 1) * HX, :, :].rearrange("p e a c -> p (e a c)")
                vec.tensor_tensor(half, half, ps_slot[:, :], ALU.add).then_inc(slot_done, 1)

            def last_onehot(n, t):
                experts, at = LAST[n], slice(LAST[n].start % HX, (LAST[n].stop - 1) % HX + 1)
                step(B - 1, 20)
                if n == 2:
                    dve.wait_ge(slot_mm, EARLIER + 2)
                else:
                    dve.wait_ge(slot_mm, EARLIER)
                width = experts.stop - experts.start
                vec.tensor_tensor(onehot[:, t, at, :], iota[:, :].unsqueeze(1).to_broadcast([P, width, P]),
                                  pos_in[:, t * NX + experts.start:t * NX + experts.stop].unsqueeze(2)
                                  .to_broadcast([P, width, P]), ALU.is_equal).then_inc(oh_done, 1)

            def add_last(n):
                experts = LAST[n]
                dve.wait_ge(slot_mm, EARLIER + n + 1)
                dve.wait_ge(slot_done, EARLIER)
                first = experts.start % HX * 16
                part = slots[:, experts, :, :].rearrange("p e a c -> p (e a c)")
                vec.tensor_tensor(part, part, ps_last[n][:, first:first + (experts.stop - experts.start) * 16], ALU.add)\
                   .then_inc(slot_done, 1)

            def tables(k):
                at = LAST[k]
                dve.wait_ge(slot_done, EARLIER + k + 1)
                vec.scalar_tensor_tensor(out=tok[:, at, :], in0=slots[:, at, 1, :], scalar=float(P), in1=slots[:, at, 0, :],
                                         op0=ALU.mult, op1=ALU.add).then_inc(table, 1)
                vec.tensor_scalar(empty[:, at, :], slots[:, at, 0, :], 0.0, None, ALU.is_equal).then_inc(table, 1)
                dve.wait_ge(table, count(k, 8, 2))
                vec.tensor_scalar(tok0[:, at, :], tok[:, at, :], -1.0, 0.0, ALU.add, ALU.max).then_inc(table, 1)
                dve.wait_ge(table, count(k, 8, 3))
                vec.tensor_tensor(tok[:, at, :], empty[:, at, :], spare[:, :].unsqueeze(1)
                                  .to_broadcast([P, at.stop - at.start, CC]), ALU.mult)\
                   .then_inc(table, 1)
                vec.tensor_copy(idx_from[:, at, :], tok0[:, at, :]).then_inc(table, 1)
                dve.wait_ge(table, count(k, 8, 4))
                vec.tensor_tensor(idx_to[:, at, :], tok0[:, at, :], tok[:, at, :], ALU.add).then_inc(table, 1)
                vec.tensor_tensor(w_slot[:, at, :], slots[:, at, 2, :], slots[:, at, 3, :], ALU.add).then_inc(table, 1)
                dve.wait_ge(table, count(k, 8, 7))
                vec.tensor_scalar(w_slot[:, at, :], w_slot[:, at, :], 1.0 / (G_SCALE * W_SCALE), None, ALU.mult).then_inc(table, 1)

            def weights_lo(e, k, part, place, n, done):
                dve.wait_ge(ew_hi, count(e, 2, n))
                if n == 1:
                    past(dve, y_mm, count(e, CC, -CC))
                low(ew[:, k, 1, part], stage[:, place, part], ew[:, k, 0, part], W_SCALE).then_inc(done, 1)

            def gate_up_lo(e, k, place):
                weights_lo(e, k, slice(0, WGU), place, 1, ew_lo_gu)

            def down_lo(e, k, place):
                weights_lo(e, k, slice(WGU, NW), place, 2, ew_lo_dn)

            def work(r, head, tail, route, fill):
                b, t, u, f = r, r - 1, r - 2, r - 3
                pair = pairs(r, head, tail)

                def step(s, between=(), soon=()):
                    pair(maxima, s - 2)
                    for on, run in soon:
                        if on:
                            run()
                    pair(turned_lo, s - 3)
                    for on, run in between:
                        if on:
                            run()
                    pair(row_scales, s - 2)

                if head and not (isinstance(r, int) and r == 0):
                    split_x(b)
                if route:
                    masked(u)
                last = last_tail(r)
                late_fill = isinstance(r, int) and r == B + 1
                if isinstance(r, int) and r == B + 2:
                    for n in range(2):
                        last_onehot(n, 0)
                        last_onehot(n, 1)
                        add_last(n)
                        tables(n)
                    return
                step(0, [(route, lambda: row_scales2(u))], soon=[(fill and not late_fill, lambda: add_slots(f, 0))])
                if late_fill:
                    slot_onehot(f, 0, 0)
                elif fill and not last:
                    slot_onehot(f, 1, 0)
                if head:
                    values_lo(b, 0)
                if isinstance(r, int) and r == 0:
                    piece_lo(Q1)
                    piece_lo(K1)
                step(1, [(route, lambda: turned2_lo(u)), (fill and not last, lambda: slot_onehot(f, 0 if late_fill else 1, 1))])
                if route:
                    o2_low(u)
                if late_fill:
                    slot_onehot(f, 1, 0)
                if head:
                    values_lo(b, 1)
                step(2, [(isinstance(r, int) and r == 0, lambda: piece_lo(V1))])
                if route:
                    residual2(u, 0)
                if fill and not last:
                    add_slots(f, 0 if late_fill else 1)
                if route:
                    residual2(u, 1)
                    moments(u, x1, stats2, mv2, ve2, ln2, ln2_rstd)
                step(3, [(isinstance(r, int) and r < 2, lambda: piece_lo((Q2, O1)[r]))], soon=[(route, lambda: norm2(u))])
                if last:
                    slot_onehot(f, 1, 0)
                    slot_onehot(f, 1, 1)
                    split_ctx(t)
                    residual1(t, 0, True)
                    x2_lo(u, 0)
                    gate_up_lo(0, 0, 0)
                    residual1(t, 1, True)
                    x2_lo(u, 1)
                    moments(t, z, stats1, mv1, ve1, ln1, ln1_rstd)
                    gate_max(u)
                    norm1(t)
                    choose(u)
                    x1_lo(t, 0, True)
                    x1_lo(t, 1, True)
                    add_slots(f, 1)
                    places(u)
                    tell(u)
                    kv2_lo(t)
                    down_lo(0, 0, 0)
                    q2_low(t)
                    return
                if route:
                    x2_lo(u, 0)
                    if late_fill:
                        slot_onehot(f, 1, 1)
                    if not head:
                        x2_lo(u, 1)
                if head:
                    values_lo(b, 2)
                if head and route:
                    x2_lo(u, 1)
                if isinstance(r, int) and r == 0:
                    piece_lo(K2)
                if isinstance(r, int) and r == 1:
                    piece_lo(X3)
                    piece_lo(XO)
                step(4)
                if tail:
                    residual1(t, 0)
                    split_ctx(t)
                    residual1(t, 1)
                    moments(t, z, stats1, mv1, ve1, ln1, ln1_rstd)
                step(5, [(route, lambda: gate_max(u))])
                if tail:
                    norm1(t)
                if route:
                    choose(u)
                if late_fill:
                    add_slots(f, 1)
                if head:
                    values_lo(b, 3)
                if isinstance(r, int) and r == 0:
                    piece_lo(O0)
                step(6, [(route, lambda: places(u))])
                if tail:
                    x1_lo(t, 0)
                if route:
                    tell(u)
                if tail:
                    x1_lo(t, 1)
                step(7, [(route and not late_fill, lambda: slot_onehot(u, 0, 0))])
                if tail:
                    kv2_lo(t)
                    q2_low(t)
                if route and not late_fill:
                    slot_onehot(u, 0, 1)

            dve.wait_ge(s_constv, N_CONSTV)
            rounds(dve, work)

            def tokens_lo(e):
                for c in range(CC):
                    dve.wait_ge(xg_hi, count(e, CC, c + 1))
                    low(xgT[:, 1, :, c * P:(c + 1) * P], ps_xg[c % 2][:, :].rearrange("p (d n) -> p d n", d=DC),
                        xgT[:, 0, :, c * P:(c + 1) * P]).then_inc(xg_lo, 1)

            def expert(e, k, ahead):
                first = isinstance(e, int) and e == 0
                if ahead and not first:
                    gate_up_lo(e + 1, 1 - k, k)
                for f in range(FC):
                    n = FC * k + f
                    if first and f < TT:
                        last_onehot(2, f)
                        if f == 0:
                            gate_up_lo(1, 1, 0)
                    dve.wait_ge(u_mm, count(e, FC, f + 1))
                    dve.wait_ge(silu_done, count(e, FC, f + 1))
                    past(dve, h_lo, count(e, FC, f - 1))
                    vec.scalar_tensor_tensor(out=h32[:, n % 2, :], in0=ps_h[n % 2][1][:, :], scalar=1.0 / W_SCALE,
                                             in1=silu[:, n % 2, :], op0=ALU.mult, op1=ALU.mult).then_inc(h_f32, 1)
                    if f == 0:
                        past(dve, y_mm, count(e, CC))
                    dve.wait_ge(h_f32, count(e, FC, f + 1))
                    vec.tensor_copy(hT[:, 0, f, :], h32[:, n % 2, :]).then_inc(h_hi, 1)
                    dve.wait_ge(h_hi, count(e, FC, f + 1))
                    vec.tensor_tensor(hT[:, 1, f, :], h32[:, n % 2, :], hT[:, 0, f, :], ALU.subtract).then_inc(h_lo, 1)
                    if f == 0 and ahead and not first:
                        down_lo(e + 1, 1 - k, k)
                    if first and f == 1:
                        add_last(2)
                        tables(2)
                if ahead:
                    tokens_lo(e + 1)
                if first:
                    down_lo(1, 1, 0)

            tokens_lo(0)
            expert(0, 0, True)
            expert(1, 1, True)
            with dve.Fori(2, NX - 3, 2) as e:
                expert(e, 0, True)
                expert(e + 1, 1, True)
            expert(NX - 2, 0, True)
            expert(NX - 1, 1, False)

            LN = 2 * GT + 2
            for g in range(GROUPS):
                dve.wait_ge(ld_acc[g % HALF], 16 * (g // HALF + 1))
                for t in range(GT):
                    vec.bn_stats(stats3[:, g, t, :], rows3[:, g, t, :]).then_inc(ln3, 1)
                for t in range(GT):
                    dve.wait_ge(ln3, count(g, LN, t + 1))
                    vec.bn_aggr(mv3[:, g, t, :], stats3[:, g, t, :]).then_inc(ln3, 1)
                dve.wait_ge(ln3, count(g, LN, 2 * GT))
                vec.tensor_scalar(ve3[:, g, :], mv3[:, g, :, 1], EPS, None, ALU.add).then_inc(ln3, 1)
                vec.tensor_scalar(neg_mean3[:, g, :], mv3[:, g, :, 0], -1.0, None, ALU.mult).then_inc(ln3, 1)

        @block.gpsimd
        def _(pool):
            gp = nc.gpsimd
            gp.memset(ident[:, :], 0.0).then_inc(s_const, 1)
            gp.memset(before_f32[:, :], 1.0).then_inc(s_const, 1)
            gp.memset(ones[:, :], 1.0).then_inc(s_const, 1)
            gp.memset(neg_half[:, :], -0.5).then_inc(s_const, 1)
            gp.iota(iota_i[:, :], [[1, P]], base=0, channel_multiplier=0).then_inc(s_const, 1)
            gp.iota(row_i[:, :], [[0, 1]], base=1, channel_multiplier=1).then_inc(s_const, 1)
            gp.iota(thr_i[:, :], [[P, CC]], base=P, channel_multiplier=0).then_inc(s_const, 1)
            gp.iota(spare_i[:, :], [[P, CC]], base=N, channel_multiplier=1).then_inc(s_const, 1)
            gp.memset(tile_no[:, 0:1], 0.0).then_inc(s_const, 1)
            gp.memset(tile_no[:, 1:2], 1.0).then_inc(s_const, 1)
            pool.wait_ge(s_const, 10)
            gp.affine_select(out=ident[:, :], in_=ident[:, :], compare_op=ALU.not_equal, fill=1.0, base=0,
                             pattern=[[-1, P]], channel_multiplier=1).then_inc(s_const, 1)
            gp.affine_select(out=before_f32[:, :], in_=before_f32[:, :], compare_op=ALU.is_ge, fill=0.0, base=-1,
                             pattern=[[1, P]], channel_multiplier=-1).then_inc(s_const, 1)

            def qk_low(b, j):
                past(pool, s_mm, count(b, EC, j - 1))
                pool.wait_ge(qk_hi, count(b, EC, j + 1))
                gp.tensor_tensor(qk[:, j % 2, 1, :], qk32[:, j % 2, :], qk[:, j % 2, 0, :], ALU.subtract).then_inc(qk_lo, 1)

            def normalise(b, j):
                pool.wait_ge(r_done, count(b, EC, j + 1))
                rows = probs[:, j % 2].rearrange("p h t k -> p (h t) k")
                gp.tensor_tensor(rows, rows, s_rden[:, j % 2, :].unsqueeze(2).to_broadcast([P, 4, S]), ALU.mult)\
                  .then_inc(p_done, 1)

            def heads_lo(b, j):
                pool.wait_ge(o_hi, count(b, EC, j + 1))
                gp.tensor_tensor(o[:, 1, j, :], o32[:, j % 2, :], o[:, 0, j, :], ALU.subtract).then_inc(o_lo, 1)

            def add_bias(b):
                pool.wait_ge(ld_row, count(b, 16, 16))
                gp.tensor_tensor(xr[:, :, :], xr[:, :, :], bo_row[:, :].unsqueeze(1).to_broadcast([P, TT, D]), ALU.add)\
                  .then_inc(xb_done, 1)

            def mask_rows(b):
                wait_apart(pool, ld_mask, count(b, 16, 16), s_const, N_CONST)
                gp.tensor_scalar(mask_add[:, :, :], mask_i[:, :, :], -1.0e9, None, ALU.mult).then_inc(mask_done, 1)

            def rstd(b, ln, dst, ve, done, read):
                pool.wait_ge(ln, count(b, 7, 7))
                past(pool, read, count(b, TT))
                gp.tensor_tensor(dst[:, :], ve[:, :], neg_half[:, 0:TT], ALU.pow).then_inc(done, 1)

            def add_bias2(b):
                pool.wait_ge(x1_done, count(b, TT, TT))
                gp.tensor_tensor(z[:, :, :], x1[:, :, :], xbo_row[:, :].unsqueeze(1).to_broadcast([P, TT, D]), ALU.add)\
                  .then_inc(x1b_done, 1)

            def normalise2(b):
                pool.wait_ge(r2_done, count(b, 1, 1))
                gp.tensor_tensor(p2[:, :, :], p2[:, :, :], rden2[:, :].unsqueeze(2).to_broadcast([P, TT, S]), ALU.mult)\
                  .then_inc(p2_done, 1)

            def work(r, head, tail, route, fill):
                b, t, u = r, r - 1, r - 2
                pair = pairs(r, head, tail)

                def step(s):
                    pair(normalise, s - 2)
                    if s != 4:
                        pair(heads_lo, s - 4)
                    if head:
                        qk_low(b, s)

                if route:
                    normalise2(u)
                step(0)
                step(1)
                if isinstance(r, int) and r == 1:
                    pool.wait_ge(s_constv, N_CONSTV)
                    pool.dma_start(acc_rows[N:N + CAP, :].rearrange("(c p) n -> p c n", p=P),
                                   slots[:, :, :, :].rearrange("p e a c -> p (e a c)").unsqueeze(1)
                                   .to_broadcast([P, CC, D])).then_inc(st_zero, 16)
                    pool.wait_ge(ld_small, 32)
                if tail:
                    add_bias(t)
                step(2)
                last = last_tail(r)
                if last:
                    step(3)
                if route:
                    rstd(u, ln2, rstd2, ve2, ln2_rstd, x2_done)
                if not last:
                    step(3)
                step(4)
                pair(heads_lo, 0)
                if tail:
                    rstd(t, ln1, rstd1, ve1, ln1_rstd, x1_done)
                step(5)
                if tail:
                    add_bias2(t)
                step(6)
                if tail:
                    mask_rows(t)
                step(7)

            rounds(pool, work)

            def column(dst, k, src, e, done):
                gp.tensor_copy(dst[:, k, :], src[:, bass.ds(e, 1), :].rearrange("p a c -> p (a c)")).then_inc(done, 1)

            def columns_out(e, k):
                column(cur_to, k, idx_to, e, cur_done)
                column(cur_w, k, w_slot, e, cur_done)

            def gather(e, k):
                column(cur_from, k, idx_from, e, from_done)
                wait_apart(pool, from_done, count(e, 1, 1), s_const, N_CONST)
                for c in range(CC):
                    gp.indirect_dma_start(xg[:, k, c, :], None, x2_rows,
                                          bass.IndirectOffsetOnAxis(ap=cur_from[:, k, c:c + 1], axis=0)).then_inc(ld_xg[k], 16)

            def scatter(e, k):
                for c in range(CC):
                    wait_apart(pool, y_done, count(e, CC, c + 1), s_const, N_CONST)
                    gp.indirect_dma_start(acc_rows, bass.IndirectOffsetOnAxis(ap=cur_to[:, k, c:c + 1], axis=0),
                                          y[:, k, c, :], None, compute_op=ALU.add).then_inc(st_y, 16)

            def expert(e, k, ahead):
                if ahead:
                    past(pool, xg_mm, count(e, CC))
                    gather(e + 1, 1 - k)
                past(pool, st_y, count(e, 64))
                if ahead:
                    past(pool, y_done, count(e, CC))
                    columns_out(e + 1, 1 - k)
                scatter(e, k)

            pool.wait_ge(table, 8)
            pool.wait_ge(st_x2, B * 32)
            pool.wait_ge(st_zero, 16)
            pool.wait_ge(pt_lo, B * 2 * EC)
            pool.wait_ge(pv_mm, B * EC)
            gather(0, 0)
            columns_out(0, 0)
            expert(0, 0, True)
            pool.wait_ge(table, 24)
            expert(1, 1, True)
            with pool.Fori(2, NX - 3, 2) as e:
                expert(e, 0, True)
                expert(e + 1, 1, True)
            expert(NX - 2, 0, True)
            expert(NX - 1, 1, False)

            for g in range(GROUPS):
                pool.wait_ge(ln3, (g + 1) * (2 * GT + 2))
                gp.tensor_tensor(rstd3[:, g, :], ve3[:, g, :], neg_half[:, :], ALU.pow).then_inc(ln3_rstd, 1)
                pool.wait_ge(ln3_rstd, 2 * g + 1)
                gp.tensor_tensor(shift3[:, g, :], neg_mean3[:, g, :], rstd3[:, g, :], ALU.mult).then_inc(ln3_rstd, 1)


INS = ["xT", "x_rows", "ctxT", "mask", "wqT", "wkT", "wvT", "woT", "bq", "bk", "bv", "bo",
       "x_wv", "x_wk", "x_wq", "x_wo", "x_bo", "gateT", "wguT", "wdnT"]


def kernel(x, ctx_1024, mask_BxSxS2_ik1, L0_attn_Wq, L0_attn_bq, L0_attn_Wk, L0_attn_bk, L0_attn_Wv, L0_attn_bv,
           L0_attn_Wo, L0_attn_bo, L0_xattn_Wv, L0_xattn_Wk, L0_xattn_Wq, L0_xattn_Wo, L0_xattn_bo,
           L0_ffn_gate_weight, L0_ffn_gate_up_proj, L0_ffn_down_proj):
    import numpy as np
    import concourse.bacc as bacc
    from concourse.bass_utils import run_bass_kernel_spmd

    a = np.asarray
    rows = lambda m: a(m).reshape(N, -1)
    cols = lambda m: a(m).reshape(EC, P).T
    given = {
        "xT": rows(x).T, "x_rows": rows(x), "ctxT": rows(ctx_1024).T, "mask": rows(mask_BxSxS2_ik1),
        "wqT": a(L0_attn_Wq).T, "wkT": a(L0_attn_Wk).T, "wvT": a(L0_attn_Wv).T, "woT": a(L0_attn_Wo).T,
        "bq": cols(L0_attn_bq), "bk": cols(L0_attn_bk), "bv": cols(L0_attn_bv), "bo": a(L0_attn_bo),
        "x_wv": a(L0_xattn_Wv), "x_wk": a(L0_xattn_Wk), "x_wq": a(L0_xattn_Wq), "x_wo": a(L0_xattn_Wo),
        "x_bo": a(L0_xattn_bo), "gateT": a(L0_ffn_gate_weight).T,
        "wguT": a(L0_ffn_gate_up_proj).transpose(0, 2, 1), "wdnT": a(L0_ffn_down_proj).transpose(0, 2, 1),
    }
    given = {k: np.ascontiguousarray(m) for k, m in given.items()}
    nc = bacc.Bacc("TRN2", target_bir_lowering=False, num_devices=1)
    args = [nc.dram_tensor(k, given[k].shape, mybir.dt.from_np(given[k].dtype), kind="ExternalInput").ap() for k in INS]
    out = nc.dram_tensor("out", [N, D], F32, kind="ExternalOutput").ap()
    build(nc, *args, out)
    r = run_bass_kernel_spmd(nc, [given], core_ids=[0])
    return r.results[0]["out"].reshape(B, S, D)
```
